# Optimizing a Trainium2 kernel written in Bass

```python
import numpy as np
import jax
import jax.numpy as jnp

def _softmax(x, axis=-1):
    return jax.nn.softmax(x, axis=axis)

def _gelu(x):
    return jax.nn.gelu(x, approximate=True)

def _silu(x):
    return jax.nn.silu(x)

def _sigmoid(x):
    return jax.nn.sigmoid(x)

def _layernorm(x, axis=-1, eps=1e-05):
    m = jnp.mean(x, axis=axis, keepdims=True)
    v = jnp.var(x, axis=axis, keepdims=True)
    return (x - m) / jnp.sqrt(v + eps)

def _scatter_add(tgt, idx, src, axis=0):
    return tgt.at[idx].add(src)

def _segment_sum(src, seg, n):
    return jax.ops.segment_sum(src, seg, n)
kernel_name = 'mk_perceiver_d1_seqx_r4_4e488f'

def setup_inputs(seed: int=0):
    np.random.seed(seed)
    _w = jnp.asarray

    def _rec_inputs():
        import jax
        import jax.numpy as jnp
        _rk = jax.random.key(seed)
        x = 7.22e-05 + 1 * jax.random.normal(jax.random.fold_in(_rk, 1), (64, 32, 256), jnp.float32)
        _lenS = 32 - jax.random.randint(jax.random.fold_in(_rk, 7), (64,), 0, max(1, 32 // 4) + 1, jnp.int32)
        _lenS2 = 257 - jax.random.randint(jax.random.fold_in(_rk, 8), (64,), 0, max(1, 257 // 4) + 1, jnp.int32)
        _ctx_768P = jax.random.normal(jax.random.fold_in(_rk, 11), (64, 16, 192), jnp.float32)
        _ctx_768c = jax.random.dirichlet(jax.random.fold_in(_rk, 511), 0.3 * jnp.ones((16,), jnp.float32), (64, 257))
        _ctx_768t = jnp.einsum('bsk,bkd->bsd', _ctx_768c, _ctx_768P)
        _ctx_768t = _ctx_768t * jax.lax.rsqrt(jnp.mean(jnp.square(_ctx_768t)) + 1e-12) * 0.953939
        ctx_768 = 3.88148e-05 + 0.999967 * (_ctx_768t + 0.3 * jax.random.normal(jax.random.fold_in(_rk, 611), (64, 257, 192), jnp.float32))
        _validS = jnp.arange(32)[None, :] < _lenS[:, None]
        _validS2 = jnp.arange(257)[None, :] < _lenS2[:, None]
        _causal = jnp.tril(jnp.ones((32, 32), dtype=bool))
        mask_BxS_bf1 = jnp.ones((64, 32), dtype=bool)
        mask_BxS2_bf1 = jnp.ones((64, 257), dtype=bool)
        return (x, ctx_768, mask_BxS_bf1, mask_BxS2_bf1)
    x, ctx_768, mask_BxS_bf1, mask_BxS2_bf1 = _rec_inputs()

    def _L0_xattn_setup():
        import jax, jax.numpy as jnp
        import numpy as np
        B, T, DT, G, DV = (16, 128, 256, 144, 192)
        H, DH = (4, 32)
        INNER = H * DH
        HID = 4 * DT
        N_STATE = 64
        K_TOP = 32

        def layernorm(x, g, b, eps=1e-05):
            m = x.mean(-1, keepdims=True)
            v = x.var(-1, keepdims=True)
            return (x - m) * jax.lax.rsqrt(v + eps) * g + b

        def s4d(x, log_dt, A_re, A_im, C_re, C_im, D_skip):
            Bb, L, D = x.shape
            dt = jnp.exp(log_dt)
            A = A_re + 1j * A_im
            C = C_re + 1j * C_im
            dtA = dt[:, None] * A
            dC = C * (jnp.exp(dtA) - 1.0) / A
            powers = jnp.exp(dtA[:, :, None] * jnp.arange(L))
            K = 2.0 * jnp.einsum('dn,dnl->dl', dC, powers).real
            n = 2 * L
            Kf = jnp.fft.rfft(K, n=n, axis=-1)
            xf = jnp.fft.rfft(x, n=n, axis=1)
            y = jnp.fft.irfft(xf * Kf.T[None], n=n, axis=1)[:, :L]
            return y + x * D_skip
        key = jax.random.key(seed)
        ks = jax.random.split(key, 16)
        s = 0.02
        inp = {'x_text': jax.random.normal(ks[0], (B, T, DT), jnp.float32), 'x_vision': jax.random.normal(ks[1], (B, G, DV), jnp.float32), 'text_mask': jnp.ones((B, T), bool), 'vision_mask': jnp.ones((B, G), bool), 'Wq': jax.random.normal(ks[2], (DT, INNER), jnp.float32) * s, 'Wk': jax.random.normal(ks[3], (DV, INNER), jnp.float32) * s, 'Wv': jax.random.normal(ks[4], (DV, DT), jnp.float32) * s, 'W_film_in': jax.random.normal(ks[5], (DT, 2 * DT), jnp.float32) * s, 'b_film_in': jnp.zeros((2 * DT,), jnp.float32), 'W_film_out': jax.random.normal(ks[6], (DT, 2 * DT), jnp.float32) * s, 'b_film_out': jnp.zeros((2 * DT,), jnp.float32), 'g_norm_in': jnp.ones((DT,), jnp.float32), 'b_norm_in': jnp.zeros((DT,), jnp.float32), 'g_norm_out': jnp.ones((DT,), jnp.float32), 'b_norm_out': jnp.zeros((DT,), jnp.float32), 'g_ffn': jnp.ones((DT,), jnp.float32), 'b_ffn': jnp.zeros((DT,), jnp.float32), 'W1': jax.random.normal(ks[7], (DT, HID), jnp.float32) * s, 'b1': jnp.zeros((HID,), jnp.float32), 'W2': jax.random.normal(ks[8], (HID, DT), jnp.float32) * s, 'b2': jnp.zeros((DT,), jnp.float32), 'log_dt': jnp.log(0.001) + jax.random.uniform(ks[9], (DT,), jnp.float32) * (jnp.log(0.1) - jnp.log(0.001)), 'A_re': -0.5 * jnp.ones((DT, N_STATE), jnp.float32), 'A_im': jnp.tile(jnp.pi * jnp.arange(N_STATE, dtype=jnp.float32), (DT, 1)), 'C_re': jax.random.normal(ks[10], (DT, N_STATE), jnp.float32) * 0.5 ** 0.5, 'C_im': jax.random.normal(ks[11], (DT, N_STATE), jnp.float32) * 0.5 ** 0.5, 'D_skip': jax.random.normal(ks[12], (DT,), jnp.float32), 'mod_gate': jnp.array(0.5, jnp.float32)}
        return inp
    _L0_xattn_all = _L0_xattn_setup()
    _L0_xattn_in = {k: v for k, v in _L0_xattn_all.items() if k in ('Wq', 'Wk', 'Wv', 'W_film_in', 'b_film_in', 'W_film_out', 'b_film_out', 'g_norm_in', 'b_norm_in', 'g_norm_out', 'b_norm_out', 'g_ffn', 'b_ffn', 'W1', 'b1', 'W2', 'b2', 'log_dt', 'A_re', 'A_im', 'C_re', 'C_im', 'D_skip', 'mod_gate')}
    del _L0_xattn_all

    def _L0_attn_setup():
        import jax, jax.numpy as jnp
        import numpy as np
        D_MODEL = 256
        HEADS = 16
        SCALE = float(np.sqrt(D_MODEL / HEADS))
        key = jax.random.key(seed)
        ks = jax.random.split(key, 5)
        B, S, D = (4, 512, D_MODEL)
        q = jax.random.normal(ks[0], (B, S, D), dtype=jnp.float32)
        init = 0.02
        wq = jax.random.normal(ks[1], (D, D), dtype=jnp.float32) * init
        wk = jax.random.normal(ks[2], (D, D), dtype=jnp.float32) * init
        wv = jax.random.normal(ks[3], (D, D), dtype=jnp.float32) * init
        wo = jax.random.normal(ks[4], (D, D), dtype=jnp.float32) * init
        return {'q': q, 'wq': wq, 'wk': wk, 'wv': wv, 'wo': wo}
    _L0_attn_all = _L0_attn_setup()
    _L0_attn_in = {k: v for k, v in _L0_attn_all.items() if k in ('wq', 'wk', 'wv', 'wo')}
    del _L0_attn_all

    def _L0_ffn_setup():
        import jax, jax.numpy as jnp
        import numpy as np
        D_MODEL = 256
        D_FF = 1024
        N_EXPERTS = 8
        D_EXPERT = D_FF // N_EXPERTS
        TOP_K = 2
        LB_WEIGHT = 0.01
        B, S = (4, 512)

        def _top_k_softmax(logits, k):
            vals, _ = jax.lax.top_k(logits, k)
            thresh = vals[..., -1:]
            masked = jnp.where(logits >= thresh, logits, -jnp.inf)
            return jax.nn.softmax(masked, axis=-1)
        key = jax.random.key(seed)
        ks = jax.random.split(key, 8)
        x = jax.random.normal(ks[0], (B, S, D_MODEL), dtype=jnp.float32)
        w1 = jax.random.normal(ks[1], (N_EXPERTS, D_MODEL, D_EXPERT), dtype=jnp.float32) * (1.0 / np.sqrt(D_MODEL))
        b1 = jnp.zeros((N_EXPERTS, D_EXPERT), dtype=jnp.float32)
        w2 = jax.random.normal(ks[2], (N_EXPERTS, D_EXPERT, D_MODEL), dtype=jnp.float32) * (1.0 / np.sqrt(D_EXPERT))
        b2 = jnp.zeros((N_EXPERTS, D_MODEL), dtype=jnp.float32)
        centroids = jax.random.normal(ks[3], (N_EXPERTS, D_MODEL), dtype=jnp.float32) * 0.02
        w_route = jax.random.normal(ks[4], (N_EXPERTS, D_MODEL), dtype=jnp.float32) * (1.0 / np.sqrt(D_MODEL))
        return {'x': x, 'w1': w1, 'b1': b1, 'w2': w2, 'b2': b2, 'centroids': centroids, 'w_route': w_route}
    _L0_ffn_all = _L0_ffn_setup()
    _L0_ffn_in = {k: v for k, v in _L0_ffn_all.items() if k in ('w1', 'b1', 'w2', 'b2', 'centroids', 'w_route')}
    del _L0_ffn_all
    return {'x': x, 'ctx_768': ctx_768, 'mask_BxS_bf1': mask_BxS_bf1, 'mask_BxS2_bf1': mask_BxS2_bf1, 'L0_xattn_Wq': _L0_xattn_in['Wq'], 'L0_xattn_Wk': _L0_xattn_in['Wk'], 'L0_xattn_Wv': _L0_xattn_in['Wv'], 'L0_xattn_W_film_in': _L0_xattn_in['W_film_in'], 'L0_xattn_b_film_in': _L0_xattn_in['b_film_in'], 'L0_xattn_W_film_out': _L0_xattn_in['W_film_out'], 'L0_xattn_b_film_out': _L0_xattn_in['b_film_out'], 'L0_xattn_g_norm_in': _L0_xattn_in['g_norm_in'], 'L0_xattn_b_norm_in': _L0_xattn_in['b_norm_in'], 'L0_xattn_g_norm_out': _L0_xattn_in['g_norm_out'], 'L0_xattn_b_norm_out': _L0_xattn_in['b_norm_out'], 'L0_xattn_g_ffn': _L0_xattn_in['g_ffn'], 'L0_xattn_b_ffn': _L0_xattn_in['b_ffn'], 'L0_xattn_W1': _L0_xattn_in['W1'], 'L0_xattn_b1': _L0_xattn_in['b1'], 'L0_xattn_W2': _L0_xattn_in['W2'], 'L0_xattn_b2': _L0_xattn_in['b2'], 'L0_xattn_log_dt': _L0_xattn_in['log_dt'], 'L0_xattn_A_re': _L0_xattn_in['A_re'], 'L0_xattn_A_im': _L0_xattn_in['A_im'], 'L0_xattn_C_re': _L0_xattn_in['C_re'], 'L0_xattn_C_im': _L0_xattn_in['C_im'], 'L0_xattn_D_skip': _L0_xattn_in['D_skip'], 'L0_xattn_mod_gate': _L0_xattn_in['mod_gate'], 'L0_attn_wq': _L0_attn_in['wq'], 'L0_attn_wk': _L0_attn_in['wk'], 'L0_attn_wv': _L0_attn_in['wv'], 'L0_attn_wo': _L0_attn_in['wo'], 'L0_ffn_w1': _L0_ffn_in['w1'], 'L0_ffn_b1': _L0_ffn_in['b1'], 'L0_ffn_w2': _L0_ffn_in['w2'], 'L0_ffn_b2': _L0_ffn_in['b2'], 'L0_ffn_centroids': _L0_ffn_in['centroids'], 'L0_ffn_w_route': _L0_ffn_in['w_route']}

def reference(x, ctx_768, mask_BxS_bf1, mask_BxS2_bf1, L0_xattn_Wq, L0_xattn_Wk, L0_xattn_Wv, L0_xattn_W_film_in, L0_xattn_b_film_in, L0_xattn_W_film_out, L0_xattn_b_film_out, L0_xattn_g_norm_in, L0_xattn_b_norm_in, L0_xattn_g_norm_out, L0_xattn_b_norm_out, L0_xattn_g_ffn, L0_xattn_b_ffn, L0_xattn_W1, L0_xattn_b1, L0_xattn_W2, L0_xattn_b2, L0_xattn_log_dt, L0_xattn_A_re, L0_xattn_A_im, L0_xattn_C_re, L0_xattn_C_im, L0_xattn_D_skip, L0_xattn_mod_gate, L0_attn_wq, L0_attn_wk, L0_attn_wv, L0_attn_wo, L0_ffn_w1, L0_ffn_b1, L0_ffn_w2, L0_ffn_b2, L0_ffn_centroids, L0_ffn_w_route):
    import jax
    import jax.numpy as jnp

    def _L0_xattn_ref(x_text, x_vision, text_mask, vision_mask, Wq, Wk, Wv, W_film_in, b_film_in, W_film_out, b_film_out, g_norm_in, b_norm_in, g_norm_out, b_norm_out, g_ffn, b_ffn, W1, b1, W2, b2, log_dt, A_re, A_im, C_re, C_im, D_skip, mod_gate):
        import jax, jax.numpy as jnp
        import numpy as np
        B, T, DT, G, DV = (16, 128, 256, 144, 192)
        H, DH = (4, 32)
        INNER = H * DH
        HID = 4 * DT
        N_STATE = 64
        K_TOP = 32

        def layernorm(x, g, b, eps=1e-05):
            m = x.mean(-1, keepdims=True)
            v = x.var(-1, keepdims=True)
            return (x - m) * jax.lax.rsqrt(v + eps) * g + b

        def s4d(x, log_dt, A_re, A_im, C_re, C_im, D_skip):
            Bb, L, D = x.shape
            dt = jnp.exp(log_dt)
            A = A_re + 1j * A_im
            C = C_re + 1j * C_im
            dtA = dt[:, None] * A
            dC = C * (jnp.exp(dtA) - 1.0) / A
            powers = jnp.exp(dtA[:, :, None] * jnp.arange(L))
            K = 2.0 * jnp.einsum('dn,dnl->dl', dC, powers).real
            n = 2 * L
            Kf = jnp.fft.rfft(K, n=n, axis=-1)
            xf = jnp.fft.rfft(x, n=n, axis=1)
            y = jnp.fft.irfft(xf * Kf.T[None], n=n, axis=1)[:, :L]
            return y + x * D_skip
        Bb, Tt, D = x_text.shape
        Gg = x_vision.shape[1]
        Q = (x_text @ Wq).reshape(Bb, Tt, H, DH)
        K = (x_vision @ Wk).reshape(Bb, Gg, H, DH)
        scores = jnp.einsum('bthd,bghd->bhtg', Q, K) / np.sqrt(DH).astype(np.float32)
        scores = jnp.where(vision_mask[:, None, None, :], scores, -jnp.inf)
        topv, topi = jax.lax.top_k(scores, K_TOP)
        probs = jax.nn.softmax(topv, axis=-1)
        bi = jnp.arange(Bb)[:, None, None, None]
        hi = jnp.arange(H)[None, :, None, None]
        ti = jnp.arange(Tt)[None, None, :, None]
        attn = jnp.zeros_like(scores).at[bi, hi, ti, topi].set(probs)
        attn_mean = attn.mean(axis=1)
        V = x_vision @ Wv
        c_t = jnp.einsum('btg,bgd->btd', attn_mean, V)
        c_t = c_t * text_mask[..., None]
        x = layernorm(x_text, g_norm_in, b_norm_in)
        scale_in, shift_in = jnp.split(c_t @ W_film_in + b_film_in, 2, axis=-1)
        x = x * (1.0 + mod_gate * scale_in) + mod_gate * shift_in
        y = s4d(x, log_dt, A_re, A_im, C_re, C_im, D_skip)
        scale_out, shift_out = jnp.split(c_t @ W_film_out + b_film_out, 2, axis=-1)
        y = y * (1.0 + mod_gate * scale_out) + mod_gate * shift_out
        xt = x_text + y
        h = layernorm(xt, g_ffn, b_ffn)
        h = jax.nn.gelu(h @ W1 + b1, approximate=False) @ W2 + b2
        xt = xt + h
        return layernorm(xt, g_norm_out, b_norm_out)

    def _L0_attn_ref(q, wq, wk, wv, wo):
        import jax, jax.numpy as jnp
        import numpy as np
        D_MODEL = 256
        HEADS = 16
        SCALE = float(np.sqrt(D_MODEL / HEADS))
        B, S, D = q.shape
        Q = jnp.einsum('bsd,ed->bse', q, wq)
        K = jnp.einsum('bsd,ed->bse', q, wk)
        V = jnp.einsum('bsd,ed->bse', q, wv)
        scores = jnp.einsum('bqe,bke->bqk', Q, K) / SCALE
        attn = jax.nn.softmax(scores, axis=-1)
        out = jnp.einsum('bqk,bke->bqe', attn, V)
        out = jnp.transpose(out, (0, 2, 1)).reshape(B, S, D)
        return jnp.einsum('bsd,ed->bse', out, wo)

    def _L0_ffn_ref(x, w1, b1, w2, b2, centroids, w_route):
        import jax, jax.numpy as jnp
        import numpy as np
        D_MODEL = 256
        D_FF = 1024
        N_EXPERTS = 8
        D_EXPERT = D_FF // N_EXPERTS
        TOP_K = 2
        LB_WEIGHT = 0.01
        B, S = (4, 512)

        def _top_k_softmax(logits, k):
            vals, _ = jax.lax.top_k(logits, k)
            thresh = vals[..., -1:]
            masked = jnp.where(logits >= thresh, logits, -jnp.inf)
            return jax.nn.softmax(masked, axis=-1)
        eps = 1e-12
        x_norm = x / jnp.maximum(jnp.linalg.norm(x, axis=-1, keepdims=True), eps)
        c_norm = centroids / jnp.maximum(jnp.linalg.norm(centroids, axis=-1, keepdims=True), eps)
        cos_scores = jnp.einsum('bsd,ed->bse', x_norm, c_norm)
        route_scores = jnp.einsum('bsd,ed->bse', x, w_route)
        logits = cos_scores + route_scores
        gates = _top_k_softmax(logits, TOP_K)
        h = jax.nn.gelu(jnp.einsum('bsd,edh->bseh', x, w1) + b1, approximate=False)
        expert_out = jnp.einsum('bseh,ehd->bsed', h, w2) + b2
        out = jnp.einsum('bse,bsed->bsd', gates, expert_out)
        return out
    x = x + _L0_xattn_ref(_layernorm(x, axis=-1), ctx_768, mask_BxS_bf1, mask_BxS2_bf1, L0_xattn_Wq, L0_xattn_Wk, L0_xattn_Wv, L0_xattn_W_film_in, L0_xattn_b_film_in, L0_xattn_W_film_out, L0_xattn_b_film_out, L0_xattn_g_norm_in, L0_xattn_b_norm_in, L0_xattn_g_norm_out, L0_xattn_b_norm_out, L0_xattn_g_ffn, L0_xattn_b_ffn, L0_xattn_W1, L0_xattn_b1, L0_xattn_W2, L0_xattn_b2, L0_xattn_log_dt, L0_xattn_A_re, L0_xattn_A_im, L0_xattn_C_re, L0_xattn_C_im, L0_xattn_D_skip, L0_xattn_mod_gate)
    x = x + _L0_attn_ref(_layernorm(x, axis=-1), L0_attn_wq, L0_attn_wk, L0_attn_wv, L0_attn_wo)
    x = x + _L0_ffn_ref(_layernorm(x, axis=-1), L0_ffn_w1, L0_ffn_b1, L0_ffn_w2, L0_ffn_b2, L0_ffn_centroids, L0_ffn_w_route)
    return x

_drawn_inputs = setup_inputs


def setup_inputs(seed=0):
    import zlib

    import numpy as np

    out = dict(_drawn_inputs(seed))
    spreads = {'L0_xattn_b_film_in': (0.0, 0.1),
     'L0_xattn_b_film_out': (0.0, 0.1),
     'L0_xattn_g_norm_in': (1.0, 0.2),
     'L0_xattn_b_norm_in': (0.0, 0.1),
     'L0_xattn_g_norm_out': (1.0, 0.2),
     'L0_xattn_b_norm_out': (0.0, 0.1),
     'L0_xattn_g_ffn': (1.0, 0.6),
     'L0_xattn_b_ffn': (0.0, 0.657),
     'L0_xattn_b1': (0.0, 0.314),
     'L0_xattn_b2': (0.0, 0.1),
     'L0_xattn_A_re': (-0.5, 0.6),
     'L0_ffn_b1': (0.0, 0.307),
     'L0_ffn_b2': (0.0, 0.1)}
    factors = {'L0_xattn_Wq': 12.839,
     'L0_xattn_Wk': 12.005,
     'L0_attn_wq': 4.899,
     'L0_attn_wk': 4.533,
     'L0_xattn_W_film_out': 2.785}
    for name, (base, spread) in spreads.items():
        noise = np.random.default_rng([zlib.crc32(name.encode()), seed]).standard_normal(out[name].shape)
        drawn = base * np.exp(spread * noise) if base else spread * noise
        out[name] = jnp.asarray(drawn.astype(out[name].dtype))
    for name, factor in factors.items():
        out[name] = (out[name] * factor).astype(out[name].dtype)
    return out
```

```python
from contextlib import ExitStack

import numpy as np
import concourse.bass as bass
from concourse import mybir
from concourse.alu_op_type import AluOpType as ALU

F32 = mybir.dt.float32
I32 = mybir.dt.int32
U8 = mybir.dt.uint8
ACT = mybir.ActivationFunctionType
AXX = mybir.AxisListType.X
ET = mybir.EngineType

NB, T, D = 64, 32, 256
G, DV = 257, 192
H, DH = 4, 32
TOPK, NS = 32, 64
HID, NE = 1024, 8
BT = 128 // T
NT = NB // BT
EPS = 1e-5
SCALE = float(1.0 / np.sqrt(np.float32(DH)))
TAKEN = -3.0e38
MASKED = 1.0e30
MAGIC = 12582912.0
RSQRT0 = float(0x5F3759DF)
TWO_PI = 2 * np.pi
PI_HI = 6.28125
PI_LO = float(TWO_PI - 6.28125)
PI_IN = 3.1415925
WEXP = [0, 1, 2, 3, 4, 5, 6, 7, 0, 8, 16, 24, 0, 8, 16, 24, 1]
NP, NPOW = 12, len(WEXP)


class Tile:

    def __init__(self, base, c):
        self.base, self.c, self.p = base, c, c % 2
        self.static = isinstance(base, int)
        self.n = base + c

    def count(self, per, more):
        if self.static:
            v = per * (self.base + self.c) + more
            return v if v > 0 else None
        return self.base * per + (per * self.c + more)

    def half(self, per, more):
        if self.static:
            v = per * ((self.base + self.c) // 2) + more
            return v if v > 0 else None
        return self.base * (per // 2) + (per * (self.c // 2) + more)


def wait(eng, sem, value):
    if value is not None:
        eng.wait_ge(sem, value)


def wait_apart(eng, sem, value, passed):
    wait(eng, sem, value)
    if value is not None and not isinstance(value, int):
        eng.sem_inc(passed, 1)


def build(nc, d, out):
    with ExitStack() as ctx:
        def sb(name, shape, dt=F32):
            return ctx.enter_context(nc.sbuf_tensor(name, shape, dt))

        def pb(name):
            return ctx.enter_context(nc.psum_tensor(name, [128, 512], F32))

        def sem(name):
            return ctx.enter_context(nc.semaphore(name))

        mask_dram = nc.dram_tensor("mask_scratch", [NT, BT * G], F32, kind="Internal").ap()
        any_dram = nc.dram_tensor("any_scratch", [NB, 1], F32, kind="Internal").ap()

        x_all = sb("x_all", [128, NT, D])
        ident = sb("ident", [128, 128])
        sel = sb("sel", [128, T])
        block_mask = sb("block_mask", [128, BT, T])
        wq = sb("wq", [128, 2, 128])
        wk_pad = sb("wk_pad", [128, H, DV])
        film1 = sb("film1", [128, 4 * D])
        film2 = sb("film2", [65, 4 * D])
        w1 = sb("w1", [128, 2, HID])
        w2 = sb("w2", [128, HID // 128, D])
        b1 = sb("b1", [128, HID // 128])
        b2 = sb("b2", [128, D])
        gout = sb("gout", [128, D])
        bout = sb("bout", [128, D])
        qk_w = sb("qk_w", [128, 2, D])
        wv_w = sb("wv_w", [128, 2, D])
        wo_w = sb("wo_w", [128, 2, D])
        route = sb("route", [128, 2, 2 * NE])
        e_w1 = sb("e_w1", [128, 2, HID])
        e_w2 = sb("e_w2", [128, NE, D])
        e_b1 = sb("e_b1", [128, NE])
        e_b2 = sb("e_b2", [NE, D])
        dft_x = sb("dft_x", [128, 3, 128])
        dft_y = sb("dft_y", [128, 3, 128])
        kern_f = sb("kern_f", [128, 3, D])
        text_m = sb("text_m", [128, NB])
        mean_x = sb("mean_x", [128, NT, 2])
        rs_x = sb("rs_x", [128, 2, NT])

        ctx_n = [sb(f"ctx_n{i}", [128, BT, 2, DV]) for i in range(2)]
        ctx_l = [sb(f"ctx_l{i}", [128, DV]) for i in range(2)]
        ctx_t1 = [sb(f"ctx_t1_{i}", [128, BT, G]) for i in range(2)]
        ctx_t2 = [sb(f"ctx_t2_{i}", [65, BT, G]) for i in range(2)]

        ang = sb("ang", [128, 2 * NPOW, D])
        expw = sb("expw", [128, NPOW, D])
        flat = {"ang": ang[:, :, :].rearrange("p a b -> p (a b)"), "expw": expw[:, :, :].rearrange("p a b -> p (a b)")}
        at = {"ang": 0, "expw": 0}

        def over(buf, *shape):
            n = int(np.prod(shape))
            v = flat[buf][:, at[buf]:at[buf] + n]
            at[buf] += n
            assert v.shape[1] == n
            if len(shape) == 1:
                return v
            if len(shape) == 2:
                return v.rearrange("p (a b) -> p a b", a=shape[0])
            return v.rearrange("p (a b c) -> p a b c", a=shape[0], b=shape[1])

        xln = [over("expw", D) for _ in range(2)]
        xhat = [over("expw", D) for _ in range(2)]
        xT = over("expw", D)
        qT = over("expw", 128)
        qk1 = over("expw", BT, H, T)
        work = over("expw", 2, G)
        expo = over("expw", 2, G)
        prob = over("expw", BT, G)
        am = over("expw", G)
        qk2 = sb("qk2", [65, BT, H, T])
        top = sb("top", [128, BT, TOPK])
        nmax = sb("nmax", [128, BT])
        psum_row = sb("psum_row", [128, BT])
        rsum_row = sb("rsum_row", [128, BT])
        tm_tile = sb("tm_tile", [128, BT])
        wsel = sb("wsel", [128, BT, T])
        amT = sb("amT", [128, 2, 128])
        z = sb("z", [128, DV])
        zT1 = sb("zT1", [128, 128])
        zT2 = sb("zT2", [65, 128])
        xf = over("ang", D)
        had = over("ang", 3, D)
        yb = over("ang", D)
        xt = over("ang", D)
        xt_b = over("ang", D)
        hn = over("ang", D)
        hT = over("ang", D)
        act1 = over("ang", HID // 128, 128)
        xt2 = over("ang", D)
        u_c = over("ang", D)
        xb_c = over("ang", D)
        x1 = over("ang", D)
        xl2 = over("ang", D)
        xT2 = over("ang", D)
        xmT = over("ang", D)
        v_c = over("ang", D)
        r_c = over("ang", 2, BT, T)
        x2 = [over("ang", D) for _ in range(2)]
        nmax_c = sb("nmax_c", [128, 1])
        p_c = sb("p_c", [128, T])
        sum_c = sb("sum_c", [128, 1])
        rsum_c = sb("rsum_c", [128, 1])
        pn_c = sb("pn_c", [128, T])
        pT_c = sb("pT_c", [128, T])
        pT_blk = sb("pT_blk", [128, BT, T])
        xl3 = over("ang", D)
        xT3 = over("ang", D)
        act2 = over("ang", NE, 128)
        acc = [over("ang", D) for _ in range(2)]
        dots = sb("dots", [128, 2 * NE])
        logit = sb("logit", [128, NE])
        best = sb("best", [128, NE])
        nbest = sb("nbest", [128, 1])
        e_d = sb("e_d", [128, NE])
        pg = sb("pg", [128, NE])
        sum_d = sb("sum_d", [128, 1])
        rsum_d = sb("rsum_d", [128, 1])
        gate = sb("gate", [128, NE])
        gateT = sb("gateT", [NE, 128])
        out_sb = [sb(f"out_sb{i}", [128, D]) for i in range(2)]
        bn = [sb(f"bn{i}", [128, 6]) for i in range(4)]
        mv = [sb(f"mv{i}", [128, 2]) for i in range(4)]
        var_in = [sb(f"var_in{i}", [128, 2]) for i in range(4)]
        rstd = [sb(f"rstd{i}", [128, 2]) for i in range(4)]
        nw_h = sb("nw_h", [128, 2 * NT])
        nw_t = sb("nw_t", [128, 2 * NT])
        inorm = sb("inorm", [128, 1])

        s4 = sb("s4", [128, 4, D])
        s4c = sb("s4c", [128, 8, D])
        s4a = sb("s4a", [128, 2, D])
        uu = sb("uu", [128, 4, D])
        brow = uu[0:65, :, :].rearrange("p a b -> p (a b)")
        logdt = sb("logdt", [128, D])
        phase = sb("phase", [128, 5])
        kern_t = sb("kern_t", [T, D])
        hot = sb("hot", [128, 2 * T - 1])
        one0 = sb("one0", [1, T])
        dskip = sb("dskip", [1, D])
        dft_k = sb("dft_k", [T, 3, 128])
        bn_x = sb("bn_x", [128, 2, 6])
        var_x = sb("var_x", [128, 2, NT])
        wvT = sb("wvT", [128, 2, DV])
        wff = s4c[:, :, :].rearrange("p (k a) b -> p k (a b)", k=2)
        brow2 = sb("brow2", [65, 3 * D])
        gin = sb("gin", [128, D])
        bin_ = sb("bin", [128, D])
        mgate = sb("mgate", [128, 1])
        film_t = sb("film_t", [128, D])
        gffn = sb("gffn", [128, 2])
        bffn = sb("bffn", [128, 2])
        b1raw = sb("b1raw", [128, HID // 128])
        awq = sb("awq", [128, 2, D])
        awk = sb("awk", [128, 2, D])
        cent = sb("cent", [NE, D])
        cent2 = ang[0:NE, 0, :]
        cent_s = sb("cent_s", [NE, 1])
        cent_r = sb("cent_r", [NE, 1])
        vm8 = sb("vm8", [NB, G], U8)
        valid = flat["ang"][0:NB, D:D + G]
        vm = sb("vm", [NB, G])
        anyv = sb("anyv", [NB, 3])
        anyb = sb("anyb", [128, NB])
        tm8 = sb("tm8", [128, NB], U8)

        S = [pb("S0"), pb("S1")]
        PA = pb("PA")
        B0, B1 = pb("B0"), pb("B1")
        C0 = pb("C0")
        D0, D1 = pb("D0"), pb("D1")

        names = ("ld_w ld_film ld_s4 ld_cent ld_any scratch_out wk_zero chain_v chain_a chain_g chain_p "
                 "bnx_done rsx_done ldx setup_dt setup_ang setup_exp setup_turn setup_red setup_sin setup_prod kt_mm kt_sb kf_mm kf_sb "
                 "film_mm film_sb b1_mm b1_sb qkw_mm qkw_sb cent_ss cent_rs cent_n cent_t setup_v ones_set tm_ready "
                 "xln_v xT_mm xT_a qT_mm qT_a qk_mm qk_a sc_mm mr1_v nmax_v exp_a prob_v rsum_v wsel_g am_mm am_a amT_mm amT_a z_mm z_v zT_mm zT_a "
                 "fin_mm xf_v fwd_mm had_v inv_mm y_a y_mm xt_v st0_v rs0_g xtb_g hn_v hT_mm hT_a w1a_mm w1b_mm ga_a gb_a h2_mm xt2_v st1_v rs1_g "
                 "xb_g x1_v st2_v rs2_g xl2_v xT2_mm xT2_a v_mm v_a s_mm nmaxc_v pc_a pt_v r_mm r_a o2_mm x2_v st3_v rs3_g inorm_g "
                 "xl3_v xT3_mm xT3_a lg_mm dots_a nbest_v ed_a gate_v gT_mm gT_a e1a_mm e1b_mm g2a_a g2b_a eo_mm acc_v fin_v bn_v av_v").split()
        s = {n: sem(n) for n in names}
        chains = {n: sem("self_" + n) for n in "tm c2 b0 c3 b1 bn0 bn1 bn2 bn3 top taken u xhat xf logit best pg rsd yb rsc pn pT".split()}
        passed_v, passed_g = sem("passed_v"), sem("passed_g")
        ld_ctx = [sem("ld_ctx0"), sem("ld_ctx1")]
        st_out = [sem("st_out0"), sem("st_out1")]

        LD_CENT, LD_S4, LD_FILM, LD_W = 16 * 7, 16 * 14, 16 * 8, 16 * 26

        LOOP0, LOOPS = 3, (NT - 3) // 2 * 2

        def run(engine, step):
            def tiles(base, first):
                return [Tile(base, first - k) if not isinstance(base, int) or 0 <= first - k < NT else None for k in range(4)]
            for n in range(LOOP0):
                step(*tiles(0, n))
            with nc.Fori(0, LOOPS - 1, 2, engines=(engine,)) as base:
                for n in range(2):
                    step(*tiles(base, LOOP0 + n))
            for n in range(LOOP0 + LOOPS, NT + 3):
                step(*tiles(0, n))

        block = ctx.enter_context(nc.Block())

        @block.sync
        def _(sp):
            def load(dst, src, to):
                sp.dma_start(dst, src).then_inc(s[to], 16)

            for k in range(4):
                load(x_all[:, 4 * k:4 * k + 4, :], d["x"][:, 4 * k:4 * k + 4, :], "ldx")
            load(vm8[:, :], d["vmask"], "ld_cent")
            load(ident[:, :], d["ident"], "ld_cent")
            load(cent[:, :], d["cent"], "ld_cent")
            for h in range(H):
                load(tm8[T * h:T * h + T, :], d["tmaskT"], "ld_cent")
            load(logdt[:, :], d["log_dt"].broadcast_to([128, D]), "ld_s4")
            for k, n in enumerate(("A_re", "A_im", "C_re", "C_im")):
                for half in range(2):
                    load(s4[NS * half:NS * half + NS, k, :], d[n], "ld_s4")
            load(phase[:, :], d["phase"], "ld_s4")
            load(hot[:, :], d["hot"], "ld_s4")
            load(one0[:, :], d["one0"], "ld_s4")
            load(dskip[:, :], d["D_skip"], "ld_s4")
            load(dft_k[:, :, :], d["dft_k"], "ld_s4")
            load(wvT[:, :, :], d["WvT"], "ld_film")
            load(wff[:, :, 0:2 * D], d["W_film_in"], "ld_film")
            load(wff[:, :, 2 * D:4 * D], d["W_film_out"], "ld_film")
            load(brow[64:65, 0:2 * D], d["b_film_in"], "ld_film")
            load(brow[64:65, 2 * D:4 * D], d["b_film_out"], "ld_film")
            load(gin[:, :], d["g_norm_in"].broadcast_to([128, D]), "ld_film")
            load(bin_[:, :], d["b_norm_in"].broadcast_to([128, D]), "ld_film")
            load(mgate[:, :], d["mod_gate"].broadcast_to([128, 1]), "ld_film")
            sp.wait_ge(s["wk_zero"], 1)
            for h in range(H):
                load(wk_pad[DH * h:DH * h + DH, h, :], d["WkT"][DH * h:DH * h + DH, :], "ld_w")
            load(wq[:, :, :], d["Wq"], "ld_w")
            load(sel[:, :], d["sel"], "ld_w")
            load(block_mask[:, :, :], d["block_mask"], "ld_w")
            load(dft_x[:, :, :], d["dft_x"], "ld_w")
            load(dft_y[:, :, :], d["dft_y"], "ld_w")
            load(w1[:, :, :], d["W1"], "ld_w")
            load(w2[:, :, :], d["W2"], "ld_w")
            load(b1raw[:, :], d["b1"], "ld_w")
            load(gffn[:, :], d["g_ffn"], "ld_w")
            load(bffn[:, :], d["b_ffn"], "ld_w")
            load(b2[:, :], d["b2"].broadcast_to([128, D]), "ld_w")
            load(gout[:, :], d["g_norm_out"].broadcast_to([128, D]), "ld_w")
            load(bout[:, :], d["b_norm_out"].broadcast_to([128, D]), "ld_w")
            load(awq[:, :, :], d["awq"], "ld_w")
            load(awk[:, :, :], d["awk"], "ld_w")
            load(wv_w[:, :, :], d["awvT"], "ld_w")
            load(wo_w[:, :, :], d["awoT"], "ld_w")
            load(route[:, :, 0:NE], d["routeT"], "ld_w")
            load(e_w1[:, :, :], d["e_w1"], "ld_w")
            load(e_w2[:, :, :], d["e_w2"], "ld_w")
            load(e_b1[:, :], d["e_b1"], "ld_w")
            load(e_b2[:, :], d["e_b2"], "ld_w")
            sp.wait_ge(s["setup_v"], 1)
            load(mask_dram.rearrange("a (b g) -> (a b) g", b=BT), vm[:, :], "scratch_out")
            load(any_dram, anyv[:, 2:3], "scratch_out")
            sp.wait_ge(s["scratch_out"], 32)
            load(anyb[:, :], any_dram.rearrange("b o -> o b").broadcast_to([128, NB]), "ld_any")

            def step(a, b, c, dd):
                if a:
                    wait(sp, s["z_v"], a.count(1, -1))
                    at = ld_ctx[a.p]
                    sp.dma_start(ctx_t1[a.p][:, :, :], d["ctxT1"][a.n]).then_inc(at, 16)
                    sp.dma_start(ctx_t2[a.p][0:64, :, :], d["ctxT2"][a.n]).then_inc(at, 16)
                    sp.dma_start(ctx_t2[a.p][64:65, :, :], mask_dram[a.n].rearrange("(o b g) -> o b g", o=1, b=BT)).then_inc(at, 16)
                    sp.dma_start(ctx_n[a.p][:, :, :, :], d["ctx_n"][a.n]).then_inc(at, 16)
                    for k in range(BT):
                        sp.dma_start(ctx_l[a.p][T * k:T * k + T, :], d["ctx_l"][a.n, k].broadcast_to([T, DV])).then_inc(at, 16)
                if dd:
                    wait(sp, s["fin_v"], dd.count(1, 1))
                    sp.dma_start(out[dd.n], out_sb[dd.p][:, :]).then_inc(st_out[dd.p], 16)

            step(Tile(0, 0), None, None, None)
            for n in range(LOOP0):
                step(Tile(0, n + 1), None, None, None)
            with nc.Fori(0, LOOPS - 1, 2, engines=(ET.SP,)) as base:
                for n in range(2):
                    step(Tile(base, LOOP0 + n + 1), None, None, Tile(base, n))
            for n in range(LOOP0 + LOOPS, NT + 3):
                step(Tile(0, n + 1) if n + 1 < NT else None, None, None, Tile(0, n - 3))
            for p in range(2):
                sp.wait_ge(st_out[p], 16 * NT // 2)

        N_CTX = 16 * (4 + BT)

        @block.gpsimd
        def _(pool):
            count = [0]

            def rsqrt_ops(w, y, h, t):
                yield lambda: nc.gpsimd.tensor_scalar(h, w, -0.5, None, ALU.mult)
                yield lambda: nc.gpsimd.tensor_scalar(y.bitcast(I32), w.bitcast(I32), -0.5, RSQRT0, ALU.mult, ALU.add)
                for _ in range(3):
                    yield lambda: nc.gpsimd.tensor_tensor(t, y, y, ALU.mult)
                    yield lambda: nc.gpsimd.tensor_tensor(t, t, h, ALU.mult)
                    yield lambda: nc.gpsimd.tensor_scalar(t, t, 1.5, None, ALU.add)
                    yield lambda: nc.gpsimd.tensor_tensor(y, y, t, ALU.mult)

            def chained(ops, done):
                ops = list(ops)
                for k, op in enumerate(ops):
                    ins = op()
                    if k + 1 < len(ops):
                        ins.then_inc(s["chain_g"], 1)
                        count[0] += 1
                        pool.wait_ge(s["chain_g"], count[0])
                    else:
                        ins.then_inc(s[done], 1)

            nc.gpsimd.memset(wk_pad[:, :, :], 0.0).then_inc(s["wk_zero"], 1)
            pool.wait_ge(s["wk_zero"], 1)
            nc.gpsimd.memset(qk2[64:65, :, :, :], 1.0).then_inc(s["ones_set"], 1)
            nc.gpsimd.memset(zT2[64:65, :], 1.0).then_inc(s["ones_set"], 1)
            pool.wait_ge(s["ones_set"], 2)
            pool.wait_ge(s["bnx_done"], 1)
            mean_v = mean_x[:, :, 1]
            chained([
                lambda: nc.gpsimd.tensor_scalar(var_x[:, 0, :], mean_v, EPS, None, ALU.add),
                lambda: nc.gpsimd.tensor_scalar(var_x[:, 1, :], mean_v, 1.0 + EPS, EPS * EPS, ALU.mult, ALU.add),
            ] + list(rsqrt_ops(var_x[:, :, :].rearrange("p a b -> p (a b)"), rs_x[:, :, :].rearrange("p a b -> p (a b)"), nw_h[:, :], nw_t[:, :])), "rsx_done")
            pool.wait_ge(s["cent_ss"], 1)
            chained(rsqrt_ops(cent_s[:, :], cent_r[:, :], nw_h[0:NE, 0:1], nw_t[0:NE, 0:1]), "cent_rs")

            pool.wait_ge(s["tm_ready"], 1)
            pool.wait_ge(s["kf_sb"], 1)
            pool.wait_ge(s["ld_w"], LD_W)

            def norm(k, tile):
                wait_apart(pool, s[f"st{k}_v"], tile.count(1, 1), passed_g)
                w, y, h, t = var_in[k][:, 0:1], rstd[k][:, 0:1], nw_h[:, 0:1], nw_t[:, 0:1]
                ops = [lambda: nc.gpsimd.tensor_scalar(w, mv[k][:, 1:2], EPS, None, ALU.add)]
                return ops + list(rsqrt_ops(w, y, h, t))

            def norm_experts(tile):
                wait_apart(pool, s["st3_v"], tile.count(1, 1), passed_g)
                w, y = var_in[3], rstd[3]
                ops = [lambda: nc.gpsimd.tensor_scalar(w[:, 0:1], mv[3][:, 1:2], EPS, None, ALU.add),
                       lambda: nc.gpsimd.tensor_copy(w[:, 1:2], mv[3][:, 1:2])]
                ops += list(rsqrt_ops(w[:, :], y[:, :], nw_h[:, 0:2], nw_t[:, 0:2]))
                ops += [lambda: nc.gpsimd.tensor_tensor(nw_t[:, 0:1], w[:, 0:1], y[:, 0:1], ALU.mult),
                        lambda: nc.gpsimd.tensor_tensor(nw_t[:, 0:1], nw_t[:, 0:1], y[:, 1:2], ALU.mult),
                        lambda: nc.gpsimd.tensor_scalar(inorm[:, :], nw_t[:, 0:1], float(D) ** -0.5, 1e12, ALU.mult, ALU.min)]
                return ops

            L1, L3 = 14, 18

            def step(a, b, c, dd):
                if c:
                    wait_apart(pool, s["x1_v"], c.count(1, 0), passed_g)
                    nc.gpsimd.tensor_tensor(xb_c[:, :], x_all[:, c.n, :], bout[:, :], ALU.add).then_inc(s["xb_g"], 1)
                    run_chain(norm(2, c), "rs2_g", "c2", c, L1)
                if b:
                    run_chain(norm(0, b), "rs0_g", "b0", b, L1)
                    nc.gpsimd.tensor_tensor(xt_b[:, :], xt[:, :], b2[:, :], ALU.add).then_inc(s["xtb_g"], 1)
                if a:
                    wait_apart(pool, s["am_mm"], a.count(1, 0), passed_g)
                    nc.gpsimd.tensor_copy(tm_tile[:, :], text_m[:, bass.ds(a.n * BT, BT)]).then_inc(chains["tm"], 1)
                    wait_apart(pool, chains["tm"], a.count(1, 1), passed_g)
                    for q in range(2):
                        wait_apart(pool, s["rsum_v"], a.count(2, q + 1), passed_g)
                        for k in (2 * q, 2 * q + 1):
                            ins = nc.gpsimd.tensor_scalar(wsel[:, k, :], sel[:, :], rsum_row[:, k:k + 1], tm_tile[:, k:k + 1], ALU.mult, ALU.mult)
                    ins.then_inc(s["wsel_g"], 1)
                if c:
                    run_chain(norm_experts(c), "inorm_g", "c3", c, L3)
                if b:
                    run_chain(norm(1, b), "rs1_g", "b1", b, L1)

            def run_chain(ops, done, name, tile, links):
                assert len(ops) == links + 1, (len(ops), name)
                for k, op in enumerate(ops):
                    ins = op()
                    if k < links:
                        ins.then_inc(chains[name], 1)
                        wait_apart(pool, chains[name], tile.count(links, k + 1), passed_g)
                    else:
                        ins.then_inc(s[done], 1)

            run(ET.Pool, step)

        @block.scalar
        def _(act):
            A = nc.scalar.activation
            act.wait_ge(s["ld_s4"], LD_S4)
            A(logdt[:, :], logdt[:, :], ACT.Exp).then_inc(s["setup_dt"], 1)
            act.wait_ge(s["setup_ang"], 1)
            for j, power in enumerate(WEXP):
                ins = A(expw[:, j, :], s4a[:, 0, :], ACT.Exp, scale=float(power))
            ins.then_inc(s["setup_exp"], 1)
            act.wait_ge(s["setup_red"], 1)
            A(ang[:, 0:NPOW, :], ang[:, 0:NPOW, :], ACT.Sin).then_inc(s["setup_sin"], 1)
            act.wait_ge(s["kt_mm"], 1)
            A(kern_t[:, :], D1[0:T, 0:D], ACT.Copy).then_inc(s["kt_sb"], 1)
            act.wait_ge(s["kf_mm"], 1)
            for k in range(2):
                A(kern_f[:, k, :], D1[:, k * D:(k + 1) * D], ACT.Copy)
            A(kern_f[:, 2, :], D0[:, 0:D], ACT.Copy).then_inc(s["kf_sb"], 1)

            def copy(dst, src, done):
                A(dst, src, ACT.Copy).then_inc(s[done], 1)

            def step(a, b, c, dd):
                one = lambda t: t.count(1, 1)
                if a:
                    wait(act, s["xT_mm"], one(a))
                    copy(xT[:, :], PA[:, 0:D], "xT_a")
                if dd:
                    wait(act, s["xT3_mm"], one(dd))
                    copy(xT3[:, :], D0[:, 0:D], "xT3_a")
                if a:
                    wait(act, s["qT_mm"], one(a))
                    copy(qT[:, :], PA[:, D:D + 128], "qT_a")
                    wait(act, s["qk_mm"], one(a))
                    A(qk1[:, :, :, :].rearrange("p b h t -> p h b t"), S[0][:, :].rearrange("p (h b t) -> p h b t", h=H, b=BT), ACT.Copy)
                    A(qk2[0:64, :, :, :].rearrange("p b h t -> p h b t"), S[1][0:64, :].rearrange("p (h b t) -> p h b t", h=H, b=BT), ACT.Copy).then_inc(s["qk_a"], 1)
                if dd:
                    wait(act, s["lg_mm"], one(dd))
                    copy(dots[:, :], D0[:, D:D + 2 * NE], "dots_a")

                def exps(q):
                    for k in range(2):
                        wait(act, s["nmax_v"], a.count(2, q + 1))
                        wait(act, s["mr1_v"], a.count(4, 2 * q + k + 1))
                        if k == 0:
                            wait(act, s["prob_v"], a.count(4, 2 * q))
                        A(expo[:, k, :], S[k][:, 0:G], ACT.Exp, bias=nmax[:, 2 * q + k:2 * q + k + 1], scale=SCALE).then_inc(s["exp_a"], 1)
                if a:
                    exps(0)
                if c:
                    wait(act, s["xT2_mm"], one(c))
                    copy(xT2[:, :], C0[:, 0:D], "xT2_a")
                if b:
                    wait(act, s["inv_mm"], one(b))
                    copy(yb[:, :], B0[:, D:2 * D], "y_a")
                if c:
                    wait(act, s["v_mm"], one(c))
                    A(xmT[:, :], C0[:, D:2 * D], ACT.Copy)
                    copy(v_c[:, :], C0[:, 0:D], "v_a")
                if dd:
                    wait(act, s["nbest_v"], one(dd))
                    A(e_d[:, :], logit[:, :], ACT.Exp, bias=nbest[:, :]).then_inc(s["ed_a"], 1)
                if c:
                    wait(act, s["nmaxc_v"], one(c))
                    A(p_c[:, :], C0[:, D:D + T], ACT.Exp, bias=nmax_c[:, :], accum_out=sum_c[:, :]).then_inc(s["pc_a"], 1)
                if a:
                    exps(1)
                if dd:
                    wait(act, s["gT_mm"], one(dd))
                    copy(gateT[:, :], D0[0:NE, 384:512], "gT_a")
                if c:
                    wait(act, s["r_mm"], one(c))
                    A(r_c[:, :, :, :].rearrange("p j b t -> p b j t"), C0[:, D:2 * D].rearrange("p (b j t) -> p b j t", b=BT, j=2), ACT.Copy).then_inc(s["r_a"], 1)
                if b:
                    wait(act, s["hT_mm"], one(b))
                    copy(hT[:, :], B0[:, 0:D], "hT_a")
                    for half, (bank, mm, done) in enumerate(((B1, "w1a_mm", "ga_a"), (B0, "w1b_mm", "gb_a"))):
                        wait(act, s[mm], one(b))
                        for k in range(4):
                            ins = A(act1[:, 4 * half + k, :], bank[:, 128 * k:128 * k + 128], ACT.Gelu, bias=b1[:, 4 * half + k:4 * half + k + 1])
                        ins.then_inc(s[done], 1)
                if a:
                    wait(act, s["am_mm"], one(a))
                    copy(am[:, :], PA[:, 0:G], "am_a")
                if dd:
                    for half, (bank, mm, done) in enumerate(((D1, "e1a_mm", "g2a_a"), (D0, "e1b_mm", "g2b_a"))):
                        wait(act, s[mm], one(dd))
                        for k in range(4):
                            ins = A(act2[:, 4 * half + k, :], bank[:, 128 * k:128 * k + 128], ACT.Gelu, bias=e_b1[:, 4 * half + k:4 * half + k + 1])
                        ins.then_inc(s[done], 1)
                if a:
                    wait(act, s["amT_mm"], one(a))
                    copy(amT[:, :, :].rearrange("p a b -> p (a b)"), PA[:, 0:256], "amT_a")
                    wait(act, s["zT_mm"], one(a))
                    A(zT1[:, :], PA[:, 256:384], ACT.Copy)
                    A(zT2[0:64, :], PA[0:64, 384:512], ACT.Copy).then_inc(s["zT_a"], 1)

            run(ET.Activation, step)

        @block.vector
        def _(dve):
            V = nc.vector
            n_chain = [0]

            def link(ins):
                ins.then_inc(s["chain_v"], 1)
                n_chain[0] += 1
                dve.wait_ge(s["chain_v"], n_chain[0])

            dve.wait_ge(s["ldx"], 64)
            for t in range(NT):
                V.bn_stats(bn_x[:, t % 2, :], x_all[:, t, :]).then_inc(s["bn_v"], 1)
                dve.wait_ge(s["bn_v"], t + 1)
                ins = V.bn_aggr(mean_x[:, t, :], bn_x[:, t % 2, :])
            ins.then_inc(s["bnx_done"], 1)
            dve.wait_ge(s["ld_cent"], LD_CENT)
            link(V.tensor_copy(valid, vm8[:, :]))
            V.tensor_scalar(vm[:, :], valid, MASKED, -MASKED, ALU.mult, ALU.add)
            link(V.reduce_max(anyv[:, 0:1], valid, AXX))
            link(V.reciprocal(anyv[:, 1:2], anyv[:, 0:1]))
            V.tensor_tensor(anyv[:, 2:3], anyv[:, 0:1], anyv[:, 1:2], ALU.mult).then_inc(s["setup_v"], 1)
            link(V.tensor_tensor(cent2[:, :], cent[:, :], cent[:, :], ALU.mult))
            V.reduce_sum(cent_s[:, :], cent2[:, :], AXX).then_inc(s["cent_ss"], 1)
            dve.wait_ge(s["setup_dt"], 1)
            V.tensor_tensor(s4a[:, 0, :], logdt[:, :], s4[:, 0, :], ALU.mult).then_inc(s["setup_ang"], 1)
            link(V.tensor_tensor(s4a[:, 1, :], logdt[:, :], s4[:, 1, :], ALU.mult))
            for j, power in enumerate(WEXP):
                ins = V.tensor_scalar(ang[:, j, :], s4a[:, 1, :], float(power), None, ALU.mult)
            link(ins)
            turn = lambda a, b: ang[:, NPOW + a:NPOW + b, :]
            V.tensor_scalar(turn(0, NP), ang[:, 0:NP, :], 1 / TWO_PI, phase[:, 0:1], ALU.mult, ALU.add)
            link(V.tensor_scalar(turn(NP, NPOW), ang[:, NP:NPOW, :], 1 / TWO_PI, phase[:, 1:2], ALU.mult, ALU.add))
            link(V.tensor_scalar(turn(0, NPOW), turn(0, NPOW), MAGIC, -MAGIC, ALU.add, ALU.add))
            link(V.scalar_tensor_tensor(ang[:, 0:NPOW, :], turn(0, NPOW), -PI_HI, ang[:, 0:NPOW, :], ALU.mult, ALU.add))
            link(V.scalar_tensor_tensor(ang[:, 0:NPOW, :], turn(0, NPOW), -PI_LO, ang[:, 0:NPOW, :], ALU.mult, ALU.add))
            V.tensor_scalar(ang[:, 0:NP, :], ang[:, 0:NP, :], phase[:, 2:3], PI_IN, ALU.add, ALU.min)
            link(V.tensor_scalar(ang[:, NP:NPOW, :], ang[:, NP:NPOW, :], phase[:, 3:4], PI_IN, ALU.add, ALU.min))
            V.tensor_scalar(ang[:, 0:NPOW, :], ang[:, 0:NPOW, :], -PI_IN, None, ALU.max).then_inc(s["setup_red"], 1)
            dve.wait_ge(s["ld_film"], LD_FILM)
            dve.wait_ge(s["film_mm"], 1)
            for rows, f_in, f_out, dst in ((slice(0, 128), B0, B1, film1), (slice(0, 64), D0, D1, film2)):
                V.scalar_tensor_tensor(dst[rows, 0:D], f_in[rows, 0:D], mgate[rows, :], gin[rows, :], ALU.mult, ALU.mult)
                link(V.scalar_tensor_tensor(film_t[rows, :], f_in[rows, 0:D], mgate[rows, :], bin_[rows, :], ALU.mult, ALU.mult))
                V.scalar_tensor_tensor(dst[rows, D:2 * D], f_in[rows, D:2 * D], mgate[rows, :], film_t[rows, :], ALU.mult, ALU.add)
                link(V.tensor_scalar(dst[rows, 2 * D:4 * D], f_out[rows, :], mgate[rows, :], None, ALU.mult))
            r = slice(64, 65)
            link(V.tensor_scalar(brow2[r, 0:D], brow[r, 0:D], mgate[r, :], 1.0, ALU.mult, ALU.add))
            V.tensor_tensor(film2[r, 0:D], brow2[r, 0:D], gin[r, :], ALU.mult)
            link(V.tensor_tensor(brow2[r, D:2 * D], brow2[r, 0:D], bin_[r, :], ALU.mult))
            V.scalar_tensor_tensor(film2[r, D:2 * D], brow[r, D:2 * D], mgate[r, :], brow2[r, D:2 * D], ALU.mult, ALU.add)
            V.tensor_scalar(film2[r, 2 * D:3 * D], brow[r, 2 * D:3 * D], mgate[r, :], 1.0, ALU.mult, ALU.add)
            V.tensor_scalar(film2[r, 3 * D:4 * D], brow[r, 3 * D:4 * D], mgate[r, :], None, ALU.mult).then_inc(s["film_sb"], 1)
            dve.wait_ge(s["setup_exp"], 1)
            dve.wait_ge(s["setup_sin"], 1)
            link(V.tensor_tensor(expw[:, :, :], expw[:, :, :], ang[:, 0:NPOW, :], ALU.mult))
            lo, hi = slice(0, NS), slice(NS, 2 * NS)
            wr, wi = s4c[:, 0, :], s4c[:, 1, :]
            V.tensor_scalar(s4c[lo, 0, :], expw[lo, 1, :], -1.0, None, ALU.add)
            V.tensor_scalar(s4c[hi, 0, :], expw[hi, NPOW - 1, :], -1.0, None, ALU.add)
            V.tensor_copy(s4c[lo, 1, :], expw[lo, NPOW - 1, :])
            link(V.tensor_copy(s4c[hi, 1, :], expw[hi, 1, :]))
            are, aim, cre, cim = (s4[:, k, :] for k in range(4))
            t0, t1, t2, t3, t4, t5 = (s4c[:, k, :] for k in range(2, 8))
            tt = lambda o, a, b, op: V.tensor_tensor(o, a, b, op)
            tt(t0, cre, wr, ALU.mult)
            tt(t1, cim, wi, ALU.mult)
            tt(t2, cre, wi, ALU.mult)
            tt(t3, cim, wr, ALU.mult)
            tt(t4, are, are, ALU.mult)
            link(tt(t5, aim, aim, ALU.mult))
            tt(t0, t0, t1, ALU.subtract)
            tt(t2, t2, t3, ALU.add)
            link(tt(t4, t4, t5, ALU.add))
            V.reciprocal(t5, t4)
            tt(t1, t0, are, ALU.mult)
            tt(t3, t2, aim, ALU.mult)
            tt(wr, t2, are, ALU.mult)
            link(tt(wi, t0, aim, ALU.mult))
            tt(t1, t1, t3, ALU.add)
            link(tt(wr, wi, wr, ALU.subtract))
            tt(t1, t1, t5, ALU.mult)
            link(tt(t3, wr, t5, ALU.mult))
            link(V.tensor_scalar(t1, t1, phase[:, 4:5], None, ALU.mult))
            wide = lambda v: v.rearrange("p (o b) -> p o b", o=1).broadcast_to([128, 4, D])
            tt(uu[:, :, :], expw[:, 8:12, :], wide(t1), ALU.mult)
            link(tt(expw[:, 12:16, :], expw[:, 12:16, :], wide(t3), ALU.mult))
            link(tt(uu[:, :, :], uu[:, :, :], expw[:, 12:16, :], ALU.add))
            for k in range(4):
                ins = tt(ang[:, 8 * k:8 * k + 8, :], expw[:, 0:8, :], uu[:, k, :].rearrange("p (o b) -> p o b", o=1).broadcast_to([128, 8, D]), ALU.mult)
            ins.then_inc(s["setup_prod"], 1)
            dve.wait_ge(s["b1_mm"], 1)
            V.tensor_tensor(b1[:, :], PA[:, 0:HID // 128], b1raw[:, :], ALU.add)
            for k in range(2):
                V.tensor_scalar(w1[:, k, :], w1[:, k, :], gffn[:, k:k + 1], None, ALU.mult)
            dve.wait_ge(s["qkw_mm"], 1)
            V.tensor_scalar(qk_w[:, :, :].rearrange("p a b -> p (a b)"), C0[:, :], 0.25, None, ALU.mult).then_inc(s["b1_sb"], 1)
            dve.wait_ge(s["cent_rs"], 1)
            link(V.tensor_scalar(cent_r[:, :], cent_r[:, :], 1e12, None, ALU.min))
            V.tensor_scalar(cent[:, :], cent[:, :], cent_r[:, :], None, ALU.mult).then_inc(s["cent_n"], 1)
            dve.wait_ge(s["cent_t"], 1)
            V.tensor_copy(route[:, :, NE:2 * NE], PA[:, 32:32 + 2 * NE].rearrange("p (a b) -> p a b", a=2)).then_inc(s["qkw_sb"], 1)
            dve.wait_ge(s["ld_any"], 16)
            link(V.tensor_copy(text_m[:, :], tm8[:, :]))
            V.scalar_tensor_tensor(text_m[:, :], text_m[:, :], 1.0 / H, anyb[:, :], ALU.mult, ALU.mult).then_inc(s["tm_ready"], 1)
            dve.wait_ge(s["rsx_done"], 1)
            dve.wait_ge(s["kf_sb"], 1)

            def stats(k, src, tile, done):
                V.bn_stats(bn[k][:, :], src).then_inc(chains[f"bn{k}"], 1)
                wait_apart(dve, chains[f"bn{k}"], tile.count(1, 1), passed_v)
                V.bn_aggr(mv[k][:, :], bn[k][:, :]).then_inc(s[done], 1)

            def step(a, b, c, dd):
                one = lambda t: t.count(1, 1)

                def first(q):
                    for k in range(2):
                        wait_apart(dve, s["sc_mm"], a.count(4, 2 * q + k + 1), passed_v)
                        V.max(top[:, 2 * q + k, 0:8], S[k][:, 0:G]).then_inc(chains["top"], 1)
                    wait(dve, chains["top"], a.count(16, 8 * q + 2))
                    V.tensor_scalar(nmax[:, 2 * q:2 * q + 2], top[:, 2 * q:2 * q + 2, 0], -SCALE, None, ALU.mult).then_inc(s["nmax_v"], 1)
                    for k in range(2):
                        V.match_replace(work[:, k, :], top[:, 2 * q + k, 0:8], S[k][:, 0:G], TAKEN).then_inc(s["mr1_v"], 1)

                def rounds(q, which):
                    for r8 in which:
                        for k in range(2):
                            if r8 == 1:
                                wait_apart(dve, s["mr1_v"], a.count(4, 2 * q + k + 1), passed_v)
                            else:
                                wait_apart(dve, chains["taken"], a.count(12, 6 * q + 2 * (r8 - 2) + k + 1), passed_v)
                            V.max(top[:, 2 * q + k, 8 * r8:8 * r8 + 8], work[:, k, :]).then_inc(chains["top"], 1)
                        for k in range(2):
                            wait_apart(dve, chains["top"], a.count(16, 8 * q + 2 * r8 + k + 1), passed_v)
                            V.match_replace(work[:, k, :], top[:, 2 * q + k, 8 * r8:8 * r8 + 8], work[:, k, :], TAKEN).then_inc(chains["taken"], 1)

                def probs(q):
                    wait(dve, s["am_mm"], a.count(1, 0))
                    for k in range(2):
                        wait(dve, chains["taken"], a.count(12, 6 * q + 4 + k + 1))
                        wait(dve, s["exp_a"], a.count(4, 2 * q + k + 1))
                        V.scalar_tensor_tensor(prob[:, 2 * q + k, :], work[:, k, :], TAKEN, expo[:, k, :], ALU.is_equal, ALU.mult,
                                               accum_out=psum_row[:, 2 * q + k:2 * q + k + 1]).then_inc(s["prob_v"], 1)
                    wait(dve, s["prob_v"], a.count(4, 2 * q + 2))
                    wait(dve, s["wsel_g"], a.count(1, 0))
                    V.reciprocal(rsum_row[:, 2 * q:2 * q + 2], psum_row[:, 2 * q:2 * q + 2]).then_inc(s["rsum_v"], 1)

                if c:
                    wait(dve, s["rs1_g"], one(c))
                    V.tensor_scalar(u_c[:, :], xt2[:, :], mv[1][:, 0:1], rstd[1][:, 0:1], ALU.subtract, ALU.mult).then_inc(chains["u"], 1)
                if dd:
                    wait(dve, s["inorm_g"], one(dd))
                    V.tensor_scalar(xl3[:, :], x2[dd.p][:, :], mv[3][:, 0:1], rstd[3][:, 0:1], ALU.subtract, ALU.mult).then_inc(s["xl3_v"], 1)
                if c:
                    wait(dve, chains["u"], c.count(2, 1))
                    V.tensor_tensor(u_c[:, :], u_c[:, :], gout[:, :], ALU.mult).then_inc(chains["u"], 1)
                if a:
                    V.tensor_scalar(xln[a.p][:, :], x_all[:, a.n, :], mean_x[:, a.n, 0:1], rs_x[:, 0, bass.ds(a.n, 1)], ALU.subtract, ALU.mult).then_inc(s["xln_v"], 1)
                    V.tensor_scalar(xhat[a.p][:, :], x_all[:, a.n, :], mean_x[:, a.n, 0:1], rs_x[:, 1, bass.ds(a.n, 1)], ALU.subtract, ALU.mult).then_inc(chains["xhat"], 1)
                if c:
                    wait(dve, chains["u"], c.count(2, 2))
                    wait(dve, s["xb_g"], one(c))
                    V.tensor_tensor(x1[:, :], u_c[:, :], xb_c[:, :], ALU.add).then_inc(s["x1_v"], 1)
                    wait(dve, s["x1_v"], one(c))
                    stats(2, x1[:, :], c, "st2_v")
                if b:
                    wait(dve, s["fin_mm"], one(b))
                    wait(dve, chains["xhat"], one(b))
                    V.tensor_tensor(xf[:, :], xhat[b.p][:, :], B0[:, 0:D], ALU.mult).then_inc(chains["xf"], 1)
                    wait(dve, chains["xf"], one(b))
                    V.tensor_tensor(xf[:, :], xf[:, :], B0[:, D:2 * D], ALU.add).then_inc(s["xf_v"], 1)
                if a:
                    first(0)
                if dd:
                    wait(dve, s["dots_a"], one(dd))
                    V.scalar_tensor_tensor(logit[:, :], dots[:, NE:2 * NE], inorm[:, :], dots[:, 0:NE], ALU.mult, ALU.add).then_inc(chains["logit"], 1)
                if a:
                    rounds(0, (1,))
                if dd:
                    wait_apart(dve, chains["logit"], one(dd), passed_v)
                    V.max(best[:, :], logit[:, :]).then_inc(chains["best"], 1)
                if b:
                    wait(dve, s["fwd_mm"], one(b))
                    V.tensor_tensor(had[:, 0:2, :].rearrange("p a b -> p (a b)"), B1[:, :], kern_f[:, 0:2, :].rearrange("p a b -> p (a b)"), ALU.mult)
                    V.tensor_tensor(had[:, 2, :], B0[:, 0:D], kern_f[:, 2, :], ALU.mult).then_inc(s["had_v"], 1)
                if dd:
                    wait(dve, chains["best"], one(dd))
                    V.tensor_scalar(nbest[:, :], best[:, 0:1], -1.0, None, ALU.mult).then_inc(s["nbest_v"], 1)
                if a:
                    rounds(0, (2, 3))
                if c:
                    wait(dve, s["rs2_g"], one(c))
                    V.tensor_scalar(xl2[:, :], x1[:, :], mv[2][:, 0:1], rstd[2][:, 0:1], ALU.subtract, ALU.mult).then_inc(s["xl2_v"], 1)
                if dd:
                    wait(dve, s["ed_a"], one(dd))
                    V.scalar_tensor_tensor(pg[:, :], logit[:, :], best[:, 1:2], e_d[:, :], ALU.is_ge, ALU.mult, accum_out=sum_d[:, :]).then_inc(chains["pg"], 1)
                if a:
                    probs(0)
                if dd:
                    wait(dve, chains["pg"], one(dd))
                    V.reciprocal(rsum_d[:, :], sum_d[:, :]).then_inc(chains["rsd"], 1)
                if b:
                    wait(dve, s["y_a"], one(b))
                    wait(dve, s["y_mm"], one(b))
                    V.tensor_tensor(yb[:, :], yb[:, :], B1[:, 0:D], ALU.mult).then_inc(chains["yb"], 1)
                if dd:
                    wait(dve, chains["rsd"], one(dd))
                    V.tensor_scalar(gate[:, :], pg[:, :], rsum_d[:, :], None, ALU.mult).then_inc(s["gate_v"], 1)
                if b:
                    wait(dve, chains["yb"], b.count(2, 1))
                    V.tensor_tensor(yb[:, :], yb[:, :], B1[:, D:2 * D], ALU.add).then_inc(chains["yb"], 1)
                    wait(dve, chains["yb"], b.count(2, 2))
                    V.tensor_tensor(xt[:, :], yb[:, :], xln[b.p][:, :], ALU.add).then_inc(s["xt_v"], 1)
                    wait(dve, s["xt_v"], one(b))
                    stats(0, xt[:, :], b, "st0_v")
                if a:
                    first(1)
                    rounds(1, (1,))
                if c:
                    wait(dve, s["s_mm"], one(c))
                    V.reduce_max(nmax_c[:, :], C0[:, D:D + T], AXX, negate=True).then_inc(s["nmaxc_v"], 1)
                if a:
                    rounds(1, (2,))
                if c:
                    wait(dve, s["pc_a"], one(c))
                    V.reciprocal(rsum_c[:, :], sum_c[:, :]).then_inc(chains["rsc"], 1)
                if a:
                    rounds(1, (3,))
                if c:
                    wait(dve, chains["rsc"], one(c))
                    V.tensor_scalar(pn_c[:, :], p_c[:, :], rsum_c[:, :], None, ALU.mult).then_inc(chains["pn"], 1)
                if b:
                    wait(dve, s["rs0_g"], one(b))
                    V.tensor_scalar(hn[:, :], xt[:, :], mv[0][:, 0:1], rstd[0][:, 0:1], ALU.subtract, ALU.mult).then_inc(s["hn_v"], 1)
                if c:
                    wait_apart(dve, chains["pn"], one(c), passed_v)
                    V.transpose(pT_c[:, :], pn_c[:, :]).then_inc(chains["pT"], 1)
                if a:
                    probs(1)
                if c:
                    wait(dve, chains["pT"], one(c))
                    V.tensor_tensor(pT_blk[:, :, :], pT_c[:, :].rearrange("p (o t) -> p o t", o=1).broadcast_to([128, BT, T]), block_mask[:, :, :], ALU.mult).then_inc(s["pt_v"], 1)
                    wait(dve, s["o2_mm"], one(c))
                    V.tensor_tensor(x2[c.p][:, :], x1[:, :], C0[:, 0:D], ALU.add).then_inc(s["x2_v"], 1)
                    wait(dve, s["x2_v"], one(c))
                    stats(3, x2[c.p][:, :], c, "st3_v")
                if b:
                    wait(dve, s["h2_mm"], one(b))
                    wait(dve, s["xtb_g"], one(b))
                    V.tensor_tensor(xt2[:, :], xt_b[:, :], B1[:, 0:D], ALU.add).then_inc(s["xt2_v"], 1)
                    wait(dve, s["xt2_v"], one(b))
                    stats(1, xt2[:, :], b, "st1_v")
                if a:
                    wait(dve, s["z_mm"], one(a))
                    V.scalar_tensor_tensor(z[:, :], ctx_l[a.p][:, :], am[:, G - 1:G], PA[:, 0:DV], ALU.mult, ALU.add).then_inc(s["z_v"], 1)
                if dd:
                    for k in range(NE + 1):
                        bank = (D1, D0)[k // 2 % 2][:, k % 2 * D:k % 2 * D + D]
                        wait(dve, s["eo_mm"], dd.count(NE + 1, min(k // 2 * 2 + 2, NE + 1)))
                        if k == 0:
                            V.tensor_tensor(acc[0][:, :], x2[dd.p][:, :], bank, ALU.add).then_inc(s["acc_v"], 1)
                        elif k == 1:
                            V.tensor_scalar(acc[1][:, :], bank, gate[:, 0:1], None, ALU.mult).then_inc(s["acc_v"], 1)
                        else:
                            wait(dve, s["acc_v"], dd.count(NE + 1, k - 1))
                            V.scalar_tensor_tensor(acc[k % 2][:, :], bank, gate[:, k - 1:k], acc[k % 2][:, :], ALU.mult, ALU.add).then_inc(s["acc_v"], 1)
                    wait(dve, s["acc_v"], dd.count(NE + 1, NE + 1))
                    wait(dve, st_out[dd.p], dd.half(16, 0))
                    V.tensor_tensor(out_sb[dd.p][:, :], acc[0][:, :], acc[1][:, :], ALU.add).then_inc(s["fin_v"], 1)

            run(ET.DVE, step)

        @block.tensor
        def _(pe):
            MM, TR = nc.tensor.matmul, nc.tensor.transpose
            pe.wait_ge(s["ld_cent"], LD_CENT)
            pe.wait_ge(s["ld_film"], LD_FILM)
            for rows, m, (f_in, f_out) in ((slice(0, 128), 128, (B0, B1)), (slice(128, 192), 64, (D0, D1))):
                for f, bank in enumerate((f_in, f_out)):
                    for k in range(2):
                        ins = MM(bank[0:m, :], wvT[:, k, rows], wff[:, k, f * 512:f * 512 + 512], start=k == 0, stop=k == 1)
            ins.then_inc(s["film_mm"], 1)
            pe.wait_ge(s["ld_w"], LD_W)
            for m in range(HID // 128):
                for k in range(2):
                    ins = MM(PA[:, m:m + 1], w1[:, k, 128 * m:128 * m + 128], bffn[:, k:k + 1], start=k == 0, stop=k == 1)
            ins.then_inc(s["b1_mm"], 1)
            for m in range(2):
                for k in range(2):
                    ins = MM(C0[:, m * D:m * D + D], awq[:, k, 128 * m:128 * m + 128], awk[:, k, :], start=k == 0, stop=k == 1)
            ins.then_inc(s["qkw_mm"], 1)
            pe.wait_ge(s["cent_n"], 1)
            pe.wait_ge(s["b1_sb"], 1)
            for k in range(2):
                ins = TR(PA[:, 32 + NE * k:32 + NE * k + NE], cent[:, 128 * k:128 * k + 128], ident[0:NE, 0:NE])
            ins.then_inc(s["cent_t"], 1)
            pe.wait_ge(s["film_sb"], 1)
            pe.wait_ge(s["setup_prod"], 1)
            for lag in range(T):
                MM(D1[0:T, 0:D], hot[:, T - 1 - lag:2 * T - 1 - lag], ang[:, lag, :], start=lag == 0, stop=False)
            MM(D1[0:T, 0:D], one0[:, :], dskip[:, :], start=False, stop=True).then_inc(s["kt_mm"], 1)
            pe.wait_ge(s["kt_sb"], 1)
            for k, bank in enumerate((D1[:, 0:D], D1[:, D:2 * D], D0[:, 0:D])):
                ins = MM(bank, dft_k[:, k, :], kern_t[:, :], start=True, stop=True)
            ins.then_inc(s["kf_mm"], 1)
            pe.wait_ge(s["kf_sb"], 1)
            pe.wait_ge(s["qkw_sb"], 1)
            pe.wait_ge(s["ones_set"], 2)

            def transposes(dst, src, done):
                for k in range(2):
                    ins = TR(dst[:, 128 * k:128 * k + 128], src[:, 128 * k:128 * k + 128], ident[:, :])
                ins.then_inc(s[done], 1)

            def step(a, b, c, dd):
                one = lambda t: t.count(1, 1)

                def scores(k):
                    wait(pe, s["qk_a"], one(a))
                    if k == 0:
                        pe_ctx = a.half(N_CTX, N_CTX)
                        wait(pe, ld_ctx[a.p], pe_ctx)
                    if k >= 2:
                        wait(pe, s["mr1_v"], a.count(4, k - 1))
                        wait(pe, s["exp_a"], a.count(4, k - 1))
                    bank = S[k % 2]
                    MM(bank[:, 0:G], qk1[:, k, :, :].rearrange("p h t -> p (h t)"), ctx_t1[a.p][:, k, :], start=True, stop=False)
                    MM(bank[:, 0:G], qk2[:, k, :, :].rearrange("p h t -> p (h t)"), ctx_t2[a.p][:, k, :], start=False, stop=True).then_inc(s["sc_mm"], 1)

                if a:
                    wait(pe, s["zT_a"], a.count(1, 0))
                    wait(pe, s["xln_v"], one(a))
                    transposes(PA, xln[a.p], "xT_mm")
                if dd:
                    wait(pe, s["xl3_v"], one(dd))
                    wait(pe, s["acc_v"], dd.count(NE + 1, 0))
                    transposes(D0, xl3, "xT3_mm")
                if b:
                    wait(pe, s["zT_a"], one(b))
                    wait(pe, s["gb_a"], b.count(1, 0))
                    MM(B0[:, :], zT1[:, :], film1[:, 0:512], start=True, stop=False)
                    MM(B0[:, :], zT2[:, :], film2[:, 0:512], start=False, stop=True).then_inc(s["fin_mm"], 1)
                if a:
                    wait(pe, s["xT_a"], one(a))
                    for k in range(2):
                        ins = MM(PA[:, D:D + 128], wq[:, k, :], xT[:, 128 * k:128 * k + 128], start=k == 0, stop=k == 1)
                    ins.then_inc(s["qT_mm"], 1)
                if dd:
                    wait(pe, s["xT3_a"], one(dd))
                    for k in range(2):
                        ins = MM(D0[:, D:D + 2 * NE], xT3[:, 128 * k:128 * k + 128], route[:, k, :], start=k == 0, stop=k == 1)
                    ins.then_inc(s["lg_mm"], 1)
                if a:
                    wait(pe, s["qT_a"], one(a))
                    wait(pe, s["mr1_v"], a.count(4, 0))
                    wait(pe, s["exp_a"], a.count(4, 0))
                    for h in range(H):
                        MM(S[0][:, 128 * h:128 * h + 128], wk_pad[:, h, 0:128], qT[:, :], start=True, stop=True)
                        ins = MM(S[1][0:64, 128 * h:128 * h + 128], wk_pad[:, h, 128:DV], qT[:, :], start=True, stop=True)
                    ins.then_inc(s["qk_mm"], 1)
                if b:
                    wait(pe, s["xf_v"], one(b))
                    wait(pe, s["xt2_v"], b.count(1, 0))
                    for k, bank in enumerate((B1[:, 0:D], B1[:, D:2 * D], B0[:, 0:D])):
                        ins = MM(bank, dft_x[:, k, :], xf[:, :], start=True, stop=True)
                    ins.then_inc(s["fwd_mm"], 1)
                if a:
                    scores(0)
                    scores(1)
                if c:
                    wait(pe, s["xl2_v"], one(c))
                    wait(pe, s["x2_v"], c.count(1, 0))
                    transposes(C0, xl2, "xT2_mm")
                if b:
                    wait(pe, s["had_v"], one(b))
                    for k in range(3):
                        ins = MM(B0[:, D:2 * D], dft_y[:, k, :], had[:, k, :], start=k == 0, stop=k == 2)
                    ins.then_inc(s["inv_mm"], 1)
                    MM(B1[:, :], zT1[:, :], film1[:, 512:1024], start=True, stop=False)
                    MM(B1[:, :], zT2[:, :], film2[:, 512:1024], start=False, stop=True).then_inc(s["y_mm"], 1)
                if c:
                    wait(pe, s["xT2_a"], one(c))
                    for m in range(2):
                        for k in range(2):
                            ins = MM(C0[:, D + 128 * m:D + 128 * m + 128], qk_w[:, k, 128 * m:128 * m + 128], xT2[:, 128 * k:128 * k + 128], start=k == 0, stop=k == 1)
                    for k in range(2):
                        ins = MM(C0[:, 0:D], xT2[:, 128 * k:128 * k + 128], wv_w[:, k, :], start=k == 0, stop=k == 1)
                    ins.then_inc(s["v_mm"], 1)
                    wait(pe, s["v_a"], one(c))
                    for k in range(BT):
                        rows = slice(T * k, T * k + T)
                        for m in range(2):
                            cols = slice(128 * m + T * k, 128 * m + T * k + T)
                            ins = MM(C0[rows, D:D + T], xmT[:, cols], xT2[:, cols], start=m == 0, stop=m == 1)
                    ins.then_inc(s["s_mm"], 1)
                if a:
                    scores(2)
                    scores(3)
                if dd:
                    wait(pe, s["gate_v"], one(dd))
                    TR(D0[0:NE, 384:512], gate[:, :], ident[:, :]).then_inc(s["gT_mm"], 1)
                if b:
                    wait(pe, s["hn_v"], one(b))
                    transposes(B0, hn, "hT_mm")
                if c:
                    wait(pe, s["pt_v"], one(c))
                    for k in range(BT):
                        for j in range(4):
                            vals = v_c[:, :].rearrange("p (j2 j t) -> p j2 j t", j2=2, j=4)[:, :, j, :]
                            o = C0[T * j:T * j + T, D + 64 * k:D + 64 * k + 64].rearrange("p (a t) -> p a t", a=2)
                            ins = MM(o, pT_blk[:, k, :], vals, start=True, stop=True)
                    ins.then_inc(s["r_mm"], 1)

                def wide(banks, w, xs, sems):
                    for half in range(2):
                        for m in range(4):
                            at = 128 * (4 * half + m)
                            for k in range(2):
                                ins = MM(banks[half][:, 128 * m:128 * m + 128], w[:, k, at:at + 128], xs[:, 128 * k:128 * k + 128], start=k == 0, stop=k == 1)
                        ins.then_inc(s[sems[half]], 1)

                if c:
                    wait(pe, s["r_a"], one(c))
                    for k in range(2):
                        ins = MM(C0[:, 0:D], r_c[:, k, :, :].rearrange("p b t -> p (b t)"), wo_w[:, k, :], start=k == 0, stop=k == 1)
                    ins.then_inc(s["o2_mm"], 1)
                if b:
                    wait(pe, s["hT_a"], one(b))
                    wait(pe, s["xt_v"], one(b))
                    wide((B1, B0), w1, hT, ("w1a_mm", "w1b_mm"))
                if dd:
                    wait(pe, s["dots_a"], one(dd))
                    wait(pe, s["gT_a"], one(dd))
                    wide((D1, D0), e_w1, xT3, ("e1a_mm", "e1b_mm"))
                if a:
                    wait(pe, s["prob_v"], a.count(4, 4))
                    wait(pe, s["wsel_g"], one(a))
                    for k in range(BT):
                        ins = MM(PA[T * k:T * k + T, 0:G], wsel[:, k, :], prob[:, k, :], start=True, stop=True)
                    ins.then_inc(s["am_mm"], 1)
                if b:
                    wait(pe, s["ga_a"], one(b))
                    for k in range(HID // 128):
                        if k == 4:
                            wait(pe, s["gb_a"], one(b))
                        ins = MM(B1[:, 0:D], act1[:, k, :], w2[:, k, :], start=k == 0, stop=k == HID // 128 - 1)
                    ins.then_inc(s["h2_mm"], 1)
                if a:
                    wait(pe, s["am_a"], one(a))
                    for k in range(2):
                        ins = TR(PA[:, 128 * k:128 * k + 128], am[:, 128 * k:128 * k + 128], ident[:, :])
                    ins.then_inc(s["amT_mm"], 1)

                def experts(ks):
                    for k in ks:
                        bank = (D1, D0)[k // 2 % 2][:, k % 2 * D:k % 2 * D + D]
                        if k <= 1:
                            wait(pe, s["g2a_a"], one(dd))
                        elif k == 2:
                            wait(pe, s["g2b_a"], one(dd))
                        elif k >= 4 and k % 2 == 0:
                            wait(pe, s["acc_v"], dd.count(NE + 1, k - 2))
                        if k == 0:
                            MM(bank, gateT[:, :], e_b2[:, :], start=True, stop=True).then_inc(s["eo_mm"], 1)
                        else:
                            MM(bank, act2[:, k - 1, :], e_w2[:, k - 1, :], start=True, stop=True).then_inc(s["eo_mm"], 1)
                if dd:
                    experts(range(0, 4))
                if a:
                    wait(pe, s["amT_a"], one(a))
                    for k in range(BT):
                        for m in range(2):
                            ins = MM(PA[T * k:T * k + T, 0:DV], amT[:, m, T * k:T * k + T], ctx_n[a.p][:, k, m, :], start=m == 0, stop=m == 1)
                    ins.then_inc(s["z_mm"], 1)
                    wait(pe, s["z_v"], one(a))
                    TR(PA[:, 256:384], z[:, 0:128], ident[:, :])
                    TR(PA[0:64, 384:512], z[:, 128:DV], ident[:, :]).then_inc(s["zT_mm"], 1)
                if dd:
                    experts(range(4, NE + 1))

            run(ET.PE, step)


def _constants():
    f = np.float32
    n = 2 * T
    ph = 2 * np.pi * np.outer(np.arange(1, T), np.arange(T)) / n
    C, S = np.cos(ph), -np.sin(ph)
    one, alt, nil = np.ones((1, T)), ((-1.0) ** np.arange(T))[None], np.zeros((1, T))
    fx = [np.vstack([C + S, one]), np.vstack([C, alt]), np.vstack([S, nil])]
    fk = [np.vstack([C, one]), np.vstack([S - C, alt]), np.vstack([C + S, nil])]
    fy = [np.vstack([(C + S) * 2 / n, one / n]), np.vstack([S * 2 / n, alt / n]), np.vstack([-C * 2 / n, nil])]
    eye = np.eye(BT)
    half = np.repeat([0.0, 1.0], NS)
    hot = np.zeros((128, 2 * T - 1), f)
    hot[:, T - 1] = 2.0
    one0 = np.zeros((1, T), f)
    one0[0, 0] = 1.0
    mask = np.kron(eye, np.ones((T, T)))
    return {
        "ident": np.eye(128, dtype=f),
        "sel": np.tile(np.eye(T, dtype=f), (H, 1)),
        "block_mask": mask.reshape(128, BT, T).astype(f),
        "dft_x": np.stack([np.kron(eye, m.T) for m in fx], 1).astype(f),
        "dft_y": np.stack([np.kron(eye, m) for m in fy], 1).astype(f),
        "dft_k": np.stack([np.tile(m.T, (1, BT)) for m in fk], 1).astype(f),
        "phase": np.stack([0.25 * (1 - half), 0.25 * half, np.pi / 2 * (1 - half), np.pi / 2 * half, 1 - 2 * half], 1).astype(f),
        "hot": hot,
        "one0": one0,
    }


def kernel(**inputs):
    import concourse.bacc as _bacc
    from concourse.bass_utils import run_bass_kernel_spmd as _run

    raw = {k: np.asarray(v) for k, v in inputs.items()}
    xa = lambda n: raw["L0_xattn_" + n]
    chunks = lambda w: w.reshape(-1, 128, w.shape[-1]).transpose(1, 0, 2)
    cols = lambda v: v.reshape(-1, 128).T
    context = raw["ctx_768"]
    ctxT = context.transpose(2, 0, 1).reshape(DV, NT, BT, G).transpose(1, 0, 2, 3)
    awvT = raw["L0_attn_wv"].T.reshape(D, T, 8).transpose(0, 2, 1).reshape(D, D)
    arrays = {
        "x": raw["x"].reshape(NT, 128, D).transpose(1, 0, 2),
        "ctx_n": context[:, :256].reshape(NT, BT, 2, 128, DV).transpose(0, 3, 1, 2, 4),
        "ctx_l": context[:, 256:].reshape(NT, BT, 1, DV),
        "ctxT1": ctxT[:, 0:128],
        "ctxT2": ctxT[:, 128:DV],
        "vmask": raw["mask_BxS2_bf1"].view(np.uint8),
        "tmaskT": raw["mask_BxS_bf1"].view(np.uint8).T,
        "Wq": chunks(xa("Wq")), "WkT": xa("Wk").T, "WvT": chunks(xa("Wv").T),
        "W_film_in": chunks(xa("W_film_in")), "W_film_out": chunks(xa("W_film_out")),
        "b_film_in": xa("b_film_in")[None], "b_film_out": xa("b_film_out")[None],
        "g_norm_in": xa("g_norm_in")[None], "b_norm_in": xa("b_norm_in")[None],
        "g_norm_out": xa("g_norm_out")[None], "b_norm_out": xa("b_norm_out")[None],
        "g_ffn": cols(xa("g_ffn")), "b_ffn": cols(xa("b_ffn")),
        "W1": chunks(xa("W1")), "b1": cols(xa("b1")), "W2": chunks(xa("W2")), "b2": xa("b2")[None],
        "log_dt": xa("log_dt")[None], "A_re": xa("A_re").T, "A_im": xa("A_im").T,
        "C_re": xa("C_re").T, "C_im": xa("C_im").T, "D_skip": xa("D_skip")[None],
        "mod_gate": xa("mod_gate").reshape(1, 1),
        "awq": chunks(raw["L0_attn_wq"]), "awk": chunks(raw["L0_attn_wk"]),
        "awvT": chunks(awvT), "awoT": chunks(raw["L0_attn_wo"].T),
        "routeT": chunks(raw["L0_ffn_w_route"].T), "cent": raw["L0_ffn_centroids"],
        "e_w1": chunks(raw["L0_ffn_w1"].transpose(1, 0, 2).reshape(D, HID)),
        "e_w2": raw["L0_ffn_w2"].transpose(1, 0, 2), "e_b1": raw["L0_ffn_b1"].T, "e_b2": raw["L0_ffn_b2"],
        **_constants(),
    }
    arrays = {f"in_{k}": np.ascontiguousarray(v) for k, v in arrays.items()}
    nc = _bacc.Bacc("TRN2", target_bir_lowering=False, num_devices=1)
    aps = {k[3:]: nc.dram_tensor(k, v.shape, mybir.dt.from_np(v.dtype), kind="ExternalInput").ap() for k, v in arrays.items()}
    out = nc.dram_tensor("out", (NT, 128, D), F32, kind="ExternalOutput").ap()
    build(nc, aps, out)
    r = _run(nc, [arrays], core_ids=[0])
    return r.results[0]["out"].reshape(NB, T, D)
```

```python
from contextlib import ExitStack

import numpy as np
import concourse.bass as bass
from concourse import mybir
from concourse.alu_op_type import AluOpType as ALU

F32 = mybir.dt.float32
I32 = mybir.dt.int32
U8 = mybir.dt.uint8
ACT = mybir.ActivationFunctionType
AXX = mybir.AxisListType.X
ET = mybir.EngineType

NB, T, D = 64, 32, 256
G, DV = 257, 192
H, DH = 4, 32
TOPK, NS = 32, 64
HID, NE = 1024, 8
BT = 128 // T
NT = NB // BT
EPS = 1e-5
SCALE = float(1.0 / np.sqrt(np.float32(DH)))
TAKEN = -3.0e38
MASKED = 1.0e30
MAGIC = 12582912.0
RSQRT0 = float(0x5F3759DF)
TWO_PI = 2 * np.pi
PI_HI = 6.28125
PI_LO = float(TWO_PI - 6.28125)
PI_IN = 3.1415925
WEXP = [0, 1, 2, 3, 4, 5, 6, 7, 8, 16, 24, 0, 8, 16, 24, 1]
NP, NPOW = 11, len(WEXP)


class Tile:

    def __init__(self, base, c):
        self.base, self.c, self.p = base, c, c % 2
        self.static = isinstance(base, int)
        self.n = base + c

    def count(self, per, more):
        if self.static:
            v = per * (self.base + self.c) + more
            return v if v > 0 else None
        return self.base * per + (per * self.c + more)

    def half(self, per, more):
        if self.static:
            v = per * ((self.base + self.c) // 2) + more
            return v if v > 0 else None
        return self.base * (per // 2) + (per * (self.c // 2) + more)


def wait(eng, sem, value):
    if value is not None:
        eng.wait_ge(sem, value)


def wait_apart(eng, sem, value, passed):
    wait(eng, sem, value)
    if value is not None and not isinstance(value, int):
        eng.sem_inc(passed, 1)


def build(nc, d, out):
    with ExitStack() as ctx:
        def sb(name, shape, dt=F32):
            return ctx.enter_context(nc.sbuf_tensor(name, shape, dt))

        def pb(name):
            return ctx.enter_context(nc.psum_tensor(name, [128, 512], F32))

        def sem(name):
            return ctx.enter_context(nc.semaphore(name))

        mask_dram = nc.dram_tensor("mask_scratch", [NT, BT * G], F32, kind="Internal").ap()
        any_dram = nc.dram_tensor("any_scratch", [NB, 1], F32, kind="Internal").ap()

        x_all = sb("x_all", [128, NT, D])
        ident = sb("ident", [128, 128])
        sel = sb("sel", [128, T])
        block_mask = sb("block_mask", [128, BT, T])
        wq = sb("wq", [128, 2, 128])
        wk_pad = sb("wk_pad", [128, H, DV])
        film1 = sb("film1", [128, 4 * D])
        film2 = sb("film2", [65, 4 * D])
        w1 = sb("w1", [128, 2, HID])
        expw = sb("expw", [128, NPOW, D])
        w2 = expw[:, 0:HID // 128, :]
        b1 = sb("b1", [128, HID // 128])
        b2 = sb("b2", [128, D])
        gout = sb("gout", [128, D])
        bout = sb("bout", [128, D])
        qk_w = sb("qk_w", [128, 2, D])
        wv_w = sb("wv_w", [128, 2, D])
        wo_w = sb("wo_w", [128, 2, D])
        route = sb("route", [128, 2, 2 * NE])
        e_w1 = sb("e_w1", [128, 2, HID])
        e_w2 = expw[:, HID // 128:HID // 128 + NE, :]
        e_b1 = sb("e_b1", [128, NE])
        e_b2 = sb("e_b2", [NE, D])
        dft_x = sb("dft_x", [128, 3, 128])
        dft_y = sb("dft_y", [128, 3, 128])
        kern_f = sb("kern_f", [128, 3, D])
        text_m = sb("text_m", [128, NB])
        mean_x = sb("mean_x", [128, NT, 2])
        rs_x = sb("rs_x", [128, 2, NT])

        ctx_n = [sb(f"ctx_n{i}", [128, BT, 2, DV]) for i in range(2)]
        ctx_l = [sb(f"ctx_l{i}", [128, DV]) for i in range(2)]
        ctx_t1 = [sb(f"ctx_t1_{i}", [128, BT, G]) for i in range(2)]
        ctx_t2 = [sb(f"ctx_t2_{i}", [65, BT, G]) for i in range(2)]

        ang = sb("ang", [128, 2 * NPOW, D])
        flat = {"ang": ang[:, :, :].rearrange("p a b -> p (a b)")}
        at = {"ang": 0}

        def over(buf, *shape):
            n = int(np.prod(shape))
            v = flat[buf][:, at[buf]:at[buf] + n]
            at[buf] += n
            assert v.shape[1] == n
            if len(shape) == 1:
                return v
            if len(shape) == 2:
                return v.rearrange("p (a b) -> p a b", a=shape[0])
            return v.rearrange("p (a b c) -> p a b c", a=shape[0], b=shape[1])

        xln = [sb(f"xln{i}", [128, D]) for i in range(2)]
        xhat = [sb(f"xhat{i}", [128, D]) for i in range(2)]
        xT = sb("xT", [128, D])
        qT = sb("qT", [128, 128])
        qk1 = sb("qk1", [128, BT, H, T])
        work = sb("work", [128, BT, G])
        expo = sb("expo", [128, BT, G])
        prob = sb("prob", [128, BT, G])
        am = sb("am", [128, G])
        qk2 = sb("qk2", [65, BT, H, T])
        top = sb("top", [128, BT, TOPK])
        nmax = sb("nmax", [128, BT])
        psum_row = sb("psum_row", [128, BT])
        rsum_row = sb("rsum_row", [128, BT])
        tm_tile = sb("tm_tile", [128, BT])
        wsel = sb("wsel", [128, BT, T])
        amT = sb("amT", [128, 2, 128])
        z = sb("z", [128, DV])
        zT1 = sb("zT1", [128, 128])
        zT2 = sb("zT2", [65, 128])
        xf = over("ang", D)
        had = over("ang", 3, D)
        yb = over("ang", D)
        xt = over("ang", D)
        xt_b = over("ang", D)
        hn = over("ang", D)
        hT = over("ang", D)
        act1 = over("ang", HID // 128, 128)
        xt2 = over("ang", D)
        u_c = over("ang", D)
        xb_c = over("ang", D)
        x1 = over("ang", D)
        xl2 = over("ang", D)
        xT2 = over("ang", D)
        xmT = over("ang", D)
        v_c = over("ang", D)
        r_c = over("ang", 2, BT, T)
        x2 = [over("ang", D) for _ in range(2)]
        nmax_c = sb("nmax_c", [128, 1])
        p_c = sb("p_c", [128, T])
        sum_c = sb("sum_c", [128, 1])
        rsum_c = sb("rsum_c", [128, 1])
        pn_c = sb("pn_c", [128, T])
        pT_c = sb("pT_c", [128, T])
        pT_blk = sb("pT_blk", [128, BT, T])
        xl3 = over("ang", D)
        xT3 = over("ang", D)
        act2 = over("ang", NE, 128)
        acc = [over("ang", D) for _ in range(2)]
        dots = sb("dots", [128, 2 * NE])
        logit = sb("logit", [128, NE])
        best = sb("best", [128, NE])
        nbest = sb("nbest", [128, 1])
        e_d = sb("e_d", [128, NE])
        pg = sb("pg", [128, NE])
        sum_d = sb("sum_d", [128, 1])
        rsum_d = sb("rsum_d", [128, 1])
        gate = sb("gate", [128, NE])
        gateT = sb("gateT", [NE, 128])
        out_sb = [sb(f"out_sb{i}", [128, D]) for i in range(2)]
        bn = [sb(f"bn{i}", [128, 6]) for i in range(4)]
        mv = [sb(f"mv{i}", [128, 2]) for i in range(4)]
        var_in = [sb(f"var_in{i}", [128, 4]) for i in range(4)]
        rstd = [sb(f"rstd{i}", [128, 1]) for i in range(4)]
        nw_h = sb("nw_h", [128, 2 * NT])
        nw_t = sb("nw_t", [128, 2 * NT])
        inorm = sb("inorm", [128, 1])

        s4 = sb("s4", [128, 4, D])
        s4c = sb("s4c", [128, 8, D])
        s4a = sb("s4a", [128, 2, D])
        uu = sb("uu", [128, 4, D])
        brow = uu[0:65, :, :].rearrange("p a b -> p (a b)")
        logdt = sb("logdt", [128, D])
        phase = sb("phase", [128, 9])
        kern_t = sb("kern_t", [T, D])
        hot = sb("hot", [128, 2 * T - 1])
        one0 = sb("one0", [1, T])
        dskip = sb("dskip", [1, D])
        dft_k = sb("dft_k", [T, 3, 128])
        bn_x = sb("bn_x", [128, 2, 6])
        var_x = sb("var_x", [128, 2, NT])
        wff = s4c[:, :, :].rearrange("p (k a) b -> p k (a b)", k=2)
        brow2 = sb("brow2", [65, 3 * D])
        gin = sb("gin", [128, D])
        bin_ = sb("bin", [128, D])
        mgate = sb("mgate", [128, 1])
        film_t = sb("film_t", [128, D])
        gffn = sb("gffn", [128, 2])
        bffn = sb("bffn", [128, 2])
        b1raw = sb("b1raw", [128, HID // 128])
        awq = e_w1[:, 0, 0:2 * D].rearrange("p (a b) -> p a b", a=2)
        awk = e_w1[:, 0, 2 * D:4 * D].rearrange("p (a b) -> p a b", a=2)
        wvT = e_w1[:, 1, 0:2 * DV].rearrange("p (a b) -> p a b", a=2)
        cent = sb("cent", [NE, D])
        cent2 = ang[0:NE, 0, :]
        cent_s = sb("cent_s", [NE, 1])
        cent_r = sb("cent_r", [NE, 1])
        vm8 = sb("vm8", [NB, G], U8)
        valid = flat["ang"][0:NB, D:D + G]
        vm = sb("vm", [NB, G])
        anyv = sb("anyv", [NB, 3])
        anyb = sb("anyb", [128, NB])
        tm8 = sb("tm8", [128, NB], U8)

        S = [pb("S0"), pb("S1")]
        PA = pb("PA")
        B0, B1 = pb("B0"), pb("B1")
        C0 = pb("C0")
        D0, D1 = pb("D0"), pb("D1")

        names = ("ld_w ld_film ld_s4 ld_cent ld_any scratch_out wk_zero chain_v chain_a chain_g chain_p "
                 "bnx_done rsx_done ldx setup_dt setup_ang setup_mul setup_exp setup_turn setup_red setup_sin setup_prod kt_mm kt_sb kf_mm kf_sb "
                 "film_mm film_sb b1_mm w1_sb b1_sb ld_w2 qkw_mm qkw_sb cent_ss cent_rs cent_n cent_t setup_v ones_set tm_ready "
                 "xln_v xT_mm xT_a qT_mm qT_a qk_mm qk_a sc_mm mr1_v nmax_v exp_a prob_v rsum_v wsel_g am_mm am_a amT_mm amT_a z_mm z_v zT_mm zT_a "
                 "fin_mm xf_v fwd_mm had_v inv_mm y_a y_mm xt_v st0_v rs0_g xtb_g hn_v hT_mm hT_a w1a_mm w1b_mm ga_a gb_a h2_mm xt2_v st1_v rs1_g "
                 "xb_g x1_v st2_v rs2_g xl2_v xT2_mm xT2_a v_mm v_a s_mm nmaxc_v pc_a pt_v r_mm r_a o2_mm x2_v st3_v rs3_g inorm_g "
                 "xl3_v xT3_mm xT3_a lg_mm dots_a nbest_v ed_a gate_v gT_mm gT_a e1a_mm e1b_mm g2a_a g2b_a eo_mm acc_v fin_v bn_v av_v").split()
        s = {n: sem(n) for n in names}
        chains = {n: sem("self_" + n) for n in "tm g0 g1 g2 g3 len bn0 bn1 bn2 bn3 top taken u xhat xf logit best pg rsd yb rsc pn pT".split()}
        passed_v, passed_g = sem("passed_v"), sem("passed_g")
        ld_ctx = [sem("ld_ctx0"), sem("ld_ctx1")]
        st_out = [sem("st_out0"), sem("st_out1")]

        LD_CENT, LD_S4, LD_FILM, LD_W, LD_W2 = 16 * 13, 16 * 14, 16 * 8, 16 * 17, 16 * 3

        LOOP0, LOOPS = 3, (NT - 3) // 2 * 2

        def tiles(base, first):
            return [Tile(base, first - k) if not isinstance(base, int) or 0 <= first - k < NT else None for k in range(4)]

        def run(engine, step):
            for n in range(1, LOOP0):
                step(*tiles(0, n))
            with nc.Fori(0, LOOPS - 1, 2, engines=(engine,)) as base:
                for n in range(2):
                    step(*tiles(base, LOOP0 + n))
            for n in range(LOOP0 + LOOPS, NT + 3):
                step(*tiles(0, n))

        block = ctx.enter_context(nc.Block())

        @block.sync
        def _(sp):
            def load(dst, src, to):
                sp.dma_start(dst, src).then_inc(s[to], 16)

            for k in range(4):
                load(x_all[:, 4 * k:4 * k + 4, :], d["x"][:, 4 * k:4 * k + 4, :], "ldx")
            load(vm8[:, :], d["vmask"], "ld_cent")
            load(ident[:, :], d["ident"], "ld_cent")
            load(cent[:, :], d["cent"], "ld_cent")
            load(sel[:, :], d["sel"], "ld_cent")
            load(wq[:, :, :], d["Wq"], "ld_cent")
            for h in range(H):
                load(tm8[T * h:T * h + T, :], d["tmaskT"], "ld_cent")
            sp.wait_ge(s["wk_zero"], 1)
            for h in range(H):
                load(wk_pad[DH * h:DH * h + DH, h, :], d["WkT"][DH * h:DH * h + DH, :], "ld_cent")
            load(logdt[:, :], d["log_dt"].broadcast_to([128, D]), "ld_s4")
            for k, n in enumerate(("A_re", "A_im", "C_re", "C_im")):
                for half in range(2):
                    load(s4[NS * half:NS * half + NS, k, :], d[n], "ld_s4")
            load(phase[:, :], d["phase"], "ld_s4")
            load(hot[:, :], d["hot"], "ld_s4")
            load(one0[:, :], d["one0"], "ld_s4")
            load(dskip[:, :], d["D_skip"], "ld_s4")
            load(dft_k[:, :, :], d["dft_k"], "ld_s4")
            sp.wait_ge(s["setup_v"], 1)
            load(mask_dram.rearrange("a (b g) -> (a b) g", b=BT), vm[:, :], "scratch_out")
            load(any_dram, anyv[:, 2:3], "scratch_out")
            sp.wait_ge(s["scratch_out"], 32)
            load(anyb[:, :], any_dram.rearrange("b o -> o b").broadcast_to([128, NB]), "ld_any")
            late_loads = [
                (wvT, d["WvT"], "ld_film"), (wff[:, :, 0:2 * D], d["W_film_in"], "ld_film"), (wff[:, :, 2 * D:4 * D], d["W_film_out"], "ld_film"),
                (brow[64:65, 0:2 * D], d["b_film_in"], "ld_film"), (brow[64:65, 2 * D:4 * D], d["b_film_out"], "ld_film"),
                (gin[:, :], d["g_norm_in"].broadcast_to([128, D]), "ld_film"), (bin_[:, :], d["b_norm_in"].broadcast_to([128, D]), "ld_film"),
                (mgate[:, :], d["mod_gate"].broadcast_to([128, 1]), "ld_film"),
                (dft_x[:, :, :], d["dft_x"], "ld_w"), (dft_y[:, :, :], d["dft_y"], "ld_w"), (block_mask[:, :, :], d["block_mask"], "ld_w"),
                (w1[:, :, :], d["W1"], "ld_w"), (b1raw[:, :], d["b1"], "ld_w"), (gffn[:, :], d["g_ffn"], "ld_w"), (bffn[:, :], d["b_ffn"], "ld_w"),
                (b2[:, :], d["b2"].broadcast_to([128, D]), "ld_w"), (gout[:, :], d["g_norm_out"].broadcast_to([128, D]), "ld_w"),
                (bout[:, :], d["b_norm_out"].broadcast_to([128, D]), "ld_w"), (awq, d["awq"], "ld_w"), (awk, d["awk"], "ld_w"),
                (wv_w[:, :, :], d["awvT"], "ld_w"), (wo_w[:, :, :], d["awoT"], "ld_w"), (route[:, :, 0:NE], d["routeT"], "ld_w"),
                (e_b1[:, :], d["e_b1"], "ld_w"), (e_b2[:, :], d["e_b2"], "ld_w"),
            ]

            def step(a, b, c, dd):
                if a:
                    wait(sp, s["z_v"], a.count(1, -1))
                    at = ld_ctx[a.p]
                    sp.dma_start(ctx_t1[a.p][:, :, :], d["ctxT1"][a.n]).then_inc(at, 16)
                    sp.dma_start(ctx_t2[a.p][0:64, :, :], d["ctxT2"][a.n]).then_inc(at, 16)
                    sp.dma_start(ctx_t2[a.p][64:65, :, :], mask_dram[a.n].rearrange("(o b g) -> o b g", o=1, b=BT)).then_inc(at, 16)
                    sp.dma_start(ctx_n[a.p][:, :, :, :], d["ctx_n"][a.n]).then_inc(at, 16)
                    for k in range(BT):
                        sp.dma_start(ctx_l[a.p][T * k:T * k + T, :], d["ctx_l"][a.n, k].broadcast_to([T, DV])).then_inc(at, 16)
                if dd:
                    wait(sp, s["fin_v"], dd.count(1, 1))
                    sp.dma_start(out[dd.n], out_sb[dd.p][:, :]).then_inc(st_out[dd.p], 16)

            step(Tile(0, 0), None, None, None)
            for dst, src, to in late_loads:
                load(dst, src, to)
            step(Tile(0, 1), None, None, None)
            sp.wait_ge(s["qkw_mm"], 1)
            load(e_w1[:, :, :], d["e_w1"], "ld_w2")
            sp.wait_ge(s["setup_prod"], 1)
            load(w2, d["W2"], "ld_w2")
            load(e_w2, d["e_w2"], "ld_w2")
            for n in range(1, LOOP0):
                step(Tile(0, n + 1), None, None, None)
            with nc.Fori(0, LOOPS - 1, 2, engines=(ET.SP,)) as base:
                for n in range(2):
                    step(Tile(base, LOOP0 + n + 1), None, None, Tile(base, n))
            for n in range(LOOP0 + LOOPS, NT + 3):
                step(Tile(0, n + 1) if n + 1 < NT else None, None, None, Tile(0, n - 3))
            for p in range(2):
                sp.wait_ge(st_out[p], 16 * NT // 2)

        N_CTX = 16 * (4 + BT)

        @block.gpsimd
        def _(pool):
            count = [0]

            def newton(w, h, y, t):
                yield lambda: nc.gpsimd.tensor_scalar(y.bitcast(I32), w.bitcast(I32), -0.5, RSQRT0, ALU.mult, ALU.add)
                for _ in range(3):
                    yield lambda: nc.gpsimd.tensor_scalar(t, y, y, h, ALU.mult, ALU.mult)
                    yield lambda: nc.gpsimd.tensor_scalar(y, t, 1.5, y, ALU.add, ALU.mult)

            def newton_wide(w, y, h, t):
                yield lambda: nc.gpsimd.tensor_scalar(h, w, -0.5, None, ALU.mult)
                yield lambda: nc.gpsimd.tensor_scalar(y.bitcast(I32), w.bitcast(I32), -0.5, RSQRT0, ALU.mult, ALU.add)
                for _ in range(3):
                    yield lambda: nc.gpsimd.tensor_tensor(t, y, y, ALU.mult)
                    yield lambda: nc.gpsimd.tensor_tensor(t, t, h, ALU.mult)
                    yield lambda: nc.gpsimd.tensor_scalar(t, t, 1.5, None, ALU.add)
                    yield lambda: nc.gpsimd.tensor_tensor(y, y, t, ALU.mult)

            def chained(ops, done):
                ops = list(ops)
                for k, op in enumerate(ops):
                    ins = op()
                    if k + 1 < len(ops):
                        ins.then_inc(s["chain_g"], 1)
                        count[0] += 1
                        pool.wait_ge(s["chain_g"], count[0])
                    else:
                        ins.then_inc(s[done], 1)

            nc.gpsimd.memset(wk_pad[:, :, :], 0.0).then_inc(s["wk_zero"], 1)
            pool.wait_ge(s["wk_zero"], 1)
            nc.gpsimd.memset(qk2[64:65, :, :, :], 1.0).then_inc(s["ones_set"], 1)
            nc.gpsimd.memset(zT2[64:65, :], 1.0).then_inc(s["ones_set"], 1)
            pool.wait_ge(s["ones_set"], 2)
            pool.wait_ge(s["bnx_done"], 1)
            var_all = mean_x[:, :, 1]
            chained([
                lambda: nc.gpsimd.tensor_scalar(var_x[:, 0, :], var_all, EPS, None, ALU.add),
                lambda: nc.gpsimd.tensor_scalar(var_x[:, 1, :], var_all, 1.0 + EPS, EPS * EPS, ALU.mult, ALU.add),
            ] + list(newton_wide(var_x[:, :, :].rearrange("p a b -> p (a b)"), rs_x[:, :, :].rearrange("p a b -> p (a b)"), nw_h[:, :], nw_t[:, :])), "rsx_done")
            pool.wait_ge(s["cent_ss"], 1)
            chained(newton_wide(cent_s[:, :], cent_r[:, :], nw_h[0:NE, 0:1], nw_t[0:NE, 0:1]), "cent_rs")
            pool.wait_ge(s["tm_ready"], 1)

            def chain(ops, done, name, tile):
                ops = list(ops)
                links = len(ops) - 1
                for k, op in enumerate(ops):
                    ins = op()
                    if k < links:
                        ins.then_inc(chains[name], 1)
                        wait_apart(pool, chains[name], tile.count(links, k + 1), passed_g)
                    else:
                        ins.then_inc(s[done], 1)

            def norm(k, tile):
                wait_apart(pool, s[f"st{k}_v"], tile.count(1, 1), passed_g)
                w, h, y, t = (var_in[k][:, i:i + 1] for i in range(4))
                v = mv[k][:, 1:2]
                chain([lambda: nc.gpsimd.tensor_scalar(h, v, EPS, -0.5, ALU.add, ALU.mult),
                       lambda: nc.gpsimd.tensor_scalar(w, v, EPS, None, ALU.add),
                       *newton(w, h, rstd[k][:, 0:1], t)], f"rs{k}_g", f"g{k}", tile)

            def length(tile):
                w, h, y, t = (var_in[3][:, i:i + 1] for i in range(4))
                v = mv[3][:, 1:2]
                wait_apart(pool, s["rs3_g"], tile.count(1, 1), passed_g)
                chain([lambda: nc.gpsimd.tensor_scalar(h, v, -0.5, None, ALU.mult),
                       *newton(v, h, y, t),
                       lambda: nc.gpsimd.tensor_scalar(t, rstd[3][:, 0:1], w, y, ALU.mult, ALU.mult),
                       lambda: nc.gpsimd.tensor_scalar(inorm[:, :], t, float(D) ** -0.5, 1e12, ALU.mult, ALU.min)], "inorm_g", "len", tile)

            def step(a, b, c, dd):
                def weights(t, q):
                    wait_apart(pool, chains["tm"], t.count(1, 1), passed_g)
                    wait_apart(pool, s["rsum_v"], t.count(2, q + 1), passed_g)
                    wait_apart(pool, s["am_mm"], t.count(1, 0), passed_g)
                    for k in (2 * q, 2 * q + 1):
                        nc.gpsimd.tensor_scalar(wsel[:, k, :], sel[:, :], rsum_row[:, k:k + 1], tm_tile[:, k:k + 1], ALU.mult, ALU.mult).then_inc(s["wsel_g"], 1)
                if b:
                    weights(b, 1)
                if a:
                    wait_apart(pool, s["wsel_g"], a.count(4, 0), passed_g)
                    nc.gpsimd.tensor_copy(tm_tile[:, :], text_m[:, bass.ds(a.n * BT, BT)]).then_inc(chains["tm"], 1)
                if c:
                    wait_apart(pool, s["x1_v"], c.count(1, 0), passed_g)
                    nc.gpsimd.tensor_tensor(xb_c[:, :], x_all[:, c.n, :], bout[:, :], ALU.add).then_inc(s["xb_g"], 1)
                    norm(1, c)
                    norm(2, c)
                if b:
                    norm(0, b)
                    nc.gpsimd.tensor_tensor(xt_b[:, :], xt[:, :], b2[:, :], ALU.add).then_inc(s["xtb_g"], 1)
                if c:
                    norm(3, c)
                    length(c)
                if a:
                    weights(a, 0)

            step(*tiles(0, 0))
            pool.wait_ge(s["kf_sb"], 1)
            pool.wait_ge(s["ld_w"], LD_W)
            run(ET.Pool, step)

        @block.scalar
        def _(act):
            A = nc.scalar.activation

            def copy(dst, src, done):
                A(dst, src, ACT.Copy).then_inc(s[done], 1)

            def gelus(dst, half, bank, bias, mm, done, tile):
                wait(act, s[mm], tile.count(1, 1))
                for k in range(4 * half, 4 * half + 4):
                    ins = A(dst[:, k, :], bank[:, 128 * (k % 4):128 * (k % 4) + 128], ACT.Gelu, bias=bias[:, k:k + 1])
                ins.then_inc(s[done], 1)

            def step(a, b, c, dd):
                one = lambda t: t.count(1, 1)

                def exps(q):
                    for k in range(2):
                        wait(act, s["mr1_v"], a.count(4, 2 * q + k + 1))
                        A(expo[:, 2 * q + k, :], S[k][:, 0:G], ACT.Exp, bias=nmax[:, 2 * q + k:2 * q + k + 1], scale=SCALE).then_inc(s["exp_a"], 1)
                if a:
                    wait(act, s["xT_mm"], one(a))
                    copy(xT[:, :], PA[:, 0:D], "xT_a")
                    wait(act, s["qT_mm"], one(a))
                    copy(qT[:, :], PA[:, D:D + 128], "qT_a")
                if dd:
                    wait(act, s["xT3_mm"], one(dd))
                    copy(xT3[:, :], D0[:, 0:D], "xT3_a")
                if a:
                    wait(act, s["qk_mm"], one(a))
                    A(qk1[:, :, :, :].rearrange("p b h t -> p h b t"), S[0][:, :].rearrange("p (h b t) -> p h b t", h=H, b=BT), ACT.Copy)
                    A(qk2[0:64, :, :, :].rearrange("p b h t -> p h b t"), S[1][0:64, :].rearrange("p (h b t) -> p h b t", h=H, b=BT), ACT.Copy).then_inc(s["qk_a"], 1)
                if dd:
                    wait(act, s["lg_mm"], one(dd))
                    copy(dots[:, :], D0[:, D:D + 2 * NE], "dots_a")
                if b:
                    wait(act, s["am_mm"], one(b))
                    copy(am[:, :], PA[:, 0:G], "am_a")
                    wait(act, s["amT_mm"], one(b))
                    copy(amT[:, :, :].rearrange("p a b -> p (a b)"), PA[:, 0:256], "amT_a")
                if dd:
                    wait(act, s["nbest_v"], one(dd))
                    A(e_d[:, :], logit[:, :], ACT.Exp, bias=nbest[:, :]).then_inc(s["ed_a"], 1)
                if b:
                    wait(act, s["zT_mm"], one(b))
                    A(zT1[:, :], PA[:, 256:384], ACT.Copy)
                    A(zT2[0:64, :], PA[0:64, 384:512], ACT.Copy).then_inc(s["zT_a"], 1)
                if a:
                    exps(0)
                if dd:
                    wait(act, s["gT_mm"], one(dd))
                    copy(gateT[:, :], PA[0:NE, 0:128], "gT_a")
                    gelus(act2, 0, D1, e_b1, "e1a_mm", "g2a_a", dd)
                if c:
                    wait(act, s["xT2_mm"], one(c))
                    copy(xT2[:, :], C0[:, 0:D], "xT2_a")
                if a:
                    exps(1)
                if c:
                    wait(act, s["v_mm"], one(c))
                    A(xmT[:, :], C0[:, D:2 * D], ACT.Copy)
                    copy(v_c[:, :], C0[:, 0:D], "v_a")
                if b:
                    wait(act, s["inv_mm"], one(b))
                    copy(yb[:, :], B0[:, D:2 * D], "y_a")
                if c:
                    wait(act, s["nmaxc_v"], one(c))
                    A(p_c[:, :], C0[:, D:D + T], ACT.Exp, bias=nmax_c[:, :], accum_out=sum_c[:, :]).then_inc(s["pc_a"], 1)
                if dd:
                    gelus(act2, 1, D0, e_b1, "e1b_mm", "g2b_a", dd)
                if c:
                    wait(act, s["r_mm"], one(c))
                    A(r_c[:, :, :, :].rearrange("p j b t -> p b j t"), C0[:, D:2 * D].rearrange("p (b j t) -> p b j t", b=BT, j=2), ACT.Copy).then_inc(s["r_a"], 1)
                if b:
                    wait(act, s["hT_mm"], one(b))
                    copy(hT[:, :], B0[:, 0:D], "hT_a")
                    gelus(act1, 0, B1, b1, "w1a_mm", "ga_a", b)
                    gelus(act1, 1, B0, b1, "w1b_mm", "gb_a", b)

            act.wait_ge(s["ld_s4"], LD_S4)
            A(logdt[:, :], logdt[:, :], ACT.Exp).then_inc(s["setup_dt"], 1)
            act.wait_ge(s["setup_ang"], 1)
            for j, power in enumerate(WEXP):
                A(ang[:, j, :], s4a[:, 1, :], ACT.Copy, scale=float(power)).then_inc(s["setup_mul"], 1)
            act.wait_ge(s["setup_mul"], NPOW)
            A(ang[:, NPOW:NPOW + NP, :], ang[:, 0:NP, :], ACT.Identity, scale=1 / TWO_PI, bias=phase[:, 0:1])
            A(ang[:, NPOW + NP:2 * NPOW, :], ang[:, NP:NPOW, :], ACT.Identity, scale=1 / TWO_PI, bias=phase[:, 1:2]).then_inc(s["setup_turn"], 1)
            for j, power in enumerate(WEXP):
                ins = A(expw[:, j, :], s4a[:, 0, :], ACT.Exp, scale=float(power))
            ins.then_inc(s["setup_exp"], 1)
            step(*tiles(0, 0))
            act.wait_ge(s["setup_red"], 1)
            A(ang[:, 0:NP, :], ang[:, 0:NP, :], ACT.Sin, bias=phase[:, 2:3])
            A(ang[:, NP:NPOW, :], ang[:, NP:NPOW, :], ACT.Sin, bias=phase[:, 3:4]).then_inc(s["setup_sin"], 1)
            act.wait_ge(s["kt_mm"], 1)
            copy(kern_t[:, :], D1[0:T, 0:D], "kt_sb")
            act.wait_ge(s["kf_mm"], 1)
            for k in range(2):
                A(kern_f[:, k, :], D1[:, k * D:(k + 1) * D], ACT.Copy)
            copy(kern_f[:, 2, :], D0[:, 0:D], "kf_sb")
            run(ET.Activation, step)

        @block.vector
        def _(dve):
            V = nc.vector
            n_chain = [0]

            def link(ins):
                ins.then_inc(s["chain_v"], 1)
                n_chain[0] += 1
                dve.wait_ge(s["chain_v"], n_chain[0])

            dve.wait_ge(s["ldx"], 64)
            for t in range(NT):
                V.bn_stats(bn_x[:, t % 2, :], x_all[:, t, :]).then_inc(s["bn_v"], 1)
                dve.wait_ge(s["bn_v"], t + 1)
                ins = V.bn_aggr(mean_x[:, t, :], bn_x[:, t % 2, :])
            ins.then_inc(s["bnx_done"], 1)
            dve.wait_ge(s["ld_cent"], LD_CENT)
            link(V.tensor_copy(valid, vm8[:, :]))
            V.tensor_scalar(vm[:, :], valid, MASKED, -MASKED, ALU.mult, ALU.add)
            link(V.reduce_max(anyv[:, 0:1], valid, AXX))
            link(V.reciprocal(anyv[:, 1:2], anyv[:, 0:1]))
            V.tensor_tensor(anyv[:, 2:3], anyv[:, 0:1], anyv[:, 1:2], ALU.mult).then_inc(s["setup_v"], 1)
            link(V.tensor_tensor(cent2[:, :], cent[:, :], cent[:, :], ALU.mult))
            V.reduce_sum(cent_s[:, :], cent2[:, :], AXX).then_inc(s["cent_ss"], 1)
            dve.wait_ge(s["setup_dt"], 1)
            V.tensor_tensor(s4a[:, 0, :], logdt[:, :], s4[:, 0, :], ALU.mult)
            V.tensor_tensor(s4a[:, 1, :], logdt[:, :], s4[:, 1, :], ALU.mult).then_inc(s["setup_ang"], 1)
            dve.wait_ge(s["ld_any"], 16)
            link(V.tensor_copy(text_m[:, :], tm8[:, :]))
            V.scalar_tensor_tensor(text_m[:, :], text_m[:, :], 1.0 / H, anyb[:, :], ALU.mult, ALU.mult).then_inc(s["tm_ready"], 1)
            dve.wait_ge(s["rsx_done"], 1)

            def setup_late():
                dve.wait_ge(s["setup_turn"], 1)
                turn = ang[:, NPOW:2 * NPOW, :]
                link(V.tensor_scalar(turn, turn, MAGIC, -MAGIC, ALU.add, ALU.add))
                link(V.scalar_tensor_tensor(ang[:, 0:NPOW, :], turn, -PI_HI, ang[:, 0:NPOW, :], ALU.mult, ALU.add))
                link(V.scalar_tensor_tensor(ang[:, 0:NPOW, :], turn, -PI_LO, ang[:, 0:NPOW, :], ALU.mult, ALU.add))
                V.tensor_scalar(ang[:, 0:NP, :], ang[:, 0:NP, :], phase[:, 5:6], phase[:, 6:7], ALU.min, ALU.max)
                V.tensor_scalar(ang[:, NP:NPOW, :], ang[:, NP:NPOW, :], phase[:, 7:8], phase[:, 8:9], ALU.min, ALU.max).then_inc(s["setup_red"], 1)
                dve.wait_ge(s["ld_film"], LD_FILM)
                dve.wait_ge(s["film_mm"], 1)
                for rows, f_in, f_out, dst in ((slice(0, 128), B0, B1, film1), (slice(0, 64), D0, D1, film2)):
                    V.scalar_tensor_tensor(dst[rows, 0:D], f_in[rows, 0:D], mgate[rows, :], gin[rows, :], ALU.mult, ALU.mult)
                    link(V.scalar_tensor_tensor(film_t[rows, :], f_in[rows, 0:D], mgate[rows, :], bin_[rows, :], ALU.mult, ALU.mult))
                    V.scalar_tensor_tensor(dst[rows, D:2 * D], f_in[rows, D:2 * D], mgate[rows, :], film_t[rows, :], ALU.mult, ALU.add)
                    link(V.tensor_scalar(dst[rows, 2 * D:4 * D], f_out[rows, :], mgate[rows, :], None, ALU.mult))
                r = slice(64, 65)
                link(V.tensor_scalar(brow2[r, 0:D], brow[r, 0:D], mgate[r, :], 1.0, ALU.mult, ALU.add))
                V.tensor_tensor(film2[r, 0:D], brow2[r, 0:D], gin[r, :], ALU.mult)
                link(V.tensor_tensor(brow2[r, D:2 * D], brow2[r, 0:D], bin_[r, :], ALU.mult))
                V.scalar_tensor_tensor(film2[r, D:2 * D], brow[r, D:2 * D], mgate[r, :], brow2[r, D:2 * D], ALU.mult, ALU.add)
                V.tensor_scalar(film2[r, 2 * D:3 * D], brow[r, 2 * D:3 * D], mgate[r, :], 1.0, ALU.mult, ALU.add)
                V.tensor_scalar(film2[r, 3 * D:4 * D], brow[r, 3 * D:4 * D], mgate[r, :], None, ALU.mult).then_inc(s["film_sb"], 1)
                dve.wait_ge(s["setup_exp"], 1)
                dve.wait_ge(s["setup_sin"], 1)
                link(V.tensor_tensor(expw[:, :, :], expw[:, :, :], ang[:, 0:NPOW, :], ALU.mult))
                lo, hi = slice(0, NS), slice(NS, 2 * NS)
                wr, wi = s4c[:, 0, :], s4c[:, 1, :]
                V.tensor_scalar(s4c[lo, 0, :], expw[lo, 1, :], -1.0, None, ALU.add)
                V.tensor_scalar(s4c[hi, 0, :], expw[hi, NPOW - 1, :], -1.0, None, ALU.add)
                V.tensor_copy(s4c[lo, 1, :], expw[lo, NPOW - 1, :])
                link(V.tensor_copy(s4c[hi, 1, :], expw[hi, 1, :]))
                are, aim, cre, cim = (s4[:, k, :] for k in range(4))
                t0, t1, t2, t3, t4, t5 = (s4c[:, k, :] for k in range(2, 8))
                tt = lambda o, a, b, op: V.tensor_tensor(o, a, b, op)
                tt(t0, cre, wr, ALU.mult)
                tt(t1, cim, wi, ALU.mult)
                tt(t2, cre, wi, ALU.mult)
                tt(t3, cim, wr, ALU.mult)
                tt(t4, are, are, ALU.mult)
                link(tt(t5, aim, aim, ALU.mult))
                tt(t0, t0, t1, ALU.subtract)
                tt(t2, t2, t3, ALU.add)
                link(tt(t4, t4, t5, ALU.add))
                V.reciprocal(t5, t4)
                tt(t1, t0, are, ALU.mult)
                tt(t3, t2, aim, ALU.mult)
                tt(wr, t2, are, ALU.mult)
                link(tt(wi, t0, aim, ALU.mult))
                tt(t1, t1, t3, ALU.add)
                link(tt(wr, wi, wr, ALU.subtract))
                tt(t1, t1, t5, ALU.mult)
                link(tt(t3, wr, t5, ALU.mult))
                link(V.tensor_scalar(t1, t1, phase[:, 4:5], None, ALU.mult))
                wide = lambda v, n: v.rearrange("p (o b) -> p o b", o=1).broadcast_to([128, n, D])
                tt(uu[:, 0, :], expw[:, 0, :], t1, ALU.mult)
                tt(uu[:, 1:4, :], expw[:, 8:11, :], wide(t1, 3), ALU.mult)
                link(tt(expw[:, 11:15, :], expw[:, 11:15, :], wide(t3, 4), ALU.mult))
                link(tt(uu[:, :, :], uu[:, :, :], expw[:, 11:15, :], ALU.add))
                for k in range(4):
                    ins = tt(ang[:, 8 * k:8 * k + 8, :], expw[:, 0:8, :], uu[:, k, :].rearrange("p (o b) -> p o b", o=1).broadcast_to([128, 8, D]), ALU.mult)
                ins.then_inc(s["setup_prod"], 1)
                dve.wait_ge(s["b1_mm"], 1)
                V.tensor_tensor(b1[:, :], S[0][:, 0:HID // 128], b1raw[:, :], ALU.add)
                for k in range(2):
                    V.tensor_scalar(w1[:, k, :], w1[:, k, :], gffn[:, k:k + 1], None, ALU.mult)
                dve.wait_ge(s["qkw_mm"], 1)
                V.tensor_scalar(qk_w[:, :, :].rearrange("p a b -> p (a b)"), C0[:, :], 0.25, None, ALU.mult).then_inc(s["b1_sb"], 1)
                dve.wait_ge(s["cent_rs"], 1)
                link(V.tensor_scalar(cent_r[:, :], cent_r[:, :], 1e12, None, ALU.min))
                V.tensor_scalar(cent[:, :], cent[:, :], cent_r[:, :], None, ALU.mult).then_inc(s["cent_n"], 1)
                dve.wait_ge(s["cent_t"], 1)
                V.tensor_copy(route[:, :, NE:2 * NE], S[1][:, 0:2 * NE].rearrange("p (a b) -> p a b", a=2)).then_inc(s["qkw_sb"], 1)
                dve.wait_ge(s["kf_sb"], 1)

            def stats(k, src, tile, done):
                V.bn_stats(bn[k][:, :], src).then_inc(chains[f"bn{k}"], 1)
                wait_apart(dve, chains[f"bn{k}"], tile.count(1, 1), passed_v)
                V.bn_aggr(mv[k][:, :], bn[k][:, :]).then_inc(s[done], 1)

            def norm_input(t):
                V.tensor_scalar(xln[t.p][:, :], x_all[:, t.n, :], mean_x[:, t.n, 0:1], rs_x[:, 0, bass.ds(t.n, 1)], ALU.subtract, ALU.mult).then_inc(s["xln_v"], 1)
                V.tensor_scalar(xhat[t.p][:, :], x_all[:, t.n, :], mean_x[:, t.n, 0:1], rs_x[:, 1, bass.ds(t.n, 1)], ALU.subtract, ALU.mult).then_inc(chains["xhat"], 1)

            TOP_AT = ((0, 2, 6, 8), (4, 10, 12, 14))

            def step(a, b, c, dd, following):
                one = lambda t: t.count(1, 1)

                def maxima(a, q):
                    for k in range(2):
                        wait_apart(dve, s["sc_mm"], a.count(4, 2 * q + k + 1), passed_v)
                        V.max(top[:, 2 * q + k, 0:8], S[k][:, 0:G]).then_inc(chains["top"], 1)
                    wait(dve, chains["top"], a.count(16, TOP_AT[q][0] + 2))
                    V.tensor_scalar(nmax[:, 2 * q:2 * q + 2], top[:, 2 * q:2 * q + 2, 0], -SCALE, None, ALU.mult).then_inc(s["nmax_v"], 1)

                def take(a, q):
                    for k in range(2):
                        V.match_replace(work[:, 2 * q + k, :], top[:, 2 * q + k, 0:8], S[k][:, 0:G], TAKEN).then_inc(s["mr1_v"], 1)

                def top8(a, q, r8):
                    for k in range(2):
                        if r8 == 1:
                            wait_apart(dve, s["mr1_v"], a.count(4, 2 * q + k + 1), passed_v)
                        else:
                            wait_apart(dve, chains["taken"], a.count(12, 6 * q + 2 * (r8 - 2) + k + 1), passed_v)
                        V.max(top[:, 2 * q + k, 8 * r8:8 * r8 + 8], work[:, 2 * q + k, :]).then_inc(chains["top"], 1)
                    for k in range(2):
                        wait_apart(dve, chains["top"], a.count(16, TOP_AT[q][r8] + k + 1), passed_v)
                        V.match_replace(work[:, 2 * q + k, :], top[:, 2 * q + k, 8 * r8:8 * r8 + 8], work[:, 2 * q + k, :], TAKEN).then_inc(chains["taken"], 1)

                def probs(a, q):
                    wait(dve, s["am_mm"], a.count(1, 0))
                    for k in range(2):
                        wait(dve, chains["taken"], a.count(12, 6 * q + 4 + k + 1))
                        wait(dve, s["exp_a"], a.count(4, 2 * q + k + 1))
                        V.scalar_tensor_tensor(prob[:, 2 * q + k, :], work[:, 2 * q + k, :], TAKEN, expo[:, 2 * q + k, :], ALU.is_equal, ALU.mult,
                                               accum_out=psum_row[:, 2 * q + k:2 * q + k + 1]).then_inc(s["prob_v"], 1)
                    wait(dve, s["prob_v"], a.count(4, 2 * q + 2))
                    wait(dve, s["wsel_g"], a.count(4, 2 * q - 2))
                    V.reciprocal(rsum_row[:, 2 * q:2 * q + 2], psum_row[:, 2 * q:2 * q + 2]).then_inc(s["rsum_v"], 1)

                def gated(ks):
                    for k in ks:
                        bank = (D1, D0)[k // 2 % 2][:, k % 2 * D:k % 2 * D + D]
                        wait(dve, s["eo_mm"], dd.count(NE + 1, min(k // 2 * 2 + 2, NE + 1)))
                        if k == 0:
                            wait(dve, s["gate_v"], one(dd))
                            V.scalar_tensor_tensor(acc[0][:, :], bank, gate[:, 0:1], x2[dd.p][:, :], ALU.mult, ALU.add).then_inc(s["acc_v"], 1)
                        elif k == 1:
                            V.tensor_scalar(acc[1][:, :], bank, gate[:, 1:2], None, ALU.mult).then_inc(s["acc_v"], 1)
                        else:
                            wait(dve, s["acc_v"], dd.count(NE + 1, k - 1))
                            if k < NE:
                                V.scalar_tensor_tensor(acc[k % 2][:, :], bank, gate[:, k:k + 1], acc[k % 2][:, :], ALU.mult, ALU.add).then_inc(s["acc_v"], 1)
                            else:
                                V.tensor_tensor(acc[0][:, :], bank, acc[0][:, :], ALU.add).then_inc(s["acc_v"], 1)

                if dd:
                    wait(dve, s["rs3_g"], one(dd))
                    V.tensor_scalar(xl3[:, :], x2[dd.p][:, :], mv[3][:, 0:1], rstd[3][:, 0:1], ALU.subtract, ALU.mult).then_inc(s["xl3_v"], 1)
                if b:
                    top8(b, 1, 3)
                if b:
                    probs(b, 1)
                if c:
                    wait(dve, s["h2_mm"], one(c))
                    wait(dve, s["xtb_g"], one(c))
                    V.tensor_tensor(xt2[:, :], xt_b[:, :], B1[:, 0:D], ALU.add).then_inc(s["xt2_v"], 1)
                    wait_apart(dve, s["xt2_v"], one(c), passed_v)
                    stats(1, xt2[:, :], c, "st1_v")
                if dd:
                    wait(dve, s["dots_a"], one(dd))
                    wait(dve, s["inorm_g"], one(dd))
                    V.scalar_tensor_tensor(logit[:, :], dots[:, NE:2 * NE], inorm[:, :], dots[:, 0:NE], ALU.mult, ALU.add).then_inc(chains["logit"], 1)
                    wait_apart(dve, chains["logit"], one(dd), passed_v)
                    V.max(best[:, :], logit[:, :]).then_inc(chains["best"], 1)
                if c:
                    wait(dve, s["rs1_g"], one(c))
                    V.tensor_scalar(u_c[:, :], xt2[:, :], mv[1][:, 0:1], rstd[1][:, 0:1], ALU.subtract, ALU.mult).then_inc(chains["u"], 1)
                if dd:
                    wait(dve, chains["best"], one(dd))
                    V.tensor_scalar(nbest[:, :], best[:, 0:1], -1.0, None, ALU.mult).then_inc(s["nbest_v"], 1)
                if c:
                    wait(dve, chains["u"], c.count(2, 1))
                    V.tensor_tensor(u_c[:, :], u_c[:, :], gout[:, :], ALU.mult).then_inc(chains["u"], 1)
                    wait(dve, chains["u"], c.count(2, 2))
                    wait(dve, s["xb_g"], one(c))
                    V.tensor_tensor(x1[:, :], u_c[:, :], xb_c[:, :], ALU.add).then_inc(s["x1_v"], 1)
                if b:
                    wait(dve, s["z_mm"], one(b))
                    V.scalar_tensor_tensor(z[:, :], ctx_l[b.p][:, :], am[:, G - 1:G], PA[:, 0:DV], ALU.mult, ALU.add).then_inc(s["z_v"], 1)
                if c:
                    wait_apart(dve, s["x1_v"], one(c), passed_v)
                    stats(2, x1[:, :], c, "st2_v")
                if a:
                    maxima(a, 0)
                    take(a, 0)
                if dd:
                    wait(dve, s["ed_a"], one(dd))
                    V.scalar_tensor_tensor(pg[:, :], logit[:, :], best[:, 1:2], e_d[:, :], ALU.is_ge, ALU.mult, accum_out=sum_d[:, :]).then_inc(chains["pg"], 1)
                if dd:
                    wait(dve, chains["pg"], one(dd))
                    V.reciprocal(rsum_d[:, :], sum_d[:, :]).then_inc(chains["rsd"], 1)
                if dd:
                    wait(dve, chains["rsd"], one(dd))
                    V.tensor_scalar(gate[:, :], pg[:, :], rsum_d[:, :], None, ALU.mult).then_inc(s["gate_v"], 1)
                if b:
                    wait(dve, s["fin_mm"], one(b))
                    wait(dve, chains["xhat"], one(b))
                    V.tensor_tensor(xf[:, :], xhat[b.p][:, :], B0[:, 0:D], ALU.mult).then_inc(chains["xf"], 1)
                    wait(dve, chains["xf"], one(b))
                    V.tensor_tensor(xf[:, :], xf[:, :], B0[:, D:2 * D], ALU.add).then_inc(s["xf_v"], 1)
                if c:
                    wait(dve, s["rs2_g"], one(c))
                    V.tensor_scalar(xl2[:, :], x1[:, :], mv[2][:, 0:1], rstd[2][:, 0:1], ALU.subtract, ALU.mult).then_inc(s["xl2_v"], 1)
                if a:
                    top8(a, 0, 1)
                if b:
                    wait(dve, s["fwd_mm"], one(b))
                    V.tensor_tensor(had[:, 0:2, :].rearrange("p a b -> p (a b)"), B1[:, :], kern_f[:, 0:2, :].rearrange("p a b -> p (a b)"), ALU.mult)
                    V.tensor_tensor(had[:, 2, :], B0[:, 0:D], kern_f[:, 2, :], ALU.mult).then_inc(s["had_v"], 1)
                if a:
                    maxima(a, 1)
                    take(a, 1)
                    top8(a, 0, 2)
                    top8(a, 0, 3)
                if c:
                    wait(dve, s["s_mm"], one(c))
                    V.reduce_max(nmax_c[:, :], C0[:, D:D + T], AXX, negate=True).then_inc(s["nmaxc_v"], 1)
                if c:
                    wait(dve, s["pc_a"], one(c))
                    V.reciprocal(rsum_c[:, :], sum_c[:, :]).then_inc(chains["rsc"], 1)
                    wait(dve, chains["rsc"], one(c))
                    V.tensor_scalar(pn_c[:, :], p_c[:, :], rsum_c[:, :], None, ALU.mult).then_inc(chains["pn"], 1)
                    wait_apart(dve, chains["pn"], one(c), passed_v)
                    V.transpose(pT_c[:, :], pn_c[:, :]).then_inc(chains["pT"], 1)
                    wait(dve, chains["pT"], one(c))
                    V.tensor_tensor(pT_blk[:, :, :], pT_c[:, :].rearrange("p (o t) -> p o t", o=1).broadcast_to([128, BT, T]), block_mask[:, :, :], ALU.mult).then_inc(s["pt_v"], 1)
                if b:
                    wait(dve, s["y_a"], one(b))
                    wait(dve, s["y_mm"], one(b))
                    V.tensor_tensor(yb[:, :], yb[:, :], B1[:, 0:D], ALU.mult).then_inc(chains["yb"], 1)
                    wait(dve, chains["yb"], b.count(2, 1))
                    V.tensor_tensor(yb[:, :], yb[:, :], B1[:, D:2 * D], ALU.add).then_inc(chains["yb"], 1)
                if b:
                    wait(dve, chains["yb"], b.count(2, 2))
                    V.tensor_tensor(xt[:, :], yb[:, :], xln[b.p][:, :], ALU.add).then_inc(s["xt_v"], 1)
                    wait_apart(dve, s["xt_v"], one(b), passed_v)
                    stats(0, xt[:, :], b, "st0_v")
                if dd:
                    gated(range(0, 4))
                if c:
                    wait(dve, s["o2_mm"], one(c))
                    V.tensor_tensor(x2[c.p][:, :], x1[:, :], C0[:, 0:D], ALU.add).then_inc(s["x2_v"], 1)
                if dd:
                    gated(range(4, 6))
                if b:
                    wait(dve, s["rs0_g"], one(b))
                    V.tensor_scalar(hn[:, :], xt[:, :], mv[0][:, 0:1], rstd[0][:, 0:1], ALU.subtract, ALU.mult).then_inc(s["hn_v"], 1)
                if c:
                    wait_apart(dve, s["x2_v"], one(c), passed_v)
                    stats(3, x2[c.p][:, :], c, "st3_v")
                if a:
                    probs(a, 0)
                if following:
                    norm_input(following)
                if a:
                    top8(a, 1, 1)
                if dd:
                    gated(range(6, 8))
                if a:
                    top8(a, 1, 2)
                if dd:
                    gated(range(8, NE + 1))
                if dd:
                    wait(dve, s["acc_v"], dd.count(NE + 1, NE + 1))
                    wait(dve, st_out[dd.p], dd.half(16, 0))
                    V.tensor_tensor(out_sb[dd.p][:, :], acc[0][:, :], acc[1][:, :], ALU.add).then_inc(s["fin_v"], 1)

            def step_on(a, b, c, dd):
                following = None
                if a and not (a.static and a.n == NT - 1):
                    following = Tile(a.base, a.c + 1)
                step(a, b, c, dd, following)

            norm_input(Tile(0, 0))
            step_on(*tiles(0, 0))
            setup_late()
            run(ET.DVE, step_on)

        @block.tensor
        def _(pe):
            MM, TR = nc.tensor.matmul, nc.tensor.transpose
            def transposes(dst, src, done):
                for k in range(2):
                    ins = TR(dst[:, 128 * k:128 * k + 128], src[:, 128 * k:128 * k + 128], ident[:, :])
                ins.then_inc(s[done], 1)

            def step(a, b, c, dd):
                one = lambda t: t.count(1, 1)

                def scores(k):
                    wait(pe, s["qk_a"], one(a))
                    if k == 0:
                        pe_ctx = a.half(N_CTX, N_CTX)
                        wait(pe, ld_ctx[a.p], pe_ctx)
                    if k >= 2:
                        wait(pe, s["mr1_v"], a.count(4, k - 1))
                        wait(pe, s["exp_a"], a.count(4, k - 1))
                    bank = S[k % 2]
                    MM(bank[:, 0:G], qk1[:, k, :, :].rearrange("p h t -> p (h t)"), ctx_t1[a.p][:, k, :], start=True, stop=False)
                    MM(bank[:, 0:G], qk2[:, k, :, :].rearrange("p h t -> p (h t)"), ctx_t2[a.p][:, k, :], start=False, stop=True).then_inc(s["sc_mm"], 1)

                def wide(half, bank, w, xs, done, ms=range(4)):
                    for m in ms:
                        at = 128 * (4 * half + m)
                        for k in range(2):
                            ins = MM(bank[:, 128 * m:128 * m + 128], w[:, k, at:at + 128], xs[:, 128 * k:128 * k + 128], start=k == 0, stop=k == 1)
                    if done:
                        ins.then_inc(s[done], 1)

                def experts(ks):
                    for k in ks:
                        bank = (D1, D0)[k // 2 % 2][:, k % 2 * D:k % 2 * D + D]
                        if k == 0:
                            wait(pe, s["g2a_a"], one(dd))
                        elif k == 2:
                            wait(pe, s["g2b_a"], one(dd))
                        elif k >= 4 and k % 2 == 0:
                            wait(pe, s["acc_v"], dd.count(NE + 1, k - 2))
                        if k == NE:
                            wait(pe, s["gT_a"], one(dd))
                            MM(bank, gateT[:, :], e_b2[:, :], start=True, stop=True).then_inc(s["eo_mm"], 1)
                        else:
                            MM(bank, act2[:, k, :], e_w2[:, k, :], start=True, stop=True).then_inc(s["eo_mm"], 1)

                def down(half):
                    wait(pe, s[("ga_a", "gb_a")[half]], one(c))
                    for k in range(4 * half, 4 * half + 4):
                        ins = MM(B1[:, 0:D], act1[:, k, :], w2[:, k, :], start=k == 0, stop=k == HID // 128 - 1)
                    if half == 1:
                        ins.then_inc(s["h2_mm"], 1)

                if a:
                    wait(pe, s["xln_v"], one(a))
                    if dd:
                        wait(pe, s["gT_a"], dd.count(1, 0))
                    transposes(PA, xln[a.p], "xT_mm")
                if c:
                    down(0)
                if a:
                    wait(pe, s["xT_a"], one(a))
                    for k in range(2):
                        ins = MM(PA[:, D:D + 128], wq[:, k, :], xT[:, 128 * k:128 * k + 128], start=k == 0, stop=k == 1)
                    ins.then_inc(s["qT_mm"], 1)
                if c:
                    down(1)
                if dd:
                    wait(pe, s["xl3_v"], one(dd))
                    wait(pe, s["acc_v"], dd.count(NE + 1, 0))
                    transposes(D0, xl3, "xT3_mm")
                if a:
                    wait(pe, s["qT_a"], one(a))
                    wait(pe, s["mr1_v"], a.count(4, 0))
                    wait(pe, s["exp_a"], a.count(4, 0))
                    for h in range(H):
                        MM(S[0][:, 128 * h:128 * h + 128], wk_pad[:, h, 0:128], qT[:, :], start=True, stop=True)
                        ins = MM(S[1][0:64, 128 * h:128 * h + 128], wk_pad[:, h, 128:DV], qT[:, :], start=True, stop=True)
                    ins.then_inc(s["qk_mm"], 1)
                if dd:
                    wait(pe, s["xT3_a"], one(dd))
                    for k in range(2):
                        ins = MM(D0[:, D:D + 2 * NE], xT3[:, 128 * k:128 * k + 128], route[:, k, :], start=k == 0, stop=k == 1)
                    ins.then_inc(s["lg_mm"], 1)
                    wide(0, D1, e_w1, xT3, "e1a_mm")
                if b:
                    wait(pe, s["prob_v"], b.count(4, 4))
                    wait(pe, s["wsel_g"], b.count(4, 4))
                    for k in range(BT):
                        ins = MM(PA[T * k:T * k + T, 0:G], wsel[:, k, :], prob[:, k, :], start=True, stop=True)
                    ins.then_inc(s["am_mm"], 1)
                if a:
                    scores(0)
                if b:
                    wait(pe, s["am_a"], one(b))
                    for k in range(2):
                        ins = TR(PA[:, 128 * k:128 * k + 128], am[:, 128 * k:128 * k + 128], ident[:, :])
                    ins.then_inc(s["amT_mm"], 1)
                if a:
                    scores(1)
                if b:
                    wait(pe, s["amT_a"], one(b))
                    for k in range(BT):
                        for m in range(2):
                            ins = MM(PA[T * k:T * k + T, 0:DV], amT[:, m, T * k:T * k + T], ctx_n[b.p][:, k, m, :], start=m == 0, stop=m == 1)
                    ins.then_inc(s["z_mm"], 1)
                if dd:
                    wait(pe, s["dots_a"], one(dd))
                    wide(1, D0, e_w1, xT3, None, range(2))
                if b:
                    wait(pe, s["z_v"], one(b))
                    TR(PA[:, 256:384], z[:, 0:128], ident[:, :])
                    TR(PA[0:64, 384:512], z[:, 128:DV], ident[:, :]).then_inc(s["zT_mm"], 1)
                if dd:
                    wide(1, D0, e_w1, xT3, "e1b_mm", range(2, 4))
                if b:
                    wait(pe, s["zT_a"], one(b))
                    wait(pe, s["gb_a"], b.count(1, 0))
                    MM(B0[:, :], zT1[:, :], film1[:, 0:512], start=True, stop=False)
                    MM(B0[:, :], zT2[:, :], film2[:, 0:512], start=False, stop=True).then_inc(s["fin_mm"], 1)
                if dd:
                    wait(pe, s["gate_v"], one(dd))
                    TR(PA[0:NE, 0:128], gate[:, :], ident[:, :]).then_inc(s["gT_mm"], 1)
                if a:
                    scores(2)
                if b:
                    wait(pe, s["xf_v"], one(b))
                    wait(pe, s["xt2_v"], b.count(1, 0))
                    for k, bank in enumerate((B1[:, 0:D], B1[:, D:2 * D], B0[:, 0:D])):
                        ins = MM(bank, dft_x[:, k, :], xf[:, :], start=True, stop=True)
                    ins.then_inc(s["fwd_mm"], 1)
                if c:
                    wait(pe, s["xl2_v"], one(c))
                    wait(pe, s["x2_v"], c.count(1, 0))
                    transposes(C0, xl2, "xT2_mm")
                if a:
                    scores(3)
                if c:
                    wait(pe, s["xT2_a"], one(c))
                    for m in range(2):
                        for k in range(2):
                            ins = MM(C0[:, D + 128 * m:D + 128 * m + 128], qk_w[:, k, 128 * m:128 * m + 128], xT2[:, 128 * k:128 * k + 128], start=k == 0, stop=k == 1)
                    for k in range(2):
                        ins = MM(C0[:, 0:D], xT2[:, 128 * k:128 * k + 128], wv_w[:, k, :], start=k == 0, stop=k == 1)
                    ins.then_inc(s["v_mm"], 1)
                if b:
                    wait(pe, s["had_v"], one(b))
                    for k in range(3):
                        ins = MM(B0[:, D:2 * D], dft_y[:, k, :], had[:, k, :], start=k == 0, stop=k == 2)
                    ins.then_inc(s["inv_mm"], 1)
                if c:
                    wait(pe, s["v_a"], one(c))
                    for k in range(BT):
                        rows = slice(T * k, T * k + T)
                        for m in range(2):
                            cols = slice(128 * m + T * k, 128 * m + T * k + T)
                            ins = MM(C0[rows, D:D + T], xmT[:, cols], xT2[:, cols], start=m == 0, stop=m == 1)
                    ins.then_inc(s["s_mm"], 1)
                if b:
                    MM(B1[:, :], zT1[:, :], film1[:, 512:1024], start=True, stop=False)
                    MM(B1[:, :], zT2[:, :], film2[:, 512:1024], start=False, stop=True).then_inc(s["y_mm"], 1)
                if dd:
                    experts(range(0, 2))
                if c:
                    wait(pe, s["pt_v"], one(c))
                    for k in range(BT):
                        for j in range(4):
                            vals = v_c[:, :].rearrange("p (j2 j t) -> p j2 j t", j2=2, j=4)[:, :, j, :]
                            o = C0[T * j:T * j + T, D + 64 * k:D + 64 * k + 64].rearrange("p (a t) -> p a t", a=2)
                            ins = MM(o, pT_blk[:, k, :], vals, start=True, stop=True)
                    ins.then_inc(s["r_mm"], 1)
                if dd:
                    experts(range(2, 4))
                if c:
                    wait(pe, s["r_a"], one(c))
                    for k in range(2):
                        ins = MM(C0[:, 0:D], r_c[:, k, :, :].rearrange("p b t -> p (b t)"), wo_w[:, k, :], start=k == 0, stop=k == 1)
                    ins.then_inc(s["o2_mm"], 1)
                if dd:
                    experts(range(4, 6))
                    experts(range(6, 8))
                if b:
                    wait(pe, s["hn_v"], one(b))
                    wait(pe, s["xt_v"], one(b))
                    transposes(B0, hn, "hT_mm")
                if dd:
                    experts(range(8, NE + 1))
                if b:
                    wait(pe, s["hT_a"], one(b))
                    wide(0, B1, w1, hT, "w1a_mm")
                    wide(1, B0, w1, hT, "w1b_mm")

            pe.wait_ge(s["ld_cent"], LD_CENT)
            pe.wait_ge(s["ones_set"], 2)
            step(*tiles(0, 0))
            pe.wait_ge(s["ld_film"], LD_FILM)
            for rows, m, (f_in, f_out) in ((slice(0, 128), 128, (B0, B1)), (slice(128, 192), 64, (D0, D1))):
                for f, bank in enumerate((f_in, f_out)):
                    for k in range(2):
                        ins = MM(bank[0:m, :], wvT[:, k, rows], wff[:, k, f * 512:f * 512 + 512], start=k == 0, stop=k == 1)
            ins.then_inc(s["film_mm"], 1)
            pe.wait_ge(s["ld_w"], LD_W)
            pe.wait_ge(s["mr1_v"], 4)
            pe.wait_ge(s["exp_a"], 4)
            for m in range(HID // 128):
                for k in range(2):
                    ins = MM(S[0][:, m:m + 1], w1[:, k, 128 * m:128 * m + 128], bffn[:, k:k + 1], start=k == 0, stop=k == 1)
            ins.then_inc(s["b1_mm"], 1)
            for m in range(2):
                for k in range(2):
                    ins = MM(C0[:, m * D:m * D + D], awq[:, k, 128 * m:128 * m + 128], awk[:, k, :], start=k == 0, stop=k == 1)
            ins.then_inc(s["qkw_mm"], 1)
            pe.wait_ge(s["cent_n"], 1)
            pe.wait_ge(s["b1_sb"], 1)
            for k in range(2):
                ins = TR(S[1][:, NE * k:NE * k + NE], cent[:, 128 * k:128 * k + 128], ident[0:NE, 0:NE])
            ins.then_inc(s["cent_t"], 1)
            pe.wait_ge(s["film_sb"], 1)
            pe.wait_ge(s["setup_prod"], 1)
            for lag in range(T):
                MM(D1[0:T, 0:D], hot[:, T - 1 - lag:2 * T - 1 - lag], ang[:, lag, :], start=lag == 0, stop=False)
            MM(D1[0:T, 0:D], one0[:, :], dskip[:, :], start=False, stop=True).then_inc(s["kt_mm"], 1)
            pe.wait_ge(s["kt_sb"], 1)
            for k, bank in enumerate((D1[:, 0:D], D1[:, D:2 * D], D0[:, 0:D])):
                ins = MM(bank, dft_k[:, k, :], kern_t[:, :], start=True, stop=True)
            ins.then_inc(s["kf_mm"], 1)
            pe.wait_ge(s["kf_sb"], 1)
            pe.wait_ge(s["qkw_sb"], 1)
            pe.wait_ge(s["ld_w2"], LD_W2)

            run(ET.PE, step)


def _constants():
    f = np.float32
    n = 2 * T
    ph = 2 * np.pi * np.outer(np.arange(1, T), np.arange(T)) / n
    C, S = np.cos(ph), -np.sin(ph)
    one, alt, nil = np.ones((1, T)), ((-1.0) ** np.arange(T))[None], np.zeros((1, T))
    fx = [np.vstack([C + S, one]), np.vstack([C, alt]), np.vstack([S, nil])]
    fk = [np.vstack([C, one]), np.vstack([S - C, alt]), np.vstack([C + S, nil])]
    fy = [np.vstack([(C + S) * 2 / n, one / n]), np.vstack([S * 2 / n, alt / n]), np.vstack([-C * 2 / n, nil])]
    eye = np.eye(BT)
    half = np.repeat([0.0, 1.0], NS)
    hot = np.zeros((128, 2 * T - 1), f)
    hot[:, T - 1] = 2.0
    one0 = np.zeros((1, T), f)
    one0[0, 0] = 1.0
    mask = np.kron(eye, np.ones((T, T)))
    return {
        "ident": np.eye(128, dtype=f),
        "sel": np.tile(np.eye(T, dtype=f), (H, 1)),
        "block_mask": mask.reshape(128, BT, T).astype(f),
        "dft_x": np.stack([np.kron(eye, m.T) for m in fx], 1).astype(f),
        "dft_y": np.stack([np.kron(eye, m) for m in fy], 1).astype(f),
        "dft_k": np.stack([np.tile(m.T, (1, BT)) for m in fk], 1).astype(f),
        "phase": np.stack([0.25 * (1 - half), 0.25 * half, np.pi / 2 * (1 - half), np.pi / 2 * half, 1 - 2 * half,
                           PI_IN - np.pi / 2 * (1 - half), -PI_IN - np.pi / 2 * (1 - half),
                           PI_IN - np.pi / 2 * half, -PI_IN - np.pi / 2 * half], 1).astype(f),
        "hot": hot,
        "one0": one0,
    }


def kernel(**inputs):
    import concourse.bacc as _bacc
    from concourse.bass_utils import run_bass_kernel_spmd as _run

    raw = {k: np.asarray(v) for k, v in inputs.items()}
    xa = lambda n: raw["L0_xattn_" + n]
    chunks = lambda w: w.reshape(-1, 128, w.shape[-1]).transpose(1, 0, 2)
    cols = lambda v: v.reshape(-1, 128).T
    context = raw["ctx_768"]
    ctxT = context.transpose(2, 0, 1).reshape(DV, NT, BT, G).transpose(1, 0, 2, 3)
    awvT = raw["L0_attn_wv"].T.reshape(D, T, 8).transpose(0, 2, 1).reshape(D, D)
    arrays = {
        "x": raw["x"].reshape(NT, 128, D).transpose(1, 0, 2),
        "ctx_n": context[:, :256].reshape(NT, BT, 2, 128, DV).transpose(0, 3, 1, 2, 4),
        "ctx_l": context[:, 256:].reshape(NT, BT, 1, DV),
        "ctxT1": ctxT[:, 0:128],
        "ctxT2": ctxT[:, 128:DV],
        "vmask": raw["mask_BxS2_bf1"].view(np.uint8),
        "tmaskT": raw["mask_BxS_bf1"].view(np.uint8).T,
        "Wq": chunks(xa("Wq")), "WkT": xa("Wk").T, "WvT": chunks(xa("Wv").T),
        "W_film_in": chunks(xa("W_film_in")), "W_film_out": chunks(xa("W_film_out")),
        "b_film_in": xa("b_film_in")[None], "b_film_out": xa("b_film_out")[None],
        "g_norm_in": xa("g_norm_in")[None], "b_norm_in": xa("b_norm_in")[None],
        "g_norm_out": xa("g_norm_out")[None], "b_norm_out": xa("b_norm_out")[None],
        "g_ffn": cols(xa("g_ffn")), "b_ffn": cols(xa("b_ffn")),
        "W1": chunks(xa("W1")), "b1": cols(xa("b1")), "W2": chunks(xa("W2")), "b2": xa("b2")[None],
        "log_dt": xa("log_dt")[None], "A_re": xa("A_re").T, "A_im": xa("A_im").T,
        "C_re": xa("C_re").T, "C_im": xa("C_im").T, "D_skip": xa("D_skip")[None],
        "mod_gate": xa("mod_gate").reshape(1, 1),
        "awq": chunks(raw["L0_attn_wq"]), "awk": chunks(raw["L0_attn_wk"]),
        "awvT": chunks(awvT), "awoT": chunks(raw["L0_attn_wo"].T),
        "routeT": chunks(raw["L0_ffn_w_route"].T), "cent": raw["L0_ffn_centroids"],
        "e_w1": chunks(raw["L0_ffn_w1"].transpose(1, 0, 2).reshape(D, HID)),
        "e_w2": raw["L0_ffn_w2"].transpose(1, 0, 2), "e_b1": raw["L0_ffn_b1"].T, "e_b2": raw["L0_ffn_b2"],
        **_constants(),
    }
    arrays = {f"in_{k}": np.ascontiguousarray(v) for k, v in arrays.items()}
    nc = _bacc.Bacc("TRN2", target_bir_lowering=False, num_devices=1)
    aps = {k[3:]: nc.dram_tensor(k, v.shape, mybir.dt.from_np(v.dtype), kind="ExternalInput").ap() for k, v in arrays.items()}
    out = nc.dram_tensor("out", (NT, 128, D), F32, kind="ExternalOutput").ap()
    build(nc, aps, out)
    r = _run(nc, [arrays], core_ids=[0])
    return r.results[0]["out"].reshape(NB, T, D)
```

```python
from contextlib import ExitStack

import numpy as np
import concourse.bass as bass
from concourse import mybir
from concourse.alu_op_type import AluOpType as ALU

F32 = mybir.dt.float32
I32 = mybir.dt.int32
U8 = mybir.dt.uint8
ACT = mybir.ActivationFunctionType
AXX = mybir.AxisListType.X
ET = mybir.EngineType

NB, T, D = 64, 32, 256
G, DV = 257, 192
H, DH = 4, 32
TOPK, NS = 32, 64
HID, NE = 1024, 8
BT = 128 // T
NT = NB // BT
EPS = 1e-5
SCALE = float(1.0 / np.sqrt(np.float32(DH)))
TAKEN = -3.0e38
MASKED = 1.0e30
MAGIC = 12582912.0
RSQRT0 = float(0x5F3759DF)
TWO_PI = 2 * np.pi
PI_HI = 6.28125
PI_LO = float(TWO_PI - 6.28125)
PI_IN = 3.1415925
WEXP = [0, 1, 2, 3, 4, 5, 6, 7, 8, 16, 24, 0, 8, 16, 24, 1]
NP, NPOW = 11, len(WEXP)


class Tile:

    def __init__(self, base, c):
        self.base, self.c, self.p = base, c, c % 2
        self.static = isinstance(base, int)
        self.n = base + c

    def count(self, per, more):
        if self.static:
            v = per * (self.base + self.c) + more
            return v if v > 0 else None
        return self.base * per + (per * self.c + more)

    def half(self, per, more):
        if self.static:
            v = per * ((self.base + self.c) // 2) + more
            return v if v > 0 else None
        return self.base * (per // 2) + (per * (self.c // 2) + more)


def wait(eng, sem, value):
    if value is not None:
        eng.wait_ge(sem, value)


def wait_apart(eng, sem, value, passed):
    wait(eng, sem, value)
    if value is not None and not isinstance(value, int):
        eng.sem_inc(passed, 1)


def build(nc, d, out):
    with ExitStack() as ctx:
        def sb(name, shape, dt=F32):
            return ctx.enter_context(nc.sbuf_tensor(name, shape, dt))

        def pb(name):
            return ctx.enter_context(nc.psum_tensor(name, [128, 512], F32))

        def sem(name):
            return ctx.enter_context(nc.semaphore(name))

        mask_dram = nc.dram_tensor("mask_scratch", [NT, BT * G], F32, kind="Internal").ap()
        any_dram = nc.dram_tensor("any_scratch", [NB, 1], F32, kind="Internal").ap()

        x_all = sb("x_all", [128, NT, D])
        ident = sb("ident", [128, 128])
        sel = sb("sel", [128, T])
        block_mask = sb("block_mask", [128, BT, T])
        wq = sb("wq", [128, 2, 128])
        wk_pad = sb("wk_pad", [128, H, DV])
        film1 = sb("film1", [128, 4 * D])
        film2 = sb("film2", [65, 4 * D])
        w1 = sb("w1", [128, 2, HID])
        expw = sb("expw", [128, NPOW, D])
        w2 = expw[:, 0:HID // 128, :]
        b1 = sb("b1", [128, HID // 128])
        b2 = sb("b2", [128, D])
        gout = sb("gout", [128, D])
        bout = sb("bout", [128, D])
        qk_w = sb("qk_w", [128, 2, D])
        wv_w = sb("wv_w", [128, 2, D])
        wo_w = sb("wo_w", [128, 2, D])
        route = sb("route", [128, 2, 2 * NE])
        e_w1 = sb("e_w1", [128, 2, HID])
        e_w2 = expw[:, HID // 128:HID // 128 + NE, :]
        e_b1 = sb("e_b1", [128, NE])
        e_b2 = sb("e_b2", [NE, D])
        dft_x = sb("dft_x", [128, 3, 128])
        dft_y = sb("dft_y", [128, 3, 128])
        kern_f = sb("kern_f", [128, 3, D])
        text_m = sb("text_m", [128, NB])
        mean_x = sb("mean_x", [128, NT, 2])
        rs_x = sb("rs_x", [128, 2, NT])

        ctx_n = [sb(f"ctx_n{i}", [128, BT, 2, DV]) for i in range(2)]
        ctx_l = [sb(f"ctx_l{i}", [128, DV]) for i in range(2)]
        ctx_t1 = [sb(f"ctx_t1_{i}", [128, BT, G]) for i in range(2)]
        ctx_t2 = [sb(f"ctx_t2_{i}", [65, BT, G]) for i in range(2)]

        ang = sb("ang", [128, 2 * NPOW, D])
        flat = {"ang": ang[:, :, :].rearrange("p a b -> p (a b)")}
        at = {"ang": 0}

        def over(buf, *shape):
            n = int(np.prod(shape))
            v = flat[buf][:, at[buf]:at[buf] + n]
            at[buf] += n
            assert v.shape[1] == n
            if len(shape) == 1:
                return v
            if len(shape) == 2:
                return v.rearrange("p (a b) -> p a b", a=shape[0])
            return v.rearrange("p (a b c) -> p a b c", a=shape[0], b=shape[1])

        xln = [sb(f"xln{i}", [128, D]) for i in range(2)]
        xhat = [sb(f"xhat{i}", [128, D]) for i in range(2)]
        xT = sb("xT", [128, D])
        qT = sb("qT", [128, 128])
        qk1 = sb("qk1", [128, BT, H, T])
        work = sb("work", [128, BT, G])
        expo = sb("expo", [128, BT, G])
        prob = sb("prob", [128, BT, G])
        am = sb("am", [128, G])
        qk2 = sb("qk2", [65, BT, H, T])
        top = sb("top", [128, BT, TOPK])
        nmax = sb("nmax", [128, BT])
        psum_row = sb("psum_row", [128, BT])
        rsum_row = sb("rsum_row", [128, BT])
        tm_tile = sb("tm_tile", [128, BT])
        wsel = sb("wsel", [128, BT, T])
        amT = sb("amT", [128, 2, 128])
        z = sb("z", [128, DV])
        zT1 = sb("zT1", [128, 128])
        zT2 = sb("zT2", [65, 128])
        xf = over("ang", D)
        had = over("ang", 3, D)
        yb = over("ang", D)
        xt = over("ang", D)
        xt_b = over("ang", D)
        hn = over("ang", D)
        hT = over("ang", D)
        act1 = over("ang", HID // 128, 128)
        xt2 = over("ang", D)
        u_c = over("ang", D)
        xb_c = over("ang", D)
        x1 = over("ang", D)
        xl2 = over("ang", D)
        xT2 = over("ang", D)
        xmT = over("ang", D)
        v_c = over("ang", D)
        r_c = over("ang", 2, BT, T)
        x2 = [over("ang", D) for _ in range(2)]
        nmax_c = sb("nmax_c", [128, 1])
        p_c = sb("p_c", [128, T])
        sum_c = sb("sum_c", [128, 1])
        rsum_c = sb("rsum_c", [128, 1])
        pn_c = sb("pn_c", [128, T])
        pT_c = sb("pT_c", [128, T])
        pT_blk = sb("pT_blk", [128, BT, T])
        xl3 = over("ang", D)
        xT3 = over("ang", D)
        act2 = over("ang", NE, 128)
        acc = [over("ang", D) for _ in range(2)]
        dots = sb("dots", [128, 2 * NE])
        logit = sb("logit", [128, NE])
        best = sb("best", [128, NE])
        nbest = sb("nbest", [128, 1])
        e_d = sb("e_d", [128, NE])
        pg = sb("pg", [128, NE])
        sum_d = sb("sum_d", [128, 1])
        rsum_d = sb("rsum_d", [128, 1])
        gate = sb("gate", [128, NE])
        gateT = sb("gateT", [NE, 128])
        out_sb = [sb(f"out_sb{i}", [128, D]) for i in range(2)]
        bn = [sb(f"bn{i}", [128, 6]) for i in range(4)]
        mv = [sb(f"mv{i}", [128, 2]) for i in range(4)]
        var_in = [sb(f"var_in{i}", [128, 4]) for i in range(4)]
        rstd = [sb(f"rstd{i}", [128, 1]) for i in range(4)]
        nw_h = sb("nw_h", [128, 2 * NT])
        nw_t = sb("nw_t", [128, 2 * NT])
        inorm = sb("inorm", [128, 1])

        s4 = sb("s4", [128, 4, D])
        s4c = sb("s4c", [128, 8, D])
        s4a = sb("s4a", [128, 2, D])
        uu = sb("uu", [128, 4, D])
        brow = uu[0:65, :, :].rearrange("p a b -> p (a b)")
        logdt = sb("logdt", [128, D])
        phase = sb("phase", [128, 9])
        kern_t = sb("kern_t", [128, D])
        hot = sb("hot", [128, 2 * T - 1])
        one0 = sb("one0", [1, T])
        dskip = sb("dskip", [1, D])
        dft_k = sb("dft_k", [128, 3, 128])
        bn_x = sb("bn_x", [128, 2, 6])
        var_x = sb("var_x", [128, 2, NT])
        wff = s4c[:, :, :].rearrange("p (k a) b -> p k (a b)", k=2)
        brow2 = sb("brow2", [65, 3 * D])
        gin = sb("gin", [128, D])
        bin_ = sb("bin", [128, D])
        mgate = sb("mgate", [128, 1])
        film_t = sb("film_t", [128, D])
        gffn = sb("gffn", [128, 2])
        bffn = sb("bffn", [128, 2])
        b1raw = sb("b1raw", [128, HID // 128])
        awq = e_w1[:, 0, 0:2 * D].rearrange("p (a b) -> p a b", a=2)
        awk = e_w1[:, 0, 2 * D:4 * D].rearrange("p (a b) -> p a b", a=2)
        wvT = e_w1[:, 1, 0:2 * DV].rearrange("p (a b) -> p a b", a=2)
        cent = sb("cent", [NE, D])
        cent2 = prob[0:NE, 0, 0:D]
        cent_s = sb("cent_s", [NE, 1])
        cent_r = sb("cent_r", [NE, 1])
        vm8 = sb("vm8", [NB, G], U8)
        valid = prob[0:NB, 1, :]
        vm = sb("vm", [NB, G])
        anyv = sb("anyv", [NB, 3])
        anyb = sb("anyb", [128, NB])
        tm8 = sb("tm8", [128, NB], U8)

        S = [pb("S0"), pb("S1")]
        PA = pb("PA")
        B0, B1 = pb("B0"), pb("B1")
        C0 = pb("C0")
        D0, D1 = pb("D0"), pb("D1")

        names = ("ld_w ld_film ld_s4 ld_cent ld_any scratch_out ld_dt fills chain_v chain_g a_sq a_rec ca uu_v prod_g "
                 "bnx_done rsx_done setup_dt setup_ang setup_mul setup_exp setup_turn setup_red setup_sin setup_prod kt_mm kt_sb kf_mm kf_sb "
                 "film_mm film_sb b1_mm ld_w2 qkw_mm qkw_sb cent_ss cent_rs cent_n cent_t setup_v tm_ready "
                 "xln_v xT_mm xT_a qT_mm qT_a qk_mm qk_a sc_mm mr1_v nmax_v exp_a prob_v rsum_v wsel_g am_mm am_a amT_mm amT_a z_mm z_v zT_mm zT_a "
                 "fin_mm xf_v fwd_mm had_v inv_mm y_a y_mm xt_v st0_v rs0_g xtb_g hn_v hT_mm hT_a w1a_mm w1b_mm ga_a gb_a h2_mm xt2_v st1_v rs1_g "
                 "xb_g x1_v st2_v rs2_g xl2_v xT2_mm xT2_a v_mm v_a s_mm nmaxc_v pc_a pt_v r_mm r_a o2_mm x2_v st3_v rs3_g inorm_g "
                 "xl3_v xT3_mm xT3_a lg_mm dots_a nbest_v ed_a gate_v gT_mm gT_a e1a_mm e1b_mm g2a_a g2b_a eo_mm acc_v fin_v").split()
        s = {n: sem(n) for n in names}
        chains = {n: sem("self_" + n) for n in "tm g0 g1 g2 g3 len bn0 bn1 bn2 bn3 top taken u xhat xf logit best pg rsd yb rsc pn pT".split()}
        passed_v, passed_g = sem("passed_v"), sem("passed_g")
        ld_x = [sem(f"ld_x{k}") for k in range(4)]
        ld_ctx = [sem("ld_ctx0"), sem("ld_ctx1")]
        st_out = [sem("st_out0"), sem("st_out1")]

        LD_DT, LD_CENT, LD_S4, LD_FILM, LD_W, LD_W2 = 16 * 6, 16 * 13, 16 * 8, 16 * 8, 16 * 17, 16 * 3

        LOOP0 = 5
        LOOPS = (NT - LOOP0) // 2 * 2

        def tiles(base, first):
            return [Tile(base, first - k) if not isinstance(base, int) or 0 <= first - k < NT else None for k in range(4)]

        def next_tile(a):
            return None if not a or (a.static and a.n == NT - 1) else Tile(a.base, a.c + 1)

        def run(engine, step):
            for n in range(1, LOOP0):
                step(*tiles(0, n))
            with nc.Fori(0, LOOPS - 1, 2, engines=(engine,)) as base:
                for n in range(2):
                    step(*tiles(base, LOOP0 + n))
            for n in range(LOOP0 + LOOPS, NT + 3):
                step(*tiles(0, n))

        block = ctx.enter_context(nc.Block())

        @block.sync
        def _(sp):
            def load(dst, src, to):
                sp.dma_start(dst, src).then_inc(s[to], 16)

            load(logdt[:, :], d["log_dt"].broadcast_to([128, D]), "ld_dt")
            for k in range(2):
                for half in range(2):
                    load(s4[NS * half:NS * half + NS, k, :], d[("A_re", "A_im")[k]], "ld_dt")
            load(phase[:, :], d["phase"], "ld_dt")
            for k in range(4):
                sp.dma_start(x_all[:, 4 * k:4 * k + 4, :], d["x"][:, 4 * k:4 * k + 4, :]).then_inc(ld_x[k], 16)
            load(vm8[:, :], d["vmask"], "ld_cent")
            load(ident[:, :], d["ident"], "ld_cent")
            load(cent[:, :], d["cent"], "ld_cent")
            load(sel[:, :], d["sel"], "ld_cent")
            load(wq[:, :, :], d["Wq"], "ld_cent")
            for h in range(H):
                load(tm8[T * h:T * h + T, :], d["tmaskT"], "ld_cent")
            sp.wait_ge(s["fills"], 1)
            for h in range(H):
                load(wk_pad[DH * h:DH * h + DH, h, :], d["WkT"][DH * h:DH * h + DH, :], "ld_cent")
            sp.wait_ge(s["setup_v"], 1)
            load(mask_dram.rearrange("a (b g) -> (a b) g", b=BT), vm[:, :], "scratch_out")
            load(any_dram, anyv[:, 2:3], "scratch_out")
            sp.wait_ge(s["scratch_out"], 32)
            load(anyb[:, :], any_dram.rearrange("b o -> o b").broadcast_to([128, NB]), "ld_any")
            late_loads = [
                (wvT, d["WvT"], "ld_film"), (wff[:, :, 0:2 * D], d["W_film_in"], "ld_film"), (wff[:, :, 2 * D:4 * D], d["W_film_out"], "ld_film"),
                (brow[64:65, 0:2 * D], d["b_film_in"], "ld_film"), (brow[64:65, 2 * D:4 * D], d["b_film_out"], "ld_film"),
                (gin[:, :], d["g_norm_in"].broadcast_to([128, D]), "ld_film"), (bin_[:, :], d["b_norm_in"].broadcast_to([128, D]), "ld_film"),
                (mgate[:, :], d["mod_gate"].broadcast_to([128, 1]), "ld_film"),
                (dft_x[:, :, :], d["dft_x"], "ld_w"), (dft_y[:, :, :], d["dft_y"], "ld_w"), (block_mask[:, :, :], d["block_mask"], "ld_w"),
                (w1[:, :, :], d["W1"], "ld_w"), (b1raw[:, :], d["b1"], "ld_w"), (gffn[:, :], d["g_ffn"], "ld_w"), (bffn[:, :], d["b_ffn"], "ld_w"),
                (b2[:, :], d["b2"].broadcast_to([128, D]), "ld_w"), (gout[:, :], d["g_norm_out"].broadcast_to([128, D]), "ld_w"),
                (bout[:, :], d["b_norm_out"].broadcast_to([128, D]), "ld_w"), (awq, d["awq"], "ld_w"), (awk, d["awk"], "ld_w"),
                (wv_w[:, :, :], d["awvT"], "ld_w"), (wo_w[:, :, :], d["awoT"], "ld_w"), (route[:, :, 0:NE], d["routeT"], "ld_w"),
                (e_b1[:, :], d["e_b1"], "ld_w"), (e_b2[:, :], d["e_b2"], "ld_w"),
            ]

            def step(a, b, c, dd):
                if a:
                    wait(sp, s["z_v"], a.count(1, -1))
                    at = ld_ctx[a.p]
                    sp.dma_start(ctx_t1[a.p][:, :, :], d["ctxT1"][a.n]).then_inc(at, 16)
                    sp.dma_start(ctx_t2[a.p][0:64, :, :], d["ctxT2"][a.n]).then_inc(at, 16)
                    sp.dma_start(ctx_t2[a.p][64:65, :, :], mask_dram[a.n].rearrange("(o b g) -> o b g", o=1, b=BT)).then_inc(at, 16)
                    sp.dma_start(ctx_n[a.p][:, :, :, :], d["ctx_n"][a.n]).then_inc(at, 16)
                    for k in range(BT):
                        sp.dma_start(ctx_l[a.p][T * k:T * k + T, :], d["ctx_l"][a.n, k].broadcast_to([T, DV])).then_inc(at, 16)
                if dd:
                    wait(sp, s["fin_v"], dd.count(1, 1))
                    sp.dma_start(out[dd.n], out_sb[dd.p][:, :]).then_inc(st_out[dd.p], 16)

            step(Tile(0, 0), None, None, None)
            for k, n in enumerate(("C_re", "C_im")):
                for half in range(2):
                    load(s4[NS * half:NS * half + NS, 2 + k, :], d[n], "ld_s4")
            load(hot[:, :], d["hot"], "ld_s4")
            load(one0[:, :], d["one0"], "ld_s4")
            load(dskip[:, :], d["D_skip"], "ld_s4")
            load(dft_k[:, :, :], d["dft_k"], "ld_s4")
            for dst, src, to in late_loads:
                load(dst, src, to)
            step(Tile(0, 1), None, None, None)
            sp.wait_ge(s["qkw_mm"], 1)
            load(e_w1[:, :, :], d["e_w1"], "ld_w2")
            sp.wait_ge(s["prod_g"], 1)
            sp.wait_ge(s["setup_prod"], 3)
            load(w2, d["W2"], "ld_w2")
            load(e_w2, d["e_w2"], "ld_w2")
            for n in range(1, LOOP0):
                step(Tile(0, n + 1), None, None, Tile(0, n - 3) if n >= 3 else None)
            with nc.Fori(0, LOOPS - 1, 2, engines=(ET.SP,)) as base:
                for n in range(2):
                    step(Tile(base, LOOP0 + n + 1), None, None, Tile(base, LOOP0 + n - 3))
            for n in range(LOOP0 + LOOPS, NT + 3):
                step(Tile(0, n + 1) if n + 1 < NT else None, None, None, Tile(0, n - 3))
            for p in range(2):
                sp.wait_ge(st_out[p], 16 * NT // 2)

        N_CTX = 16 * (4 + BT)

        @block.gpsimd
        def _(pool):
            ts, tt = nc.gpsimd.tensor_scalar, nc.gpsimd.tensor_tensor
            count = [0]

            def link(ins):
                ins.then_inc(s["chain_g"], 1)
                count[0] += 1
                pool.wait_ge(s["chain_g"], count[0])

            def newton(w, h, y, t, link):
                link(ts(y.bitcast(I32), w.bitcast(I32), -0.5, RSQRT0, ALU.mult, ALU.add))
                for k in range(3):
                    link(ts(t, y, y, h, ALU.mult, ALU.mult))
                    last = ts(y, t, 1.5, y, ALU.add, ALU.mult)
                    if k < 2:
                        link(last)
                return last

            def newton_wide(w, y, h, t):
                link(ts(h, w, -0.5, None, ALU.mult))
                link(ts(y.bitcast(I32), w.bitcast(I32), -0.5, RSQRT0, ALU.mult, ALU.add))
                for k in range(3):
                    link(tt(t, y, y, ALU.mult))
                    link(tt(t, t, h, ALU.mult))
                    link(ts(t, t, 1.5, None, ALU.add))
                    last = tt(y, y, t, ALU.mult)
                    if k < 2:
                        link(last)
                return last

            nc.gpsimd.memset(wk_pad[:, :, :], 0.0).then_inc(s["fills"], 1)
            pool.wait_ge(s["fills"], 1)
            nc.gpsimd.memset(qk2[64:65, :, :, :], 1.0).then_inc(s["fills"], 1)
            nc.gpsimd.memset(zT2[64:65, :], 1.0).then_inc(s["fills"], 1)
            pool.wait_ge(s["fills"], 3)
            are, aim, cre, cim = (s4[:, k, :] for k in range(4))
            over_re, over_im, part, square = out_sb[0][:, :], out_sb[1][:, :], amT[:, :, :].rearrange("p a b -> p (a b)"), am[:, 0:D]
            pool.wait_ge(s["ld_dt"], LD_DT)
            link(tt(part, are, are, ALU.mult))
            link(tt(square, aim, aim, ALU.mult))
            tt(square, square, part, ALU.add).then_inc(s["a_sq"], 1)
            pool.wait_ge(s["bnx_done"], 1)
            var_all = mean_x[:, :, 1]
            link(ts(var_x[:, 0, :], var_all, EPS, None, ALU.add))
            link(ts(var_x[:, 1, :], var_all, 1.0 + EPS, EPS * EPS, ALU.mult, ALU.add))
            newton_wide(var_x[:, :, :].rearrange("p a b -> p (a b)"), rs_x[:, :, :].rearrange("p a b -> p (a b)"), nw_h[:, :], nw_t[:, :]).then_inc(s["rsx_done"], 1)
            pool.wait_ge(s["cent_ss"], 1)
            newton_wide(cent_s[:, :], cent_r[:, :], nw_h[0:NE, 0:1], nw_t[0:NE, 0:1]).then_inc(s["cent_rs"], 1)
            pool.wait_ge(s["tm_ready"], 1)
            pool.wait_ge(s["ld_s4"], LD_S4)
            pool.wait_ge(s["a_rec"], 1)
            link(tt(over_re, cre, are, ALU.mult))
            link(tt(over_im, cim, aim, ALU.mult))
            link(tt(over_re, over_re, over_im, ALU.add))
            link(tt(over_im, cim, are, ALU.mult))
            link(tt(part, cre, aim, ALU.mult))
            link(tt(over_im, over_im, part, ALU.subtract))
            link(tt(over_re, over_re, square, ALU.mult))
            tt(over_im, over_im, square, ALU.mult).then_inc(s["ca"], 1)

            def links(name, tile, n):
                k = [0]

                def link(ins):
                    ins.then_inc(chains[name], 1)
                    k[0] += 1
                    wait_apart(pool, chains[name], tile.count(n, k[0]), passed_g)
                return link

            def norm(k, tile):
                wait_apart(pool, s[f"st{k}_v"], tile.count(1, 1), passed_g)
                w, h, y, t = (var_in[k][:, i:i + 1] for i in range(4))
                v = mv[k][:, 1:2]
                link = links(f"g{k}", tile, 8)
                link(ts(h, v, EPS, -0.5, ALU.add, ALU.mult))
                link(ts(w, v, EPS, None, ALU.add))
                newton(w, h, rstd[k][:, 0:1], t, link).then_inc(s[f"rs{k}_g"], 1)

            def length(tile):
                w, h, y, t = (var_in[3][:, i:i + 1] for i in range(4))
                v = mv[3][:, 1:2]
                wait_apart(pool, s["rs3_g"], tile.count(1, 1), passed_g)
                link = links("len", tile, 9)
                link(ts(h, v, -0.5, None, ALU.mult))
                link(newton(v, h, y, t, link))
                link(ts(t, rstd[3][:, 0:1], w, y, ALU.mult, ALU.mult))
                ts(inorm[:, :], t, float(D) ** -0.5, 1e12, ALU.mult, ALU.min).then_inc(s["inorm_g"], 1)

            def step(a, b, c, dd):
                def weights(t, q):
                    wait_apart(pool, chains["tm"], t.count(1, 1), passed_g)
                    wait_apart(pool, s["rsum_v"], t.count(2, q + 1), passed_g)
                    wait_apart(pool, s["am_mm"], t.count(1, 0), passed_g)
                    for k in (2 * q, 2 * q + 1):
                        nc.gpsimd.tensor_scalar(wsel[:, k, :], sel[:, :], rsum_row[:, k:k + 1], tm_tile[:, k:k + 1], ALU.mult, ALU.mult).then_inc(s["wsel_g"], 1)
                if b:
                    weights(b, 1)
                if a:
                    wait_apart(pool, s["wsel_g"], a.count(4, 0), passed_g)
                    nc.gpsimd.tensor_copy(tm_tile[:, :], text_m[:, bass.ds(a.n * BT, BT)]).then_inc(chains["tm"], 1)
                if c:
                    wait_apart(pool, s["x1_v"], c.count(1, 0), passed_g)
                    nc.gpsimd.tensor_tensor(xb_c[:, :], x_all[:, c.n, :], bout[:, :], ALU.add).then_inc(s["xb_g"], 1)
                    norm(1, c)
                    norm(2, c)
                if b:
                    norm(0, b)
                    nc.gpsimd.tensor_tensor(xt_b[:, :], xt[:, :], b2[:, :], ALU.add).then_inc(s["xtb_g"], 1)
                if c:
                    norm(3, c)
                    length(c)
                if a:
                    weights(a, 0)

            step(*tiles(0, 0))
            pool.wait_ge(s["uu_v"], 1)
            tt(ang[:, 24:32, :], expw[:, 0:8, :], uu[:, 3, :].rearrange("p (o b) -> p o b", o=1).broadcast_to([128, 8, D]), ALU.mult).then_inc(s["prod_g"], 1)
            pool.wait_ge(s["kf_sb"], 1)
            pool.wait_ge(s["ld_w"], LD_W)
            run(ET.Pool, step)

        @block.scalar
        def _(act):
            A = nc.scalar.activation

            def copy(dst, src, done):
                A(dst, src, ACT.Copy).then_inc(s[done], 1)

            def gelus(dst, half, bank, bias, mm, done, tile):
                wait(act, s[mm], tile.count(1, 1))
                for k in range(4 * half, 4 * half + 4):
                    ins = A(dst[:, k, :], bank[:, 128 * (k % 4):128 * (k % 4) + 128], ACT.Gelu, bias=bias[:, k:k + 1])
                ins.then_inc(s[done], 1)

            def transposed(a):
                wait(act, s["xT_mm"], a.count(1, 1))
                copy(xT[:, :], PA[:, 0:D], "xT_a")

            def query(a):
                wait(act, s["qT_mm"], a.count(1, 1))
                copy(qT[:, :], PA[:, D:D + 128], "qT_a")

            def keyed(a):
                wait(act, s["qk_mm"], a.count(1, 1))
                A(qk1[:, :, :, :].rearrange("p b h t -> p h b t"), S[0][:, :].rearrange("p (h b t) -> p h b t", h=H, b=BT), ACT.Copy)
                A(qk2[0:64, :, :, :].rearrange("p b h t -> p h b t"), S[1][0:64, :].rearrange("p (h b t) -> p h b t", h=H, b=BT), ACT.Copy).then_inc(s["qk_a"], 1)

            def step(a, b, c, dd, setup=None):
                one = lambda t: t.count(1, 1)
                following = next_tile(a)

                def exps(q):
                    for k in range(2):
                        wait(act, s["mr1_v"], a.count(4, 2 * q + k + 1))
                        A(expo[:, 2 * q + k, :], S[k][:, 0:G], ACT.Exp, bias=nmax[:, 2 * q + k:2 * q + k + 1], scale=SCALE).then_inc(s["exp_a"], 1)
                if dd:
                    wait(act, s["xT3_mm"], one(dd))
                    copy(xT3[:, :], D0[:, 0:D], "xT3_a")
                    wait(act, s["lg_mm"], one(dd))
                    copy(dots[:, :], D0[:, D:D + 2 * NE], "dots_a")
                if b:
                    wait(act, s["am_mm"], one(b))
                    copy(am[:, :], PA[:, 0:G], "am_a")
                    wait(act, s["amT_mm"], one(b))
                    copy(amT[:, :, :].rearrange("p a b -> p (a b)"), PA[:, 0:256], "amT_a")
                if a:
                    exps(0)
                if setup:
                    setup()
                if dd:
                    wait(act, s["nbest_v"], one(dd))
                    A(e_d[:, :], logit[:, :], ACT.Exp, bias=nbest[:, :]).then_inc(s["ed_a"], 1)
                if b:
                    wait(act, s["zT_mm"], one(b))
                    A(zT1[:, :], PA[:, 256:384], ACT.Copy)
                    A(zT2[0:64, :], PA[0:64, 384:512], ACT.Copy).then_inc(s["zT_a"], 1)
                if dd:
                    wait(act, s["gT_mm"], one(dd))
                    copy(gateT[:, :], PA[0:NE, 0:128], "gT_a")
                    gelus(act2, 0, D1, e_b1, "e1a_mm", "g2a_a", dd)
                    gelus(act2, 1, D0, e_b1, "e1b_mm", "g2b_a", dd)
                if c:
                    wait(act, s["xT2_mm"], one(c))
                    copy(xT2[:, :], C0[:, 0:D], "xT2_a")
                if a:
                    exps(1)
                if b:
                    wait(act, s["inv_mm"], one(b))
                    copy(yb[:, :], B0[:, D:2 * D], "y_a")
                if c:
                    wait(act, s["v_mm"], one(c))
                    A(xmT[:, :], C0[:, D:2 * D], ACT.Copy)
                    copy(v_c[:, :], C0[:, 0:D], "v_a")
                    wait(act, s["nmaxc_v"], one(c))
                    A(p_c[:, :], C0[:, D:D + T], ACT.Exp, bias=nmax_c[:, :], accum_out=sum_c[:, :]).then_inc(s["pc_a"], 1)
                if following:
                    transposed(following)
                if c:
                    wait(act, s["r_mm"], one(c))
                    A(r_c[:, :, :, :].rearrange("p j b t -> p b j t"), C0[:, D:2 * D].rearrange("p (b j t) -> p b j t", b=BT, j=2), ACT.Copy).then_inc(s["r_a"], 1)
                if following:
                    query(following)
                if b:
                    wait(act, s["hT_mm"], one(b))
                    copy(hT[:, :], B0[:, 0:D], "hT_a")
                if following:
                    keyed(following)
                if b:
                    gelus(act1, 0, B1, b1, "w1a_mm", "ga_a", b)
                    gelus(act1, 1, B0, b1, "w1b_mm", "gb_a", b)

            act.wait_ge(s["ld_dt"], LD_DT)
            A(logdt[:, :], logdt[:, :], ACT.Exp).then_inc(s["setup_dt"], 1)
            act.wait_ge(s["setup_ang"], 1)
            for j, power in enumerate(WEXP):
                A(ang[:, j, :], s4a[:, 1, :], ACT.Copy, scale=float(power)).then_inc(s["setup_mul"], 1)
            act.wait_ge(s["setup_mul"], NPOW)
            A(ang[:, NPOW:NPOW + NP, :], ang[:, 0:NP, :], ACT.Identity, scale=1 / TWO_PI, bias=phase[:, 0:1])
            A(ang[:, NPOW + NP:2 * NPOW, :], ang[:, NP:NPOW, :], ACT.Identity, scale=1 / TWO_PI, bias=phase[:, 1:2]).then_inc(s["setup_turn"], 1)
            for j, power in enumerate(WEXP):
                ins = A(expw[:, j, :], s4a[:, 0, :], ACT.Exp, scale=float(power))
            ins.then_inc(s["setup_exp"], 1)

            def sines():
                act.wait_ge(s["setup_red"], 1)
                A(ang[:, 0:NP, :], ang[:, 0:NP, :], ACT.Sin, bias=phase[:, 2:3])
                A(ang[:, NP:NPOW, :], ang[:, NP:NPOW, :], ACT.Sin, bias=phase[:, 3:4]).then_inc(s["setup_sin"], 1)

            transposed(Tile(0, 0))
            query(Tile(0, 0))
            keyed(Tile(0, 0))
            step(*tiles(0, 0), sines)
            act.wait_ge(s["kt_mm"], 1)
            copy(kern_t[:, :], PA[:, 0:D], "kt_sb")
            act.wait_ge(s["kf_mm"], 1)
            for k in range(2):
                A(kern_f[:, k, :], D1[:, k * D:(k + 1) * D], ACT.Copy)
            copy(kern_f[:, 2, :], D0[:, 0:D], "kf_sb")
            run(ET.Activation, step)

        @block.vector
        def _(dve):
            V = nc.vector
            n_chain = [0]

            def link(ins):
                ins.then_inc(s["chain_v"], 1)
                n_chain[0] += 1
                dve.wait_ge(s["chain_v"], n_chain[0])

            dve.wait_ge(s["setup_dt"], 1)
            V.tensor_tensor(s4a[:, 0, :], logdt[:, :], s4[:, 0, :], ALU.mult)
            V.tensor_tensor(s4a[:, 1, :], logdt[:, :], s4[:, 1, :], ALU.mult).then_inc(s["setup_ang"], 1)
            for t in range(NT):
                if t % 4 == 0:
                    dve.wait_ge(ld_x[t // 4], 16)
                link(V.bn_stats(bn_x[:, t % 2, :], x_all[:, t, :]))
                ins = V.bn_aggr(mean_x[:, t, :], bn_x[:, t % 2, :])
            ins.then_inc(s["bnx_done"], 1)
            dve.wait_ge(s["ld_cent"], LD_CENT)
            link(V.tensor_copy(valid, vm8[:, :]))
            V.tensor_scalar(vm[:, :], valid, MASKED, -MASKED, ALU.mult, ALU.add)
            link(V.reduce_max(anyv[:, 0:1], valid, AXX))
            link(V.reciprocal(anyv[:, 1:2], anyv[:, 0:1]))
            V.tensor_tensor(anyv[:, 2:3], anyv[:, 0:1], anyv[:, 1:2], ALU.mult).then_inc(s["setup_v"], 1)
            link(V.tensor_tensor(cent2[:, :], cent[:, :], cent[:, :], ALU.mult))
            V.reduce_sum(cent_s[:, :], cent2[:, :], AXX).then_inc(s["cent_ss"], 1)
            dve.wait_ge(s["a_sq"], 1)
            V.reciprocal(am[:, 0:D], am[:, 0:D]).then_inc(s["a_rec"], 1)
            dve.wait_ge(s["setup_turn"], 1)
            turn = ang[:, NPOW:2 * NPOW, :]
            link(V.tensor_scalar(turn, turn, MAGIC, -MAGIC, ALU.add, ALU.add))

            def reduce_angles():
                link(V.scalar_tensor_tensor(ang[:, 0:NPOW, :], turn, -PI_HI, ang[:, 0:NPOW, :], ALU.mult, ALU.add))
                link(V.scalar_tensor_tensor(ang[:, 0:NPOW, :], turn, -PI_LO, ang[:, 0:NPOW, :], ALU.mult, ALU.add))
                V.tensor_scalar(ang[:, 0:NP, :], ang[:, 0:NP, :], phase[:, 5:6], phase[:, 6:7], ALU.min, ALU.max)
                V.tensor_scalar(ang[:, NP:NPOW, :], ang[:, NP:NPOW, :], phase[:, 7:8], phase[:, 8:9], ALU.min, ALU.max).then_inc(s["setup_red"], 1)

            def film_bias():
                dve.wait_ge(s["ld_film"], LD_FILM)
                r = slice(64, 65)
                link(V.tensor_scalar(brow2[r, 0:D], brow[r, 0:D], mgate[r, :], 1.0, ALU.mult, ALU.add))
                V.tensor_tensor(film2[r, 0:D], brow2[r, 0:D], gin[r, :], ALU.mult)
                link(V.tensor_tensor(brow2[r, D:2 * D], brow2[r, 0:D], bin_[r, :], ALU.mult))
                V.scalar_tensor_tensor(film2[r, D:2 * D], brow[r, D:2 * D], mgate[r, :], brow2[r, D:2 * D], ALU.mult, ALU.add)
                V.tensor_scalar(film2[r, 2 * D:3 * D], brow[r, 2 * D:3 * D], mgate[r, :], 1.0, ALU.mult, ALU.add)
                V.tensor_scalar(film2[r, 3 * D:4 * D], brow[r, 3 * D:4 * D], mgate[r, :], None, ALU.mult)

            def film_weights():
                dve.wait_ge(s["film_mm"], 1)
                for rows, f_in, f_out, dst in ((slice(0, 128), B0, B1, film1), (slice(0, 64), D0, D1, film2)):
                    V.tensor_scalar(dst[rows, 2 * D:4 * D], f_out[rows, :], mgate[rows, :], None, ALU.mult)
                    V.scalar_tensor_tensor(dst[rows, 0:D], f_in[rows, 0:D], mgate[rows, :], gin[rows, :], ALU.mult, ALU.mult)
                    link(V.scalar_tensor_tensor(film_t[rows, :], f_in[rows, 0:D], mgate[rows, :], bin_[rows, :], ALU.mult, ALU.mult))
                    link(V.scalar_tensor_tensor(dst[rows, D:2 * D], f_in[rows, D:2 * D], mgate[rows, :], film_t[rows, :], ALU.mult, ALU.add))
                dve.sem_inc(s["film_sb"], 1)

            def kernel_terms():
                dve.wait_ge(s["ld_s4"], LD_S4)
                dve.wait_ge(s["setup_exp"], 1)
                dve.wait_ge(s["setup_sin"], 1)
                link(V.tensor_tensor(expw[:, :, :], expw[:, :, :], ang[:, 0:NPOW, :], ALU.mult))
                dve.wait_ge(s["film_mm"], 1)
                lo, hi = slice(0, NS), slice(NS, 2 * NS)
                wr, wi = s4c[:, 0, :], s4c[:, 1, :]
                V.tensor_scalar(s4c[lo, 0, :], expw[lo, 1, :], -1.0, None, ALU.add)
                V.tensor_scalar(s4c[hi, 0, :], expw[hi, NPOW - 1, :], -1.0, None, ALU.add)
                V.tensor_copy(s4c[lo, 1, :], expw[lo, NPOW - 1, :])
                link(V.tensor_copy(s4c[hi, 1, :], expw[hi, 1, :]))
                t0, t1, t2, t3 = (s4c[:, k, :] for k in range(2, 6))
                qr, qi = out_sb[0][:, :], out_sb[1][:, :]
                tt = lambda o, a, b, op: V.tensor_tensor(o, a, b, op)
                dve.wait_ge(s["ca"], 1)
                tt(t0, qr, wr, ALU.mult)
                tt(t1, qi, wi, ALU.mult)
                tt(t2, qr, wi, ALU.mult)
                link(tt(t3, qi, wr, ALU.mult))
                tt(t1, t0, t1, ALU.subtract)
                link(V.scalar_tensor_tensor(t3, t2, -1.0, t3, ALU.mult, ALU.subtract))
                link(V.tensor_scalar(t1, t1, phase[:, 4:5], None, ALU.mult))
                wide = lambda v, n: v.rearrange("p (o b) -> p o b", o=1).broadcast_to([128, n, D])
                tt(uu[:, 0, :], expw[:, 0, :], t1, ALU.mult)
                tt(uu[:, 1:4, :], expw[:, 8:11, :], wide(t1, 3), ALU.mult)
                link(tt(expw[:, 11:15, :], expw[:, 11:15, :], wide(t3, 4), ALU.mult))
                link(tt(uu[:, :, :], uu[:, :, :], expw[:, 11:15, :], ALU.add))
                dve.sem_inc(s["uu_v"], 1)
                for k in range(3):
                    tt(ang[:, 8 * k:8 * k + 8, :], expw[:, 0:8, :], wide(uu[:, k, :], 8), ALU.mult).then_inc(s["setup_prod"], 1)

            def other_weights():
                dve.wait_ge(s["b1_mm"], 1)
                V.tensor_tensor(b1[:, :], S[0][:, 0:HID // 128], b1raw[:, :], ALU.add)
                for k in range(2):
                    V.tensor_scalar(w1[:, k, :], w1[:, k, :], gffn[:, k:k + 1], None, ALU.mult)
                dve.wait_ge(s["qkw_mm"], 1)
                V.tensor_scalar(qk_w[:, :, :].rearrange("p a b -> p (a b)"), C0[:, :], 0.25, None, ALU.mult)
                dve.wait_ge(s["cent_t"], 1)
                V.tensor_copy(route[:, :, NE:2 * NE], S[1][:, 0:2 * NE].rearrange("p (a b) -> p a b", a=2)).then_inc(s["qkw_sb"], 1)
                dve.wait_ge(s["kf_sb"], 1)

            def stats(k, src, tile, done):
                V.bn_stats(bn[k][:, :], src).then_inc(chains[f"bn{k}"], 1)
                wait_apart(dve, chains[f"bn{k}"], tile.count(1, 1), passed_v)
                V.bn_aggr(mv[k][:, :], bn[k][:, :]).then_inc(s[done], 1)

            def norm_input(t):
                V.tensor_scalar(xln[t.p][:, :], x_all[:, t.n, :], mean_x[:, t.n, 0:1], rs_x[:, 0, bass.ds(t.n, 1)], ALU.subtract, ALU.mult).then_inc(s["xln_v"], 1)

            def norm_twice(t):
                V.tensor_scalar(xhat[t.p][:, :], x_all[:, t.n, :], mean_x[:, t.n, 0:1], rs_x[:, 1, bass.ds(t.n, 1)], ALU.subtract, ALU.mult).then_inc(chains["xhat"], 1)

            TOP_AT = ((0, 4, 6, 8), (2, 10, 12, 14))

            def step(a, b, c, dd):
                one = lambda t: t.count(1, 1)
                following = next_tile(a)

                def maxima(a, q):
                    for k in range(2):
                        wait_apart(dve, s["sc_mm"], a.count(4, 2 * q + k + 1), passed_v)
                        V.max(top[:, 2 * q + k, 0:8], S[k][:, 0:G]).then_inc(chains["top"], 1)
                    wait(dve, chains["top"], a.count(16, TOP_AT[q][0] + 2))
                    V.tensor_scalar(nmax[:, 2 * q:2 * q + 2], top[:, 2 * q:2 * q + 2, 0], -SCALE, None, ALU.mult).then_inc(s["nmax_v"], 1)

                def take(a, q):
                    for k in range(2):
                        V.match_replace(work[:, 2 * q + k, :], top[:, 2 * q + k, 0:8], S[k][:, 0:G], TAKEN).then_inc(s["mr1_v"], 1)

                def top8(a, q, r8):
                    find8(a, q, r8)
                    take8(a, q, r8)

                def find8(a, q, r8):
                    for k in range(2):
                        if r8 == 1:
                            wait_apart(dve, s["mr1_v"], a.count(4, 2 * q + k + 1), passed_v)
                        else:
                            wait_apart(dve, chains["taken"], a.count(12, 6 * q + 2 * (r8 - 2) + k + 1), passed_v)
                        V.max(top[:, 2 * q + k, 8 * r8:8 * r8 + 8], work[:, 2 * q + k, :]).then_inc(chains["top"], 1)

                def take8(a, q, r8):
                    for k in range(2):
                        wait_apart(dve, chains["top"], a.count(16, TOP_AT[q][r8] + k + 1), passed_v)
                        V.match_replace(work[:, 2 * q + k, :], top[:, 2 * q + k, 8 * r8:8 * r8 + 8], work[:, 2 * q + k, :], TAKEN).then_inc(chains["taken"], 1)

                def probs(a, q):
                    wait(dve, s["am_mm"], a.count(1, 0))
                    for k in range(2):
                        wait(dve, chains["taken"], a.count(12, 6 * q + 4 + k + 1))
                        wait(dve, s["exp_a"], a.count(4, 2 * q + k + 1))
                        V.scalar_tensor_tensor(prob[:, 2 * q + k, :], work[:, 2 * q + k, :], TAKEN, expo[:, 2 * q + k, :], ALU.is_equal, ALU.mult,
                                               accum_out=psum_row[:, 2 * q + k:2 * q + k + 1]).then_inc(s["prob_v"], 1)
                    wait(dve, s["prob_v"], a.count(4, 2 * q + 2))
                    wait(dve, s["wsel_g"], a.count(4, 2 * q - 2))
                    V.reciprocal(rsum_row[:, 2 * q:2 * q + 2], psum_row[:, 2 * q:2 * q + 2]).then_inc(s["rsum_v"], 1)

                def gated(ks):
                    for k in ks:
                        bank = (D1, D0)[k // 2 % 2][:, k % 2 * D:k % 2 * D + D]
                        wait(dve, s["eo_mm"], dd.count(NE + 1, min(k // 2 * 2 + 2, NE + 1)))
                        if k == 0:
                            wait(dve, s["gate_v"], one(dd))
                            V.scalar_tensor_tensor(acc[0][:, :], bank, gate[:, 0:1], x2[dd.p][:, :], ALU.mult, ALU.add).then_inc(s["acc_v"], 1)
                        elif k == 1:
                            V.tensor_scalar(acc[1][:, :], bank, gate[:, 1:2], None, ALU.mult).then_inc(s["acc_v"], 1)
                        else:
                            wait(dve, s["acc_v"], dd.count(NE + 1, k - 1))
                            if k < NE:
                                V.scalar_tensor_tensor(acc[k % 2][:, :], bank, gate[:, k:k + 1], acc[k % 2][:, :], ALU.mult, ALU.add).then_inc(s["acc_v"], 1)
                            else:
                                V.tensor_tensor(acc[0][:, :], bank, acc[0][:, :], ALU.add).then_inc(s["acc_v"], 1)

                if dd:
                    wait(dve, s["rs3_g"], one(dd))
                    V.tensor_scalar(xl3[:, :], x2[dd.p][:, :], mv[3][:, 0:1], rstd[3][:, 0:1], ALU.subtract, ALU.mult).then_inc(s["xl3_v"], 1)
                if b:
                    top8(b, 1, 3)
                    probs(b, 1)
                if c:
                    wait(dve, s["h2_mm"], one(c))
                    wait(dve, s["xtb_g"], one(c))
                    V.tensor_tensor(xt2[:, :], xt_b[:, :], B1[:, 0:D], ALU.add).then_inc(s["xt2_v"], 1)
                    wait_apart(dve, s["xt2_v"], one(c), passed_v)
                    stats(1, xt2[:, :], c, "st1_v")
                if a:
                    maxima(a, 0)
                    take(a, 0)
                if dd:
                    wait(dve, s["dots_a"], one(dd))
                    wait(dve, s["inorm_g"], one(dd))
                    V.scalar_tensor_tensor(logit[:, :], dots[:, NE:2 * NE], inorm[:, :], dots[:, 0:NE], ALU.mult, ALU.add).then_inc(chains["logit"], 1)
                    wait_apart(dve, chains["logit"], one(dd), passed_v)
                    V.max(best[:, :], logit[:, :]).then_inc(chains["best"], 1)
                if b:
                    wait(dve, s["z_mm"], one(b))
                    V.scalar_tensor_tensor(z[:, :], ctx_l[b.p][:, :], am[:, G - 1:G], PA[:, 0:DV], ALU.mult, ALU.add).then_inc(s["z_v"], 1)
                if c:
                    wait(dve, s["rs1_g"], one(c))
                    V.tensor_scalar(u_c[:, :], xt2[:, :], mv[1][:, 0:1], rstd[1][:, 0:1], ALU.subtract, ALU.mult).then_inc(chains["u"], 1)
                if dd:
                    wait(dve, chains["best"], one(dd))
                    V.tensor_scalar(nbest[:, :], best[:, 0:1], -1.0, None, ALU.mult).then_inc(s["nbest_v"], 1)
                if c:
                    wait(dve, chains["u"], c.count(2, 1))
                    V.tensor_tensor(u_c[:, :], u_c[:, :], gout[:, :], ALU.mult).then_inc(chains["u"], 1)
                    wait(dve, chains["u"], c.count(2, 2))
                    wait(dve, s["xb_g"], one(c))
                    V.tensor_tensor(x1[:, :], u_c[:, :], xb_c[:, :], ALU.add).then_inc(s["x1_v"], 1)
                    wait_apart(dve, s["x1_v"], one(c), passed_v)
                    stats(2, x1[:, :], c, "st2_v")
                if dd:
                    wait(dve, s["ed_a"], one(dd))
                    V.scalar_tensor_tensor(pg[:, :], logit[:, :], best[:, 1:2], e_d[:, :], ALU.is_ge, ALU.mult, accum_out=sum_d[:, :]).then_inc(chains["pg"], 1)
                    wait(dve, chains["pg"], one(dd))
                    V.reciprocal(rsum_d[:, :], sum_d[:, :]).then_inc(chains["rsd"], 1)
                    wait(dve, chains["rsd"], one(dd))
                    V.tensor_scalar(gate[:, :], pg[:, :], rsum_d[:, :], None, ALU.mult).then_inc(s["gate_v"], 1)
                if b:
                    wait(dve, s["fin_mm"], one(b))
                    wait(dve, chains["xhat"], one(b))
                    V.tensor_tensor(xf[:, :], xhat[b.p][:, :], B0[:, 0:D], ALU.mult).then_inc(chains["xf"], 1)
                    wait(dve, chains["xf"], one(b))
                    V.tensor_tensor(xf[:, :], xf[:, :], B0[:, D:2 * D], ALU.add).then_inc(s["xf_v"], 1)
                if c:
                    wait(dve, s["rs2_g"], one(c))
                    V.tensor_scalar(xl2[:, :], x1[:, :], mv[2][:, 0:1], rstd[2][:, 0:1], ALU.subtract, ALU.mult).then_inc(s["xl2_v"], 1)
                if b:
                    wait(dve, s["fwd_mm"], one(b))
                    V.tensor_tensor(had[:, 0:2, :].rearrange("p a b -> p (a b)"), B1[:, :], kern_f[:, 0:2, :].rearrange("p a b -> p (a b)"), ALU.mult)
                    V.tensor_tensor(had[:, 2, :], B0[:, 0:D], kern_f[:, 2, :], ALU.mult).then_inc(s["had_v"], 1)
                if a:
                    maxima(a, 1)
                    take(a, 1)
                    top8(a, 0, 1)
                    top8(a, 0, 2)
                if b:
                    wait(dve, s["y_a"], one(b))
                    wait(dve, s["y_mm"], one(b))
                    V.tensor_tensor(yb[:, :], yb[:, :], B1[:, 0:D], ALU.mult).then_inc(chains["yb"], 1)
                    wait(dve, chains["yb"], b.count(2, 1))
                    V.tensor_tensor(yb[:, :], yb[:, :], B1[:, D:2 * D], ALU.add).then_inc(chains["yb"], 1)
                    wait(dve, chains["yb"], b.count(2, 2))
                    V.tensor_tensor(xt[:, :], yb[:, :], xln[b.p][:, :], ALU.add).then_inc(s["xt_v"], 1)
                    wait_apart(dve, s["xt_v"], one(b), passed_v)
                    V.bn_stats(bn[0][:, :], xt[:, :]).then_inc(chains["bn0"], 1)
                if following:
                    norm_input(following)
                if b:
                    wait_apart(dve, chains["bn0"], one(b), passed_v)
                    V.bn_aggr(mv[0][:, :], bn[0][:, :]).then_inc(s["st0_v"], 1)
                if c:
                    wait(dve, s["s_mm"], one(c))
                    V.reduce_max(nmax_c[:, :], C0[:, D:D + T], AXX, negate=True).then_inc(s["nmaxc_v"], 1)
                if dd:
                    gated(range(0, 2))
                if c:
                    wait(dve, s["pc_a"], one(c))
                    V.reciprocal(rsum_c[:, :], sum_c[:, :]).then_inc(chains["rsc"], 1)
                    wait(dve, chains["rsc"], one(c))
                    V.tensor_scalar(pn_c[:, :], p_c[:, :], rsum_c[:, :], None, ALU.mult).then_inc(chains["pn"], 1)
                    wait_apart(dve, chains["pn"], one(c), passed_v)
                    V.transpose(pT_c[:, :], pn_c[:, :]).then_inc(chains["pT"], 1)
                    wait(dve, chains["pT"], one(c))
                    V.tensor_tensor(pT_blk[:, :, :], pT_c[:, :].rearrange("p (o t) -> p o t", o=1).broadcast_to([128, BT, T]), block_mask[:, :, :], ALU.mult).then_inc(s["pt_v"], 1)
                if following:
                    norm_twice(following)
                if dd:
                    gated(range(2, 4))
                if a:
                    find8(a, 0, 3)
                    take8(a, 0, 3)
                if dd:
                    gated(range(4, 6))
                if b:
                    wait(dve, s["rs0_g"], one(b))
                    V.tensor_scalar(hn[:, :], xt[:, :], mv[0][:, 0:1], rstd[0][:, 0:1], ALU.subtract, ALU.mult).then_inc(s["hn_v"], 1)
                if c:
                    wait(dve, s["o2_mm"], one(c))
                    V.tensor_tensor(x2[c.p][:, :], x1[:, :], C0[:, 0:D], ALU.add).then_inc(s["x2_v"], 1)
                    wait_apart(dve, s["x2_v"], one(c), passed_v)
                    stats(3, x2[c.p][:, :], c, "st3_v")
                if a:
                    probs(a, 0)
                    top8(a, 1, 1)
                if dd:
                    gated(range(6, 8))
                if a:
                    top8(a, 1, 2)
                if dd:
                    gated(range(8, NE + 1))
                    wait(dve, s["acc_v"], dd.count(NE + 1, NE + 1))
                    wait(dve, st_out[dd.p], dd.half(16, 0))
                    V.tensor_tensor(out_sb[dd.p][:, :], acc[0][:, :], acc[1][:, :], ALU.add).then_inc(s["fin_v"], 1)

            dve.wait_ge(s["rsx_done"], 1)
            norm_input(Tile(0, 0))
            norm_twice(Tile(0, 0))
            dve.wait_ge(s["ld_any"], 16)
            link(V.tensor_copy(text_m[:, :], tm8[:, :]))
            V.scalar_tensor_tensor(text_m[:, :], text_m[:, :], 1.0 / H, anyb[:, :], ALU.mult, ALU.mult).then_inc(s["tm_ready"], 1)
            reduce_angles()
            dve.wait_ge(s["cent_rs"], 1)
            link(V.tensor_scalar(cent_r[:, :], cent_r[:, :], 1e12, None, ALU.min))
            V.tensor_scalar(cent[:, :], cent[:, :], cent_r[:, :], None, ALU.mult).then_inc(s["cent_n"], 1)
            step(*tiles(0, 0))
            film_bias()
            kernel_terms()
            film_weights()
            other_weights()
            run(ET.DVE, step)

        @block.tensor
        def _(pe):
            MM, TR = nc.tensor.matmul, nc.tensor.transpose
            def transposes(dst, src, done):
                for k in range(2):
                    ins = TR(dst[:, 128 * k:128 * k + 128], src[:, 128 * k:128 * k + 128], ident[:, :])
                ins.then_inc(s[done], 1)

            def transposed(a):
                wait(pe, s["xln_v"], a.count(1, 1))
                transposes(PA, xln[a.p], "xT_mm")

            def query(a):
                wait(pe, s["xT_a"], a.count(1, 1))
                for k in range(2):
                    ins = MM(PA[:, D:D + 128], wq[:, k, :], xT[:, 128 * k:128 * k + 128], start=k == 0, stop=k == 1)
                ins.then_inc(s["qT_mm"], 1)

            def keyed(a, heads):
                wait(pe, s["qT_a"], a.count(1, 1))
                wait(pe, s["mr1_v"], a.count(4, 0))
                wait(pe, s["exp_a"], a.count(4, 0))
                for h in heads:
                    MM(S[0][:, 128 * h:128 * h + 128], wk_pad[:, h, 0:128], qT[:, :], start=True, stop=True)
                    ins = MM(S[1][0:64, 128 * h:128 * h + 128], wk_pad[:, h, 128:DV], qT[:, :], start=True, stop=True)
                if h == H - 1:
                    ins.then_inc(s["qk_mm"], 1)

            def step(a, b, c, dd, setup=None):
                one = lambda t: t.count(1, 1)
                following = next_tile(a)

                def scores(k):
                    wait(pe, s["qk_a"], one(a))
                    if k == 0:
                        pe_ctx = a.half(N_CTX, N_CTX)
                        wait(pe, ld_ctx[a.p], pe_ctx)
                    if k >= 2:
                        wait(pe, s["mr1_v"], a.count(4, k - 1))
                        wait(pe, s["exp_a"], a.count(4, k - 1))
                    bank = S[k % 2]
                    MM(bank[:, 0:G], qk1[:, k, :, :].rearrange("p h t -> p (h t)"), ctx_t1[a.p][:, k, :], start=True, stop=False)
                    MM(bank[:, 0:G], qk2[:, k, :, :].rearrange("p h t -> p (h t)"), ctx_t2[a.p][:, k, :], start=False, stop=True).then_inc(s["sc_mm"], 1)

                def wide(half, bank, w, xs, done, ms=range(4)):
                    for m in ms:
                        at = 128 * (4 * half + m)
                        for k in range(2):
                            ins = MM(bank[:, 128 * m:128 * m + 128], w[:, k, at:at + 128], xs[:, 128 * k:128 * k + 128], start=k == 0, stop=k == 1)
                    if done:
                        ins.then_inc(s[done], 1)

                def experts(ks):
                    for k in ks:
                        bank = (D1, D0)[k // 2 % 2][:, k % 2 * D:k % 2 * D + D]
                        if k == 0:
                            wait(pe, s["g2a_a"], one(dd))
                        elif k == 2:
                            wait(pe, s["g2b_a"], one(dd))
                        elif k >= 4 and k % 2 == 0:
                            wait(pe, s["acc_v"], dd.count(NE + 1, k - 2))
                        if k == NE:
                            wait(pe, s["gT_a"], one(dd))
                            MM(bank, gateT[:, :], e_b2[:, :], start=True, stop=True).then_inc(s["eo_mm"], 1)
                        else:
                            MM(bank, act2[:, k, :], e_w2[:, k, :], start=True, stop=True).then_inc(s["eo_mm"], 1)

                def down(half):
                    wait(pe, s[("ga_a", "gb_a")[half]], one(c))
                    for k in range(4 * half, 4 * half + 4):
                        ins = MM(B1[:, 0:D], act1[:, k, :], w2[:, k, :], start=k == 0, stop=k == HID // 128 - 1)
                    if half == 1:
                        ins.then_inc(s["h2_mm"], 1)

                if c:
                    down(0)
                    down(1)
                if dd:
                    wait(pe, s["xl3_v"], one(dd))
                    wait(pe, s["acc_v"], dd.count(NE + 1, 0))
                    transposes(D0, xl3, "xT3_mm")
                if a:
                    scores(0)
                    scores(1)
                if dd:
                    wait(pe, s["xT3_a"], one(dd))
                    for k in range(2):
                        ins = MM(D0[:, D:D + 2 * NE], xT3[:, 128 * k:128 * k + 128], route[:, k, :], start=k == 0, stop=k == 1)
                    ins.then_inc(s["lg_mm"], 1)
                if b:
                    wait(pe, s["prob_v"], b.count(4, 4))
                    wait(pe, s["wsel_g"], b.count(4, 4))
                    for k in range(BT):
                        ins = MM(PA[T * k:T * k + T, 0:G], wsel[:, k, :], prob[:, k, :], start=True, stop=True)
                    ins.then_inc(s["am_mm"], 1)
                if dd:
                    wide(0, D1, e_w1, xT3, None, range(2))
                if b:
                    wait(pe, s["am_a"], one(b))
                    for k in range(2):
                        ins = TR(PA[:, 128 * k:128 * k + 128], am[:, 128 * k:128 * k + 128], ident[:, :])
                    ins.then_inc(s["amT_mm"], 1)
                if dd:
                    wide(0, D1, e_w1, xT3, "e1a_mm", range(2, 4))
                if b:
                    wait(pe, s["amT_a"], one(b))
                    for k in range(BT):
                        for m in range(2):
                            ins = MM(PA[T * k:T * k + T, 0:DV], amT[:, m, T * k:T * k + T], ctx_n[b.p][:, k, m, :], start=m == 0, stop=m == 1)
                    ins.then_inc(s["z_mm"], 1)
                if dd:
                    wait(pe, s["dots_a"], one(dd))
                    wide(1, D0, e_w1, xT3, None, range(2))
                if b:
                    wait(pe, s["z_v"], one(b))
                    TR(PA[:, 256:384], z[:, 0:128], ident[:, :])
                    TR(PA[0:64, 384:512], z[:, 128:DV], ident[:, :]).then_inc(s["zT_mm"], 1)
                if dd:
                    wide(1, D0, e_w1, xT3, "e1b_mm", range(2, 4))
                if b:
                    wait(pe, s["zT_a"], one(b))
                    wait(pe, s["gb_a"], b.count(1, 0))
                    MM(B0[:, :], zT1[:, :], film1[:, 0:512], start=True, stop=False)
                    MM(B0[:, :], zT2[:, :], film2[:, 0:512], start=False, stop=True).then_inc(s["fin_mm"], 1)
                if dd:
                    wait(pe, s["gate_v"], one(dd))
                    TR(PA[0:NE, 0:128], gate[:, :], ident[:, :]).then_inc(s["gT_mm"], 1)
                if a:
                    scores(2)
                if b:
                    wait(pe, s["xf_v"], one(b))
                    wait(pe, s["xt2_v"], b.count(1, 0))
                    for k, bank in enumerate((B1[:, 0:D], B1[:, D:2 * D], B0[:, 0:D])):
                        ins = MM(bank, dft_x[:, k, :], xf[:, :], start=True, stop=True)
                    ins.then_inc(s["fwd_mm"], 1)
                if a:
                    scores(3)
                if setup:
                    setup()
                if c:
                    wait(pe, s["xl2_v"], one(c))
                    wait(pe, s["x2_v"], c.count(1, 0))
                    transposes(C0, xl2, "xT2_mm")
                if b:
                    wait(pe, s["had_v"], one(b))
                    for k in range(3):
                        ins = MM(B0[:, D:2 * D], dft_y[:, k, :], had[:, k, :], start=k == 0, stop=k == 2)
                    ins.then_inc(s["inv_mm"], 1)
                    MM(B1[:, :], zT1[:, :], film1[:, 512:1024], start=True, stop=False)
                    MM(B1[:, :], zT2[:, :], film2[:, 512:1024], start=False, stop=True).then_inc(s["y_mm"], 1)
                if c:
                    wait(pe, s["xT2_a"], one(c))
                    for m in range(2):
                        for k in range(2):
                            ins = MM(C0[:, D + 128 * m:D + 128 * m + 128], qk_w[:, k, 128 * m:128 * m + 128], xT2[:, 128 * k:128 * k + 128], start=k == 0, stop=k == 1)
                    for k in range(2):
                        ins = MM(C0[:, 0:D], xT2[:, 128 * k:128 * k + 128], wv_w[:, k, :], start=k == 0, stop=k == 1)
                    ins.then_inc(s["v_mm"], 1)
                if dd:
                    experts(range(0, 2))
                if c:
                    wait(pe, s["v_a"], one(c))
                    for k in range(BT):
                        rows = slice(T * k, T * k + T)
                        for m in range(2):
                            cols = slice(128 * m + T * k, 128 * m + T * k + T)
                            ins = MM(C0[rows, D:D + T], xmT[:, cols], xT2[:, cols], start=m == 0, stop=m == 1)
                    ins.then_inc(s["s_mm"], 1)
                if dd:
                    experts(range(2, 4))
                if following:
                    if dd:
                        wait(pe, s["gT_a"], one(dd))
                    transposed(following)
                if dd:
                    experts(range(4, 6))
                if c:
                    wait(pe, s["pt_v"], one(c))
                    for k in range(BT):
                        for j in range(4):
                            vals = v_c[:, :].rearrange("p (j2 j t) -> p j2 j t", j2=2, j=4)[:, :, j, :]
                            o = C0[T * j:T * j + T, D + 64 * k:D + 64 * k + 64].rearrange("p (a t) -> p a t", a=2)
                            ins = MM(o, pT_blk[:, k, :], vals, start=True, stop=True)
                    ins.then_inc(s["r_mm"], 1)
                if following:
                    query(following)
                if dd:
                    experts(range(6, 8))
                if c:
                    wait(pe, s["r_a"], one(c))
                    for k in range(2):
                        ins = MM(C0[:, 0:D], r_c[:, k, :, :].rearrange("p b t -> p (b t)"), wo_w[:, k, :], start=k == 0, stop=k == 1)
                    ins.then_inc(s["o2_mm"], 1)
                if following:
                    keyed(following, range(0, 3))
                if b:
                    wait(pe, s["hn_v"], one(b))
                    wait(pe, s["xt_v"], one(b))
                    transposes(B0, hn, "hT_mm")
                if dd:
                    experts(range(8, NE + 1))
                if following:
                    keyed(following, range(3, H))
                if b:
                    wait(pe, s["hT_a"], one(b))
                    wide(0, B1, w1, hT, "w1a_mm")
                    wide(1, B0, w1, hT, "w1b_mm")

            pe.wait_ge(s["ld_cent"], LD_CENT)
            pe.wait_ge(s["fills"], 3)
            def film_products():
                pe.wait_ge(s["ld_film"], LD_FILM)
                for rows, m, (f_in, f_out) in ((slice(0, 128), 128, (B0, B1)), (slice(128, 192), 64, (D0, D1))):
                    for f, bank in enumerate((f_in, f_out)):
                        for k in range(2):
                            ins = MM(bank[0:m, :], wvT[:, k, rows], wff[:, k, f * 512:f * 512 + 512], start=k == 0, stop=k == 1)
                ins.then_inc(s["film_mm"], 1)

            transposed(Tile(0, 0))
            query(Tile(0, 0))
            keyed(Tile(0, 0), range(H))
            step(*tiles(0, 0), film_products)
            pe.wait_ge(s["ld_w"], LD_W)
            for m in range(2):
                for k in range(2):
                    ins = MM(C0[:, m * D:m * D + D], awq[:, k, 128 * m:128 * m + 128], awk[:, k, :], start=k == 0, stop=k == 1)
            ins.then_inc(s["qkw_mm"], 1)
            pe.wait_ge(s["qk_a"], 2)
            for m in range(HID // 128):
                for k in range(2):
                    ins = MM(S[0][:, m:m + 1], w1[:, k, 128 * m:128 * m + 128], bffn[:, k:k + 1], start=k == 0, stop=k == 1)
            ins.then_inc(s["b1_mm"], 1)
            pe.wait_ge(s["cent_n"], 1)
            for k in range(2):
                ins = TR(S[1][:, NE * k:NE * k + NE], cent[:, 128 * k:128 * k + 128], ident[0:NE, 0:NE])
            ins.then_inc(s["cent_t"], 1)
            pe.wait_ge(s["qT_a"], 2)
            for lag in range(T):
                if lag == 24:
                    pe.wait_ge(s["prod_g"], 1)
                elif lag % 8 == 0:
                    pe.wait_ge(s["setup_prod"], lag // 8 + 1)
                rows = slice(T * (lag % 4), T * (lag % 4) + T)
                ins = MM(PA[rows, 0:D], hot[:, T - 1 - lag:2 * T - 1 - lag], ang[:, lag, :], start=lag < 4, stop=lag >= T - 4 and lag % 4 > 0)
            MM(PA[0:T, 0:D], one0[:, :], dskip[:, :], start=False, stop=True).then_inc(s["kt_mm"], 1)
            pe.wait_ge(s["film_sb"], 1)
            pe.wait_ge(s["kt_sb"], 1)
            for k, bank in enumerate((D1[:, 0:D], D1[:, D:2 * D], D0[:, 0:D])):
                ins = MM(bank, dft_k[:, k, :], kern_t[:, :], start=True, stop=True)
            ins.then_inc(s["kf_mm"], 1)
            pe.wait_ge(s["kf_sb"], 1)
            pe.wait_ge(s["qkw_sb"], 1)
            pe.wait_ge(s["ld_w2"], LD_W2)

            run(ET.PE, step)


def _constants():
    f = np.float32
    n = 2 * T
    ph = 2 * np.pi * np.outer(np.arange(1, T), np.arange(T)) / n
    C, S = np.cos(ph), -np.sin(ph)
    one, alt, nil = np.ones((1, T)), ((-1.0) ** np.arange(T))[None], np.zeros((1, T))
    fx = [np.vstack([C + S, one]), np.vstack([C, alt]), np.vstack([S, nil])]
    fk = [np.vstack([C, one]), np.vstack([S - C, alt]), np.vstack([C + S, nil])]
    fy = [np.vstack([(C + S) * 2 / n, one / n]), np.vstack([S * 2 / n, alt / n]), np.vstack([-C * 2 / n, nil])]
    eye = np.eye(BT)
    half = np.repeat([0.0, 1.0], NS)
    hot = np.zeros((128, 2 * T - 1), f)
    hot[:, T - 1] = 2.0
    one0 = np.zeros((1, T), f)
    one0[0, 0] = 1.0
    mask = np.kron(eye, np.ones((T, T)))
    return {
        "ident": np.eye(128, dtype=f),
        "sel": np.tile(np.eye(T, dtype=f), (H, 1)),
        "block_mask": mask.reshape(128, BT, T).astype(f),
        "dft_x": np.stack([np.kron(eye, m.T) for m in fx], 1).astype(f),
        "dft_y": np.stack([np.kron(eye, m) for m in fy], 1).astype(f),
        "dft_k": np.stack([np.tile(m.T, (4, BT)) for m in fk], 1).astype(f),
        "phase": np.stack([0.25 * (1 - half), 0.25 * half, np.pi / 2 * (1 - half), np.pi / 2 * half, 1 - 2 * half,
                           PI_IN - np.pi / 2 * (1 - half), -PI_IN - np.pi / 2 * (1 - half),
                           PI_IN - np.pi / 2 * half, -PI_IN - np.pi / 2 * half], 1).astype(f),
        "hot": hot,
        "one0": one0,
    }


def kernel(**inputs):
    import concourse.bacc as _bacc
    from concourse.bass_utils import run_bass_kernel_spmd as _run

    raw = {k: np.asarray(v) for k, v in inputs.items()}
    xa = lambda n: raw["L0_xattn_" + n]
    chunks = lambda w: w.reshape(-1, 128, w.shape[-1]).transpose(1, 0, 2)
    cols = lambda v: v.reshape(-1, 128).T
    context = raw["ctx_768"]
    ctxT = context.transpose(2, 0, 1).reshape(DV, NT, BT, G).transpose(1, 0, 2, 3)
    awvT = raw["L0_attn_wv"].T.reshape(D, T, 8).transpose(0, 2, 1).reshape(D, D)
    arrays = {
        "x": raw["x"].reshape(NT, 128, D).transpose(1, 0, 2),
        "ctx_n": context[:, :256].reshape(NT, BT, 2, 128, DV).transpose(0, 3, 1, 2, 4),
        "ctx_l": context[:, 256:].reshape(NT, BT, 1, DV),
        "ctxT1": ctxT[:, 0:128],
        "ctxT2": ctxT[:, 128:DV],
        "vmask": raw["mask_BxS2_bf1"].view(np.uint8),
        "tmaskT": raw["mask_BxS_bf1"].view(np.uint8).T,
        "Wq": chunks(xa("Wq")), "WkT": xa("Wk").T, "WvT": chunks(xa("Wv").T),
        "W_film_in": chunks(xa("W_film_in")), "W_film_out": chunks(xa("W_film_out")),
        "b_film_in": xa("b_film_in")[None], "b_film_out": xa("b_film_out")[None],
        "g_norm_in": xa("g_norm_in")[None], "b_norm_in": xa("b_norm_in")[None],
        "g_norm_out": xa("g_norm_out")[None], "b_norm_out": xa("b_norm_out")[None],
        "g_ffn": cols(xa("g_ffn")), "b_ffn": cols(xa("b_ffn")),
        "W1": chunks(xa("W1")), "b1": cols(xa("b1")), "W2": chunks(xa("W2")), "b2": xa("b2")[None],
        "log_dt": xa("log_dt")[None], "A_re": xa("A_re").T, "A_im": xa("A_im").T,
        "C_re": xa("C_re").T, "C_im": xa("C_im").T, "D_skip": xa("D_skip")[None],
        "mod_gate": xa("mod_gate").reshape(1, 1),
        "awq": chunks(raw["L0_attn_wq"]), "awk": chunks(raw["L0_attn_wk"]),
        "awvT": chunks(awvT), "awoT": chunks(raw["L0_attn_wo"].T),
        "routeT": chunks(raw["L0_ffn_w_route"].T), "cent": raw["L0_ffn_centroids"],
        "e_w1": chunks(raw["L0_ffn_w1"].transpose(1, 0, 2).reshape(D, HID)),
        "e_w2": raw["L0_ffn_w2"].transpose(1, 0, 2), "e_b1": raw["L0_ffn_b1"].T, "e_b2": raw["L0_ffn_b2"],
        **_constants(),
    }
    arrays = {f"in_{k}": np.ascontiguousarray(v) for k, v in arrays.items()}
    nc = _bacc.Bacc("TRN2", target_bir_lowering=False, num_devices=1)
    aps = {k[3:]: nc.dram_tensor(k, v.shape, mybir.dt.from_np(v.dtype), kind="ExternalInput").ap() for k, v in arrays.items()}
    out = nc.dram_tensor("out", (NT, 128, D), F32, kind="ExternalOutput").ap()
    build(nc, aps, out)
    r = _run(nc, [arrays], core_ids=[0])
    return r.results[0]["out"].reshape(NB, T, D)
```
